# Optimizing a Trainium2 kernel written in Bass

```python
import numpy as np
import jax
import jax.numpy as jnp

def _softmax(x, axis=-1):
    return jax.nn.softmax(x, axis=axis)

def _gelu(x):
    return jax.nn.gelu(x, approximate=True)

def _silu(x):
    return jax.nn.silu(x)

def _sigmoid(x):
    return jax.nn.sigmoid(x)

def _layernorm(x, axis=-1, eps=1e-05):
    m = jnp.mean(x, axis=axis, keepdims=True)
    v = jnp.var(x, axis=axis, keepdims=True)
    return (x - m) / jnp.sqrt(v + eps)

def _scatter_add(tgt, idx, src, axis=0):
    return tgt.at[idx].add(src)

def _segment_sum(src, seg, n):
    return jax.ops.segment_sum(src, seg, n)
kernel_name = 'mk_hybrid_d2_jaxref_r4_899c4c'

def setup_inputs(seed: int=0):
    np.random.seed(seed)
    _w = jnp.asarray

    def _L0_attn_a_setup():
        import jax, jax.numpy as jnp
        import numpy as np
        B, T, D_IN = (8, 1024, 512)
        D_HIDDEN = 512
        D_OUT = 512
        N_BLOCKS = 8
        R_MIN, R_MAX = (0.9, 0.999)
        INIT_IMAG = 0.1

        def _lecun(key, shape, fan_in):
            return (jax.random.normal(key, shape, dtype=jnp.float32) * np.sqrt(1.0 / fan_in)).astype(jnp.float32)

        def _block_diag_linear(x, W, b):
            h, i, j = W.shape
            xb = x.reshape(x.shape[0], x.shape[1], h, i)
            y = jnp.einsum('bthi,hij->bthj', xb, W) + b
            return y.reshape(y.shape[0], y.shape[1], h * j)

        def _linear_scan(a, x):

            def combine(l, r):
                al, bl = l
                ar, br = r
                return (al * ar, ar * bl + br)
            _, h = jax.lax.associative_scan(combine, (a, x), axis=1)
            return h

        def _reference_tuple_inner(x, W_in, b_in, W_gx, b_gx, W_ga, b_ga, a_real, a_imag, W_out, b_out):
            xh = x @ W_in + b_in
            gate_x = jax.nn.sigmoid(_block_diag_linear(xh, W_gx, b_gx))
            gate_a = jax.nn.sigmoid(_block_diag_linear(xh, W_ga, b_ga))
            log_a_re = -8.0 * gate_a * jax.nn.softplus(a_real)
            log_a_im = a_imag * gate_a
            a = jnp.exp(jax.lax.complex(log_a_re, log_a_im))
            a_sq = jnp.exp(jax.lax.complex(2.0 * log_a_re, 2.0 * log_a_im))
            xr, xi = jnp.split(xh, 2, axis=-1)
            xc = jax.lax.complex(xr, xi) * gate_x
            xc = jnp.sqrt(1.0 - a_sq) * xc
            h = _linear_scan(a, xc)
            h_m = jnp.concatenate([h.real, h.imag], axis=-1)
            out = h_m @ W_out + b_out
            h_last = h_m[:, -1]
            return (out, h_last)
        key = jax.random.key(seed)
        ks = jax.random.split(key, 12)
        dh2 = D_HIDDEN // 2
        bin_, bout = (dh2 // N_BLOCKS, None)
        blk_in = D_HIDDEN // N_BLOCKS
        blk_out = dh2 // N_BLOCKS
        u1 = jax.random.uniform(ks[8], (dh2,))
        a_r = 0.5 * jnp.log(u1 * (R_MAX ** 2 - R_MIN ** 2) + R_MIN ** 2 + 1e-08)
        a_real = jnp.log(jnp.exp(-a_r) - 1.0)
        u2 = jax.random.uniform(ks[9], (dh2,))
        a_imag = jnp.pi * INIT_IMAG * u2
        return {'x': jax.random.normal(ks[0], (B, T, D_IN), dtype=jnp.float32), 'W_in': _lecun(ks[1], (D_IN, D_HIDDEN), D_IN), 'b_in': jnp.zeros((D_HIDDEN,), jnp.float32), 'W_gx': _lecun(ks[2], (N_BLOCKS, blk_in, blk_out), blk_in), 'b_gx': _lecun(ks[3], (N_BLOCKS, blk_out), blk_in), 'W_ga': _lecun(ks[4], (N_BLOCKS, blk_in, blk_out), blk_in), 'b_ga': _lecun(ks[5], (N_BLOCKS, blk_out), blk_in), 'a_real': a_real, 'a_imag': a_imag, 'W_out': _lecun(ks[6], (D_HIDDEN, D_OUT), D_HIDDEN), 'b_out': jnp.zeros((D_OUT,), jnp.float32)}
    _L0_attn_a_in = _L0_attn_a_setup()

    def _L0_attn_b_setup():
        import jax, jax.numpy as jnp
        import numpy as np
        D_INNER = 512
        STATE_DIM = 16
        DT_MIN = 0.0001

        def _softplus(x):
            return jnp.log1p(jnp.exp(-jnp.abs(x))) + jnp.maximum(x, 0)

        def _reference_tuple_inner(u, Wdt, bdt, Wb, bb, Wc, bc, a_raw, B_base, C_base, D):
            B, L, d = u.shape
            N = a_raw.shape[1]
            A = -_softplus(a_raw)
            dt = _softplus(jnp.einsum('bld,de->ble', u, Wdt) + bdt) + DT_MIN
            b_t = jnp.einsum('bld,de->ble', u, Wb) + bb
            c_t = jnp.einsum('bld,de->ble', u, Wc) + bc

            def step(x, inp):
                u_s, dt_s, b_s, c_s = inp
                Abar = jnp.exp(dt_s[:, :, None] * A)
                Bbar = dt_s[:, :, None] * (b_s[:, :, None] * B_base)
                x = Abar * x + Bbar * u_s[:, :, None]
                y = jnp.sum(c_s[:, :, None] * C_base * x, axis=-1) + D * u_s
                return (x, y)
            carry0 = jnp.zeros((B, d, N), dtype=u.dtype)
            xs = (jnp.swapaxes(u, 0, 1), jnp.swapaxes(dt, 0, 1), jnp.swapaxes(b_t, 0, 1), jnp.swapaxes(c_t, 0, 1))
            carry_out, ys = jax.lax.scan(step, carry0, xs)
            y = jnp.swapaxes(ys, 0, 1)
            return (carry_out, y)
        key = jax.random.key(seed)
        ks = jax.random.split(key, 11)
        B, L, d, N = (4, 1024, D_INNER, STATE_DIM)
        u = jax.random.normal(ks[0], (B, L, d), dtype=jnp.float32)
        s = 0.02
        return {'u': u, 'Wdt': jax.random.normal(ks[1], (d, d), jnp.float32) / jnp.sqrt(d), 'bdt': jnp.zeros((d,), jnp.float32), 'Wb': jax.random.normal(ks[2], (d, d), jnp.float32) / jnp.sqrt(d), 'bb': jnp.zeros((d,), jnp.float32), 'Wc': jax.random.normal(ks[3], (d, d), jnp.float32) / jnp.sqrt(d), 'bc': jnp.zeros((d,), jnp.float32), 'a_raw': s * jax.random.normal(ks[4], (d, N), jnp.float32), 'B_base': s * jax.random.normal(ks[5], (d, N), jnp.float32), 'C_base': s * jax.random.normal(ks[6], (d, N), jnp.float32), 'D': jnp.zeros((d,), jnp.float32)}
    _L0_attn_b_in = _L0_attn_b_setup()

    def _L0_ffn_setup():
        import jax, jax.numpy as jnp
        import numpy as np

        def binarize_weight(w):
            alpha = jnp.mean(jnp.abs(w), axis=tuple(range(1, w.ndim)), keepdims=True)
            bw = jnp.where(w >= 0, 1.0, -1.0) * alpha
            return jax.lax.stop_gradient(bw - w) + w
        key = jax.random.key(seed)
        k1, k2, k3 = jax.random.split(key, 3)
        in_features, out_features = (512, 512)
        x = jax.random.normal(k1, (8, 512, in_features), dtype=jnp.float32)
        std = np.sqrt(2.0 / out_features).astype(np.float32)
        weight = jax.random.normal(k2, (out_features, in_features), dtype=jnp.float32) * std
        bias = jax.random.normal(k3, (out_features,), dtype=jnp.float32) * 0.01
        return {'x': x, 'weight': weight, 'bias': bias}
    _L0_ffn_in = _L0_ffn_setup()

    def _L1_attn_a_setup():
        import jax, jax.numpy as jnp
        import numpy as np
        B, S, D, H = (4, 512, 512, 16)
        DH = D // H
        key = jax.random.key(seed)
        ks = jax.random.split(key, 11)
        p = 0.02
        return {'x': jax.random.normal(ks[0], (B, S, D), jnp.float32), 'Wq': jax.random.normal(ks[1], (D, D), jnp.float32) * p, 'bq': jax.random.normal(ks[2], (D,), jnp.float32) * p, 'Wk': jax.random.normal(ks[3], (D, D), jnp.float32) * p, 'bk': jax.random.normal(ks[4], (D,), jnp.float32) * p, 'Wv': jax.random.normal(ks[5], (D, D), jnp.float32) * p, 'bv': jax.random.normal(ks[6], (D,), jnp.float32) * p, 'Wo': jax.random.normal(ks[7], (D, D), jnp.float32) * p, 'bo': jax.random.normal(ks[8], (D,), jnp.float32) * p, 'spiral_weight': jax.random.normal(ks[9], (H,), jnp.float32), 'helix_rotation': jax.random.normal(ks[10], (D,), jnp.float32)}
    _L1_attn_a_in = _L1_attn_a_setup()

    def _L1_attn_b_setup():
        import jax, jax.numpy as jnp
        import numpy as np
        H = 32
        D = 64
        BS = 64
        LAYER_IDX = 0
        NUM_LAYERS = 32
        EPS = 1e-05

        def _decay_buffers():
            base = 1.0 / 2.0 ** (8.0 / H)
            rate = base ** (jnp.arange(H, dtype=jnp.float32) + 1.0)
            factor = 1.0 - LAYER_IDX / (NUM_LAYERS - 1 + 1e-05) + 1e-05
            slope = (rate * factor)[:, None, None]
            r = jnp.arange(BS, dtype=jnp.float32) + 1.0
            query_decay = jnp.exp(-slope * r[:, None])
            key_decay = jnp.exp(-slope * (BS - r[:, None]))
            dd = r[:, None] - r[None, :]
            dd = slope * dd[None, :, :]
            dd = jnp.where(dd >= 0, -dd, -jnp.inf)
            diagonal_decay = jnp.exp(dd)[None]
            block_decay = jnp.exp(-slope * BS)
            return (slope, query_decay, key_decay, diagonal_decay, block_decay)

        def _rmsnorm(x, w):
            v = jnp.mean(x.astype(jnp.float32) ** 2, axis=-1, keepdims=True)
            return (x * jax.lax.rsqrt(v + EPS)).astype(x.dtype) * w
        key = jax.random.key(seed)
        ks = jax.random.split(key, 4)
        b, s, hid = (2, 1024, 512)
        return {'hidden_states': jax.random.normal(ks[0], (b, s, hid), jnp.float32), 'qkv_w': jax.random.normal(ks[1], (3 * H * D, hid), jnp.float32) * 0.02, 'out_w': jax.random.normal(ks[2], (hid, H * D), jnp.float32) * 0.02, 'gate_w': jax.random.normal(ks[3], (H * D, hid), jnp.float32) * 0.02, 'norm_w': jnp.ones((H * D,), jnp.float32)}
    _L1_attn_b_in = _L1_attn_b_setup()

    def _L1_ffn_setup():
        import jax, jax.numpy as jnp
        import numpy as np
        TOP_K = 8
        CAPACITY = 256
        key = jax.random.key(seed)
        k1, k2, k3, k4 = jax.random.split(key, 4)
        B, S, H, E, I = (2, 256, 512, 64, 192)
        hidden_states = jax.random.normal(k1, (B, S, H), dtype=jnp.float32)
        router_weight = jax.random.normal(k2, (E, H), dtype=jnp.float32) * 0.02
        gate_up_proj = jax.random.normal(k3, (E, H, 2 * I), dtype=jnp.float32) * 0.02
        down_proj = jax.random.normal(k4, (E, I, H), dtype=jnp.float32) * 0.02
        return {'hidden_states': hidden_states, 'router_weight': router_weight, 'gate_up_proj': gate_up_proj, 'down_proj': down_proj}
    _L1_ffn_in = _L1_ffn_setup()
    _d = {'L0_attn_a_x': _L0_attn_a_in['x'], 'L0_attn_a_W_in': _L0_attn_a_in['W_in'], 'L0_attn_a_b_in': _L0_attn_a_in['b_in'], 'L0_attn_a_W_gx': _L0_attn_a_in['W_gx'], 'L0_attn_a_b_gx': _L0_attn_a_in['b_gx'], 'L0_attn_a_W_ga': _L0_attn_a_in['W_ga'], 'L0_attn_a_b_ga': _L0_attn_a_in['b_ga'], 'L0_attn_a_a_real': _L0_attn_a_in['a_real'], 'L0_attn_a_a_imag': _L0_attn_a_in['a_imag'], 'L0_attn_a_W_out': _L0_attn_a_in['W_out'], 'L0_attn_a_b_out': _L0_attn_a_in['b_out'], 'L0_attn_b_Wdt': _L0_attn_b_in['Wdt'], 'L0_attn_b_bdt': _L0_attn_b_in['bdt'], 'L0_attn_b_Wb': _L0_attn_b_in['Wb'], 'L0_attn_b_bb': _L0_attn_b_in['bb'], 'L0_attn_b_Wc': _L0_attn_b_in['Wc'], 'L0_attn_b_bc': _L0_attn_b_in['bc'], 'L0_attn_b_a_raw': _L0_attn_b_in['a_raw'], 'L0_attn_b_B_base': _L0_attn_b_in['B_base'], 'L0_attn_b_C_base': _L0_attn_b_in['C_base'], 'L0_attn_b_D': _L0_attn_b_in['D'], 'L0_ffn_weight': _L0_ffn_in['weight'], 'L0_ffn_bias': _L0_ffn_in['bias'], 'L1_attn_a_Wq': _L1_attn_a_in['Wq'], 'L1_attn_a_bq': _L1_attn_a_in['bq'], 'L1_attn_a_Wk': _L1_attn_a_in['Wk'], 'L1_attn_a_bk': _L1_attn_a_in['bk'], 'L1_attn_a_Wv': _L1_attn_a_in['Wv'], 'L1_attn_a_bv': _L1_attn_a_in['bv'], 'L1_attn_a_Wo': _L1_attn_a_in['Wo'], 'L1_attn_a_bo': _L1_attn_a_in['bo'], 'L1_attn_a_spiral_weight': _L1_attn_a_in['spiral_weight'], 'L1_attn_a_helix_rotation': _L1_attn_a_in['helix_rotation'], 'L1_attn_b_qkv_w': _L1_attn_b_in['qkv_w'], 'L1_attn_b_out_w': _L1_attn_b_in['out_w'], 'L1_attn_b_gate_w': _L1_attn_b_in['gate_w'], 'L1_attn_b_norm_w': _L1_attn_b_in['norm_w'], 'L1_ffn_router_weight': _L1_ffn_in['router_weight'], 'L1_ffn_gate_up_proj': _L1_ffn_in['gate_up_proj'], 'L1_ffn_down_proj': _L1_ffn_in['down_proj']}
    _x0 = _d['L0_attn_a_x']
    _d['L0_attn_a_x'] = jax.random.normal(jax.random.fold_in(jax.random.key(seed), 1), (1, 2048, 512), dtype=_x0.dtype)
    del _x0
    return _d

def reference(L0_attn_a_x, L0_attn_a_W_in, L0_attn_a_b_in, L0_attn_a_W_gx, L0_attn_a_b_gx, L0_attn_a_W_ga, L0_attn_a_b_ga, L0_attn_a_a_real, L0_attn_a_a_imag, L0_attn_a_W_out, L0_attn_a_b_out, L0_attn_b_Wdt, L0_attn_b_bdt, L0_attn_b_Wb, L0_attn_b_bb, L0_attn_b_Wc, L0_attn_b_bc, L0_attn_b_a_raw, L0_attn_b_B_base, L0_attn_b_C_base, L0_attn_b_D, L0_ffn_weight, L0_ffn_bias, L1_attn_a_Wq, L1_attn_a_bq, L1_attn_a_Wk, L1_attn_a_bk, L1_attn_a_Wv, L1_attn_a_bv, L1_attn_a_Wo, L1_attn_a_bo, L1_attn_a_spiral_weight, L1_attn_a_helix_rotation, L1_attn_b_qkv_w, L1_attn_b_out_w, L1_attn_b_gate_w, L1_attn_b_norm_w, L1_ffn_router_weight, L1_ffn_gate_up_proj, L1_ffn_down_proj):

    def _L0_attn_a_ref(x, W_in, b_in, W_gx, b_gx, W_ga, b_ga, a_real, a_imag, W_out, b_out):
        import jax, jax.numpy as jnp
        import numpy as np
        B, T, D_IN = (8, 1024, 512)
        D_HIDDEN = 512
        D_OUT = 512
        N_BLOCKS = 8
        R_MIN, R_MAX = (0.9, 0.999)
        INIT_IMAG = 0.1

        def _lecun(key, shape, fan_in):
            return (jax.random.normal(key, shape, dtype=jnp.float32) * np.sqrt(1.0 / fan_in)).astype(jnp.float32)

        def _block_diag_linear(x, W, b):
            h, i, j = W.shape
            xb = x.reshape(x.shape[0], x.shape[1], h, i)
            y = jnp.einsum('bthi,hij->bthj', xb, W) + b
            return y.reshape(y.shape[0], y.shape[1], h * j)

        def _linear_scan(a, x):

            def combine(l, r):
                al, bl = l
                ar, br = r
                return (al * ar, ar * bl + br)
            _, h = jax.lax.associative_scan(combine, (a, x), axis=1)
            return h

        def _reference_tuple_inner(x, W_in, b_in, W_gx, b_gx, W_ga, b_ga, a_real, a_imag, W_out, b_out):
            xh = x @ W_in + b_in
            gate_x = jax.nn.sigmoid(_block_diag_linear(xh, W_gx, b_gx))
            gate_a = jax.nn.sigmoid(_block_diag_linear(xh, W_ga, b_ga))
            log_a_re = -8.0 * gate_a * jax.nn.softplus(a_real)
            log_a_im = a_imag * gate_a
            a = jnp.exp(jax.lax.complex(log_a_re, log_a_im))
            a_sq = jnp.exp(jax.lax.complex(2.0 * log_a_re, 2.0 * log_a_im))
            xr, xi = jnp.split(xh, 2, axis=-1)
            xc = jax.lax.complex(xr, xi) * gate_x
            xc = jnp.sqrt(1.0 - a_sq) * xc
            h = _linear_scan(a, xc)
            h_m = jnp.concatenate([h.real, h.imag], axis=-1)
            out = h_m @ W_out + b_out
            h_last = h_m[:, -1]
            return (out, h_last)
        return _reference_tuple_inner(x, W_in, b_in, W_gx, b_gx, W_ga, b_ga, a_real, a_imag, W_out, b_out)[0]

    def _L0_attn_b_ref(u, Wdt, bdt, Wb, bb, Wc, bc, a_raw, B_base, C_base, D):
        import jax, jax.numpy as jnp
        import numpy as np
        D_INNER = 512
        STATE_DIM = 16
        DT_MIN = 0.0001

        def _softplus(x):
            return jnp.log1p(jnp.exp(-jnp.abs(x))) + jnp.maximum(x, 0)

        def _reference_tuple_inner(u, Wdt, bdt, Wb, bb, Wc, bc, a_raw, B_base, C_base, D):
            B, L, d = u.shape
            N = a_raw.shape[1]
            A = -_softplus(a_raw)
            dt = _softplus(jnp.einsum('bld,de->ble', u, Wdt) + bdt) + DT_MIN
            b_t = jnp.einsum('bld,de->ble', u, Wb) + bb
            c_t = jnp.einsum('bld,de->ble', u, Wc) + bc

            def step(x, inp):
                u_s, dt_s, b_s, c_s = inp
                Abar = jnp.exp(dt_s[:, :, None] * A)
                Bbar = dt_s[:, :, None] * (b_s[:, :, None] * B_base)
                x = Abar * x + Bbar * u_s[:, :, None]
                y = jnp.sum(c_s[:, :, None] * C_base * x, axis=-1) + D * u_s
                return (x, y)
            carry0 = jnp.zeros((B, d, N), dtype=u.dtype)
            xs = (jnp.swapaxes(u, 0, 1), jnp.swapaxes(dt, 0, 1), jnp.swapaxes(b_t, 0, 1), jnp.swapaxes(c_t, 0, 1))
            carry_out, ys = jax.lax.scan(step, carry0, xs)
            y = jnp.swapaxes(ys, 0, 1)
            return (carry_out, y)
        return _reference_tuple_inner(u, Wdt, bdt, Wb, bb, Wc, bc, a_raw, B_base, C_base, D)[1]

    def _L0_ffn_ref(x, weight, bias):
        import jax, jax.numpy as jnp
        import numpy as np

        def binarize_weight(w):
            alpha = jnp.mean(jnp.abs(w), axis=tuple(range(1, w.ndim)), keepdims=True)
            bw = jnp.where(w >= 0, 1.0, -1.0) * alpha
            return jax.lax.stop_gradient(bw - w) + w
        bw = binarize_weight(weight)
        return jnp.einsum('bsi,oi->bso', x, bw) + bias

    def _L1_attn_a_ref(x, Wq, bq, Wk, bk, Wv, bv, Wo, bo, spiral_weight, helix_rotation):
        import jax, jax.numpy as jnp
        import numpy as np
        B, S, D, H = (4, 512, 512, 16)
        DH = D // H
        b, s, d = x.shape
        h, dh = (H, d // H)
        q = (x @ Wq.T + bq).reshape(b, s, h, dh)
        k = (x @ Wk.T + bk).reshape(b, s, h, dh)
        v = (x @ Wv.T + bv).reshape(b, s, h, dh)
        rot = helix_rotation.reshape(h, dh)
        q = q * jnp.cos(rot)
        k = k * jnp.sin(rot)
        scores = jnp.einsum('bshd,bthd->bhst', q, k) / np.sqrt(dh).astype(np.float32)
        scores = scores * spiral_weight[None, :, None, None]
        attn = jax.nn.softmax(scores, axis=-1)
        out = jnp.einsum('bhst,bthd->bshd', attn, v).reshape(b, s, d)
        return out @ Wo.T + bo

    def _L1_attn_b_ref(hidden_states, qkv_w, out_w, gate_w, norm_w):
        import jax, jax.numpy as jnp
        import numpy as np
        H = 32
        D = 64
        BS = 64
        LAYER_IDX = 0
        NUM_LAYERS = 32
        EPS = 1e-05

        def _decay_buffers():
            base = 1.0 / 2.0 ** (8.0 / H)
            rate = base ** (jnp.arange(H, dtype=jnp.float32) + 1.0)
            factor = 1.0 - LAYER_IDX / (NUM_LAYERS - 1 + 1e-05) + 1e-05
            slope = (rate * factor)[:, None, None]
            r = jnp.arange(BS, dtype=jnp.float32) + 1.0
            query_decay = jnp.exp(-slope * r[:, None])
            key_decay = jnp.exp(-slope * (BS - r[:, None]))
            dd = r[:, None] - r[None, :]
            dd = slope * dd[None, :, :]
            dd = jnp.where(dd >= 0, -dd, -jnp.inf)
            diagonal_decay = jnp.exp(dd)[None]
            block_decay = jnp.exp(-slope * BS)
            return (slope, query_decay, key_decay, diagonal_decay, block_decay)

        def _rmsnorm(x, w):
            v = jnp.mean(x.astype(jnp.float32) ** 2, axis=-1, keepdims=True)
            return (x * jax.lax.rsqrt(v + EPS)).astype(x.dtype) * w
        b, s, hid = hidden_states.shape
        nb = s // BS
        _, qd, kd, dd, bd = _decay_buffers()
        qkv = jax.nn.silu(hidden_states @ qkv_w.T)
        qkv = qkv.reshape(b, s, H, 3 * D)
        q, k, v = jnp.split(qkv, 3, axis=-1)

        def to_blocks(t):
            return t.transpose(0, 2, 1, 3).reshape(b, H, nb, BS, D).transpose(2, 0, 1, 3, 4)
        qb, kb, vb = (to_blocks(q), to_blocks(k), to_blocks(v))
        qd_ = qd[None]
        kd_ = kd[None]
        bd_ = bd[None]

        def step(state, blk):
            qi, ki, vi = blk
            aw = jnp.einsum('bhid,bhjd->bhij', qi, ki) * dd
            intra = jnp.einsum('bhij,bhjd->bhid', aw, vi)
            inter = jnp.einsum('bhid,bhde->bhie', qi * qd_, state)
            new_state = state * bd_ + jnp.einsum('bhsd,bhse->bhde', ki * kd_, vi)
            return (new_state, intra + inter)
        state0 = jnp.zeros((b, H, D, D), hidden_states.dtype)
        _, ys = jax.lax.scan(step, state0, (qb, kb, vb))
        attn = ys.transpose(1, 2, 0, 3, 4).reshape(b, H, s, D)
        attn = attn.transpose(0, 2, 1, 3).reshape(b, s, H * D)
        attn = _rmsnorm(attn, norm_w)
        gate = jax.nn.sigmoid(hidden_states @ gate_w.T)
        return gate * attn @ out_w.T

    def _L1_ffn_ref(hidden_states, router_weight, gate_up_proj, down_proj):
        import jax, jax.numpy as jnp
        import numpy as np
        TOP_K = 8
        CAPACITY = 256
        B, S, H = hidden_states.shape
        E = router_weight.shape[0]
        K, C = (TOP_K, CAPACITY)
        x = hidden_states.reshape(-1, H)
        logits = x @ router_weight.T
        probs = jax.nn.softmax(logits, axis=-1)
        topw, topi = jax.lax.top_k(probs, K)
        topw = topw / jnp.sum(topw, axis=-1, keepdims=True)
        flat_e = topi.reshape(-1)
        oh = jax.nn.one_hot(flat_e, E, dtype=jnp.int32)
        pos = jnp.take_along_axis(jnp.cumsum(oh, axis=0), flat_e[:, None], axis=1)[:, 0] - 1
        x_rep = jnp.repeat(x, K, axis=0)
        xe = jnp.zeros((E, C, H), x.dtype).at[flat_e, pos].set(x_rep, mode='drop')
        gu = jnp.einsum('ech,ehf->ecf', xe, gate_up_proj)
        g, u = jnp.split(gu, 2, axis=-1)
        h = jax.nn.silu(g) * u
        ye = jnp.einsum('eci,eih->ech', h, down_proj)
        valid = pos < C
        y_flat = jnp.where(valid[:, None], ye[flat_e, jnp.minimum(pos, C - 1)], 0.0)
        y = jnp.sum(y_flat.reshape(-1, K, H) * topw.reshape(-1, K)[..., None], axis=1)
        return y.reshape(B, S, H)
    x = L0_attn_a_x
    x = x + _L0_attn_a_ref(_layernorm(x, axis=-1), L0_attn_a_W_in, L0_attn_a_b_in, L0_attn_a_W_gx, L0_attn_a_b_gx, L0_attn_a_W_ga, L0_attn_a_b_ga, L0_attn_a_a_real, L0_attn_a_a_imag, L0_attn_a_W_out, L0_attn_a_b_out)
    x = x + _L0_ffn_ref(_layernorm(x, axis=-1), L0_ffn_weight, L0_ffn_bias)
    x = x + _L0_attn_b_ref(_layernorm(x, axis=-1), L0_attn_b_Wdt, L0_attn_b_bdt, L0_attn_b_Wb, L0_attn_b_bb, L0_attn_b_Wc, L0_attn_b_bc, L0_attn_b_a_raw, L0_attn_b_B_base, L0_attn_b_C_base, L0_attn_b_D)
    x = x + _L0_ffn_ref(_layernorm(x, axis=-1), L0_ffn_weight, L0_ffn_bias)
    x = x + _L1_attn_a_ref(_layernorm(x, axis=-1), L1_attn_a_Wq, L1_attn_a_bq, L1_attn_a_Wk, L1_attn_a_bk, L1_attn_a_Wv, L1_attn_a_bv, L1_attn_a_Wo, L1_attn_a_bo, L1_attn_a_spiral_weight, L1_attn_a_helix_rotation)
    x = x + _L1_ffn_ref(_layernorm(x, axis=-1), L1_ffn_router_weight, L1_ffn_gate_up_proj, L1_ffn_down_proj)
    x = x + _L1_attn_b_ref(_layernorm(x, axis=-1), L1_attn_b_qkv_w, L1_attn_b_out_w, L1_attn_b_gate_w, L1_attn_b_norm_w)
    x = x + _L1_ffn_ref(_layernorm(x, axis=-1), L1_ffn_router_weight, L1_ffn_gate_up_proj, L1_ffn_down_proj)
    return x

_drawn_inputs = setup_inputs


def setup_inputs(seed=0):
    import zlib

    import numpy as np

    out = dict(_drawn_inputs(seed))
    spreads = {'L0_attn_a_b_in': (0.0, 0.1),
     'L0_attn_a_b_out': (0.0, 0.1),
     'L0_attn_b_bdt': (0.0, 0.8),
     'L0_attn_b_bb': (0.0, 0.8),
     'L0_attn_b_bc': (0.0, 0.8),
     'L0_attn_b_D': (0.0, 2.0),
     'L1_attn_b_norm_w': (1.0, 0.6)}
    factors = {'L0_attn_b_Wdt': 8.0,
     'L0_attn_b_Wb': 8.0,
     'L0_attn_b_Wc': 8.0,
     'L0_attn_b_a_raw': 8.0,
     'L0_attn_b_B_base': 8.0,
     'L0_attn_b_C_base': 8.0,
     'L0_ffn_bias': 5.735,
     'L1_attn_a_Wq': 8.0,
     'L1_attn_a_bq': 41.377,
     'L1_attn_a_Wk': 8.0,
     'L1_attn_a_bk': 200.0,
     'L1_attn_a_Wv': 3.362,
     'L1_attn_a_bv': 42.78,
     'L1_attn_a_Wo': 3.405,
     'L1_attn_a_bo': 45.098,
     'L1_attn_a_spiral_weight': 8.0,
     'L1_attn_a_helix_rotation': 8.0,
     'L1_ffn_router_weight': 7.599,
     'L1_ffn_gate_up_proj': 6.95,
     'L1_ffn_down_proj': 6.95,
     'L1_attn_b_qkv_w': 16.684,
     'L1_attn_b_out_w': 5.282,
     'L1_attn_b_gate_w': 8.0}
    for name, (base, spread) in spreads.items():
        noise = np.random.default_rng([zlib.crc32(name.encode()), seed]).standard_normal(out[name].shape)
        drawn = base * np.exp(spread * noise) if base else spread * noise
        out[name] = jnp.asarray(drawn.astype(out[name].dtype))
    for name, factor in factors.items():
        out[name] = (out[name] * factor).astype(out[name].dtype)
    return out
```

```python
import math
from contextlib import ExitStack

import concourse.bass as bass
import concourse.mybir as mybir

F32 = mybir.dt.float32
BF16 = mybir.dt.bfloat16
I32 = mybir.dt.int32
U32 = mybir.dt.uint32
ALU = mybir.AluOpType
ACT = mybir.ActivationFunctionType
AX = mybir.AxisListType

P = 128
T = 2048
D = 512
TT = T // P
DT = D // P
NB = 512
TC = T // NB
LN_EPS = 1e-5


class Chain:

    def __init__(self, eng, sem):
        self.eng, self.sem, self.n = eng, sem, 0

    def __call__(self, ins):
        self.n += 1
        ins.then_inc(self.sem, 1)
        self.eng.wait_ge(self.sem, self.n)
        return ins


class Layer:

    def __init__(self, nc, name):
        self.nc, self.name, self.ctx, self.sems = nc, name, ExitStack(), []

    def __enter__(self):
        self.ctx.__enter__()
        return self

    def __exit__(self, *a):
        done = self.ctx.__exit__(*a)
        if a[0] is None:
            self.nc.clear_and_free_semaphores(self.sems)
            self.nc.all_engine_barrier()
        return done

    def sb(self, name, shape, dt=F32):
        return self.ctx.enter_context(self.nc.sbuf_tensor(f"{self.name}_{name}", shape, dt))

    def ps(self, name, shape, dt=F32):
        return self.ctx.enter_context(self.nc.psum_tensor(f"{self.name}_{name}", shape, dt))

    def sem(self, name):
        self.sems.append(self.nc.alloc_semaphore(f"{self.name}_{name}"))
        return self.sems[-1]

    def block(self):
        return self.ctx.enter_context(self.nc.Block())


def per_partition(vec, tiles):
    return vec.rearrange("(c p) -> p c", p=P)


def setup(nc, g):
    with Layer(nc, "setup") as L:
        loaded, zeroed = L.sem("loaded"), L.sem("zeroed")
        block = L.block()

        @block.sync
        def _(sp):
            sp.dma_start(g.X[:, :, :], g.dram["L0_attn_a_x"][0].rearrange("(i p) d -> p i d", p=P)).then_inc(loaded, 16)
            sp.wait_ge(loaded, 16)

        @block.gpsimd
        def _(pool):
            pool.memset(g.ident[:, :], 0.0).then_inc(zeroed, 1)
            pool.wait_ge(zeroed, 1)
            pool.affine_select(out=g.ident[:, :], in_=g.ident[:, :], compare_op=ALU.not_equal, fill=1.0, base=0,
                               pattern=[[-1, P]], channel_multiplier=1).then_inc(zeroed, 1)
            pool.wait_ge(zeroed, 2)
            pool.tensor_copy(g.ident16[:, :], g.ident[:, :]).then_inc(zeroed, 1)


def store(nc, g):
    with Layer(nc, "store") as L:
        stored = L.sem("stored")
        block = L.block()

        @block.sync
        def _(sp):
            sp.dma_start(g.dram["out"][0].rearrange("(i p) d -> p i d", p=P), g.X[:, :, :]).then_inc(stored, 16)
            sp.wait_ge(stored, 16)


class Norm:

    def __init__(self, L, nc, X):
        self.nc, self.X = nc, X
        self.stats, self.mv = L.sb("norm_stats", [P, TT, 6]), L.sb("norm_mv", [P, TT, 2])
        self.dev, self.rstd = L.sb("norm_dev", [P, TT]), L.sb("norm_rstd", [P, TT])
        self.summed, self.have_var, self.have_dev, self.have_rstd = (
            L.sem(n) for n in ("norm_summed", "norm_have_var", "norm_have_dev", "norm_have_rstd"))

    def on_vector(self, dve):
        nc = self.nc
        for i in range(TT):
            nc.vector.bn_stats(self.stats[:, i, :], self.X[:, i, :]).then_inc(self.summed, 1)
        for i in range(TT):
            dve.wait_ge(self.summed, i + 1)
            nc.vector.bn_aggr(self.mv[:, i, :], self.stats[:, i, :]).then_inc(self.summed, 1)
        dve.wait_ge(self.summed, 2 * TT)
        nc.vector.tensor_scalar(self.dev[:, :], self.mv[:, :, 1], LN_EPS, None, ALU.add).then_inc(self.have_var, 1)
        dve.wait_ge(self.have_dev, 1)
        nc.vector.reciprocal(self.rstd[:, :], self.dev[:, :]).then_inc(self.have_rstd, 1)
        dve.wait_ge(self.have_rstd, 1)

    def on_scalar(self, act):
        act.wait_ge(self.have_var, 1)
        self.nc.scalar.activation(self.dev[:, :], self.dev[:, :], ACT.Sqrt).then_inc(self.have_dev, 1)


def normalized_features(nc, g, name, zt):
    with Layer(nc, name) as L:
        norm = Norm(L, nc, g.X)
        z = L.sb("z", [P, 2, D])
        zt_ps = L.ps("zt_ps", [P, 2, DT, P])
        z_ready, zt_done, zt_ready = (L.sem(s) for s in ("z_ready", "zt_done", "zt_ready"))
        block = L.block()

        @block.vector
        def _(dve):
            norm.on_vector(dve)

            def normalize(i, b):
                nc.vector.tensor_scalar(z[:, b:b + 1, :], g.X[:, bass.ds(i, 1), :], norm.mv[:, bass.ds(i, 1), 0:1],
                                        norm.rstd[:, bass.ds(i, 1)], ALU.subtract, ALU.mult).then_inc(z_ready, 1)

            for b in range(2):
                normalize(b, b)
            with dve.Fori(0, TT // 2 - 1) as pair:
                for b in range(2):
                    dve.wait_ge(zt_done, pair * 2 + (b + 1))
                    normalize(pair * 2 + (2 + b), b)

        @block.tensor
        def _(pe):
            def transposes(i, b, first):
                pe.wait_ge(z_ready, i + 1)
                if not first:
                    pe.wait_ge(zt_ready, i - 1)
                for k in range(DT):
                    last = nc.tensor.transpose(zt_ps[:, b, k, :], z[:, b, k * P:(k + 1) * P], g.ident[:, :])
                last.then_inc(zt_done, 1)

            for b in range(2):
                transposes(b, b, True)
            with pe.Fori(0, TT // 2 - 1) as pair:
                for b in range(2):
                    transposes(pair * 2 + (2 + b), b, False)

        @block.scalar
        def _(act):
            norm.on_scalar(act)
            with act.Fori(0, TT // 2) as pair:
                for b in range(2):
                    act.wait_ge(zt_done, pair * 2 + b + 1)
                    nc.scalar.copy(zt[:, :, bass.ds((pair * 2 + b) * P, P)], zt_ps[:, b, :, :]).then_inc(zt_ready, 1)


def project_and_add(nc, g, name, h, w, bias_dram):
    with Layer(nc, name) as L:
        bias = L.sb("bias", [P, D])
        ht = L.sb("ht", [P, 2, DT, P])
        y_ps = L.ps("y_ps", [P, 2, D])
        loaded, h_ready, y_ready, y_used, biased = (L.sem(s) for s in ("loaded", "h_ready", "y_ready", "y_used", "biased"))
        block = L.block()

        @block.sync
        def _(sp):
            sp.dma_start(bias[:, :], bias_dram.partition_broadcast(P)).then_inc(loaded, 16)
            sp.wait_ge(loaded, 16)

        @block.scalar
        def _(act):
            with act.Fori(0, TT // 2) as pair:
                for b in range(2):
                    i = pair * 2 + b
                    act.wait_ge(y_ready, i + 1)
                    nc.scalar.copy(ht[:, b, :, :], h[:, :, bass.ds(i * P, P)]).then_inc(h_ready, 1)

        @block.tensor
        def _(pe):
            pe.sem_inc(y_ready, 2)
            pe.wait_ge(loaded, 16)
            with pe.Fori(0, TT // 2) as pair:
                for b in range(2):
                    i = pair * 2 + b
                    pe.wait_ge(h_ready, i + 1)
                    pe.wait_ge(y_used, i + 1)
                    for k in range(DT):
                        last = nc.tensor.matmul(y_ps[:, b, :], ht[:, b, k, :], w[:, k, :], start=(k == 0), stop=(k == DT - 1))
                    last.then_inc(y_ready, 1)

        @block.gpsimd
        def _(pool):
            pool.wait_ge(loaded, 16)
            with pool.Fori(0, TT) as i:
                pool.tensor_tensor(g.X[:, bass.ds(i, 1), :], g.X[:, bass.ds(i, 1), :],
                                   bias[:, :].rearrange("p (o d) -> p o d", o=1), ALU.add).then_inc(biased, 1)

        @block.vector
        def _(dve):
            dve.sem_inc(y_used, 2)
            with dve.Fori(0, TT // 2) as pair:
                for b in range(2):
                    i = pair * 2 + b
                    dve.wait_ge(y_ready, i + 3)
                    dve.wait_ge(biased, i + 1)
                    nc.vector.tensor_tensor(g.X[:, bass.ds(i, 1), :], g.X[:, bass.ds(i, 1), :], y_ps[:, b:b + 1, :],
                                            ALU.add).then_inc(y_used, 1)


GATES = D // 2
GT = GATES // P
BLK = 8
BI, BO = D // BLK, GATES // BLK
TWO_PI = 2.0 * math.pi
ROUND = 1.5 * 2.0 ** 23
PI_BELOW = 3.1415925


def lru(nc, g):
    with ExitStack() as ctx:
        xh = ctx.enter_context(nc.sbuf_tensor("lru_xh", [P, DT, T], F32))
        z = ctx.enter_context(nc.sbuf_tensor("lru_z", [P, DT, T], F32))
        gates = ctx.enter_context(nc.sbuf_tensor("lru_gates", [P, 2, GT, T], F32))
        normalized_features(nc, g, "lrua", z)
        lru_inputs(nc, g, "lrub", z, xh, gates)
        lru_recurrence(nc, g, "lruc", z, xh, gates)
        lru_outputs(nc, g, "lrud", xh)


def lru_inputs(nc, g, name, z, xh, gates):
    with Layer(nc, name) as L:
        w_in = L.sb("w_in", [P, DT, D])
        wg = L.sb("wg", [P, 2, DT, P])
        b_in = L.sb("b_in", [P, DT])
        b_g = L.sb("b_g", [P, 2, GT])
        x_ps = L.ps("x_ps", [P, 4, NB])
        g_ps = L.ps("g_ps", [P, 4, NB])
        cleared, loaded, blocks_loaded, x_done, x_out, g_done, g_out = (
            L.sem(s) for s in ("cleared", "loaded", "blocks_loaded", "x_done", "x_out", "g_done", "g_out"))
        block = L.block()

        @block.sync
        def _(sp):
            sp.dma_start(w_in[:, :, :], g.dram["L0_attn_a_W_in"].rearrange("(k p) f -> p k f", p=P)).then_inc(loaded, 16)
            sp.dma_start(b_in[:, :], g.dram["L0_attn_a_b_in"].rearrange("(c p) -> p c", p=P),
                         allow_slow_non_contiguous=True).then_inc(loaded, 16)
            for j, n in enumerate(("b_gx", "b_ga")):
                for r in range(GT):
                    for b in range(P // BO):
                        sp.dma_start(b_g[b * BO:(b + 1) * BO, j, r:r + 1], g.dram["L0_attn_a_" + n][r * (P // BO) + b, :].rearrange("(f o) -> f o", o=1),
                                     allow_slow_non_contiguous=True).then_inc(loaded, 16)
            sp.wait_ge(cleared, 1)
            for j, n in enumerate(("W_gx", "W_ga")):
                for k in range(DT):
                    for r in range(2):
                        col = (k % 2) * (2 * BO) + r * BO
                        sp.dma_start(wg[r * BI:(r + 1) * BI, j, k, col:col + BO],
                                     g.dram["L0_attn_a_" + n][2 * k + r, :, :]).then_inc(blocks_loaded, 16)
            sp.wait_ge(loaded, 16 * (2 + 2 * BLK))
            sp.wait_ge(blocks_loaded, 16 * 4 * DT)

        @block.gpsimd
        def _(pool):
            pool.memset(wg[:, :, :, :], 0.0).then_inc(cleared, 1)

        @block.tensor
        def _(pe):
            pe.sem_inc(g_done, 1)
            pe.wait_ge(loaded, 16 * (2 + 2 * BLK))
            pe.wait_ge(blocks_loaded, 16 * 4 * DT)
            with pe.Fori(0, TC) as t:
                for f in range(DT):
                    pe.wait_ge(x_out, t * DT + (f + 1))
                    for k in range(DT):
                        last = nc.tensor.matmul(x_ps[:, f, :], w_in[:, k, f * P:(f + 1) * P], z[:, k, bass.ds(t * NB, NB)],
                                                start=(k == 0), stop=(k == DT - 1))
                    last.then_inc(x_done, 1)
                for j in range(2):
                    for r in range(GT):
                        n = 2 * j + r
                        if j == 0:
                            pe.wait_ge(x_out, t * DT + (2 * r + 2 + DT))
                        pe.wait_ge(g_out, t * 4 + (n + 1))
                        for k in range(2):
                            last = nc.tensor.matmul(g_ps[:, n, :], wg[:, j, 2 * r + k, :], xh[:, 2 * r + k, bass.ds(t * NB, NB)],
                                                    start=(k == 0), stop=(k == 1))
                        last.then_inc(g_done, 1)

        @block.scalar
        def _(act):
            act.sem_inc(x_out, DT)
            act.sem_inc(g_out, 4)
            act.wait_ge(loaded, 16 * (2 + 2 * BLK))
            with act.Fori(0, TC) as t:
                for f in range(DT):
                    act.wait_ge(x_done, t * DT + (f + 1))
                    nc.scalar.activation(xh[:, f, bass.ds(t * NB, NB)], x_ps[:, f, :], ACT.Identity,
                                         bias=b_in[:, f:f + 1]).then_inc(x_out, 1)
                for n in range(4):
                    act.wait_ge(g_done, t * 4 + (n + 2))
                    nc.scalar.activation(gates[:, n // 2, n % 2, bass.ds(t * NB, NB)], g_ps[:, n, :], ACT.Sigmoid,
                                         bias=b_g[:, n // 2, n % 2:n % 2 + 1]).then_inc(g_out, 1)


def lru_recurrence(nc, g, name, z, xh, gates):
    with Layer(nc, name) as L:
        a_real, a_imag, fall = L.sb("a_real", [P, GT]), L.sb("a_imag", [P, GT]), L.sb("fall", [P, GT])
        half_pi = L.sb("half_pi", [P, 1])
        ones = L.sb("ones", [P, NB])
        start = L.sb("start", [P, 4])
        t4, t5, t6, t7 = (L.sb(f"t{n}", [P, T]) for n in range(4, 8))
        t0, t1, t2, t3 = (z[:, k, :] for k in range(4))
        loaded, chain, asked, answered, consts = (L.sem(s) for s in ("loaded", "chain", "asked", "answered", "consts"))
        block = L.block()

        @block.sync
        def _(sp):
            for t, n in ((a_real, "a_real"), (a_imag, "a_imag")):
                sp.dma_start(t[:, :], g.dram["L0_attn_a_" + n].rearrange("(c p) -> p c", p=P),
                             allow_slow_non_contiguous=True).then_inc(loaded, 16)
            sp.wait_ge(loaded, 32)

        @block.scalar
        def _(act):
            link = Chain(act, answered)
            act.wait_ge(loaded, 32)
            act.wait_ge(asked, 1)
            link(nc.scalar.activation(fall[:, :], a_real[:, :], ACT.Abs))
            link(nc.scalar.activation(fall[:, :], fall[:, :], ACT.Exp, scale=-1.0))
            link(nc.scalar.activation(fall[:, :], fall[:, :], ACT.Ln, bias=1.0))
            for r in range(GT):
                act.wait_ge(asked, 5 * r + 2)
                link(nc.scalar.activation(t7[:, :], gates[:, 1, r, :], ACT.Exp, scale=fall[:, r:r + 1]))
                act.wait_ge(asked, 5 * r + 3)
                link(nc.scalar.activation(t2, t1, ACT.Abs))
                link(nc.scalar.activation(t1, t1, ACT.Sin))
                link(nc.scalar.activation(t2, t2, ACT.Sin, scale=-1.0, bias=half_pi[:, 0:1]))
                act.wait_ge(asked, 5 * r + 4)
                link(nc.scalar.activation(t4[:, :], t3, ACT.Abs))
                link(nc.scalar.activation(t3, t3, ACT.Sin))
                link(nc.scalar.activation(t4[:, :], t4[:, :], ACT.Sin, scale=-1.0, bias=half_pi[:, 0:1]))
                act.wait_ge(asked, 5 * r + 5)
                link(nc.scalar.activation(t2, t2, ACT.Sqrt))
                act.wait_ge(asked, 5 * r + 6)
                link(nc.scalar.activation(t2, t2, ACT.Sqrt, scale=0.5))

        @block.vector
        def _(dve):
            link = Chain(dve, chain)
            V = nc.vector

            def mul(out, a, b):
                link(V.tensor_tensor(out, a, b, ALU.mult))

            def add(out, a, b, op=ALU.add):
                link(V.tensor_tensor(out, a, b, op))

            def ask():
                dve.sem_inc(asked, 1)

            def reduce_angle(out, angle, tmp):
                link(V.tensor_scalar(tmp, angle, 1.0 / TWO_PI, ROUND, ALU.mult, ALU.add))
                link(V.tensor_scalar(tmp, tmp, ROUND, -TWO_PI, ALU.subtract, ALU.mult))
                add(out, angle, tmp)
                link(V.tensor_scalar(out, out, PI_BELOW, -PI_BELOW, ALU.min, ALU.max))

            link(V.memset(half_pi[:, :], math.pi / 2))
            link(V.memset(ones[:, :], 1.0))
            ask()
            dve.wait_ge(loaded, 32)
            dve.wait_ge(answered, 3)
            link(V.scalar_tensor_tensor(out=fall[:, :], in0=a_real[:, :], scalar=0.0, in1=fall[:, :], op0=ALU.max, op1=ALU.add))
            link(V.tensor_scalar(fall[:, :], fall[:, :], -8.0, None, ALU.mult))
            got = 3
            for r in range(GT):
                gx, ga = gates[:, 0, r, :], gates[:, 1, r, :]
                xr, xi = xh[:, r, :], xh[:, GT + r, :]
                ask()
                link(V.tensor_scalar(t0, ga, a_imag[:, r:r + 1], None, ALU.mult))
                reduce_angle(t1, t0, t2)
                ask()
                for c in range(TC):
                    cols = slice(c * NB, (c + 1) * NB)
                    if c:
                        reduce_angle(start[:, 0:1], t3[:, c * NB - 1:c * NB], start[:, 1:2])
                    link(V.tensor_tensor_scan(t3[:, cols], ones[:, :], t0[:, cols], start[:, 0:1] if c else 0.0, ALU.mult, ALU.add))
                reduce_angle(t3, t3, t0)
                ask()
                mul(xr, xr, gx)
                mul(xi, xi, gx)
                dve.wait_ge(answered, got + 4)
                mul(t0, t7[:, :], t7[:, :])
                mul(t2, t1, t2)
                link(V.scalar_tensor_tensor(out=t5[:, :], in0=t2, scalar=-2.0, in1=t0, op0=ALU.mult, op1=ALU.mult))
                mul(t1, t1, t1)
                link(V.tensor_scalar(t1, t1, 2.0, -1.0, ALU.mult, ALU.add))
                mul(t1, t1, t0)
                link(V.tensor_scalar(t6[:, :], t1, 1.0, None, ALU.add))
                mul(t0, t6[:, :], t6[:, :])
                mul(t1, t5[:, :], t5[:, :])
                link(V.scalar_tensor_tensor(out=t2, in0=t0, scalar=1e-30, in1=t1, op0=ALU.max, op1=ALU.add))
                ask()
                dve.wait_ge(answered, got + 8)
                link(V.scalar_tensor_tensor(out=t2, in0=t6[:, :], scalar=0.0, in1=t2, op0=ALU.max, op1=ALU.add))
                ask()
                dve.wait_ge(answered, got + 9)
                link(V.reciprocal(t0, t2))
                link(V.scalar_tensor_tensor(out=t5[:, :], in0=t5[:, :], scalar=0.5, in1=t0, op0=ALU.mult, op1=ALU.mult))

                def rotate(out_r, out_i, cr, ci, tmp, tmp2, sign):
                    mul(tmp, ci, xi)
                    mul(tmp2, ci, xr)
                    mul(xr, cr, xr)
                    mul(xi, cr, xi)
                    add(out_r, xr, tmp, ALU.subtract if sign > 0 else ALU.add)
                    add(out_i, xi, tmp2, ALU.add if sign > 0 else ALU.subtract)

                rotate(xr, xi, t2, t5[:, :], t0, t1, 1)
                rotate(xr, xi, t4[:, :], t3, t0, t1, -1)
                link(V.tensor_tensor_scan(t0, t7[:, :], xr, 0.0, ALU.mult, ALU.add))
                link(V.tensor_tensor_scan(t1, t7[:, :], xi, 0.0, ALU.mult, ALU.add))
                mul(xr, t4[:, :], t0)
                mul(t2, t3, t1)
                add(xr, xr, t2, ALU.subtract)
                mul(xi, t4[:, :], t1)
                mul(t2, t3, t0)
                add(xi, xi, t2)
                got += 9


def lru_outputs(nc, g, name, h):
    with nc.sbuf_tensor(f"{name}_w", [P, DT, D], F32) as w:
        with Layer(nc, name + "l") as L:
            loaded = L.sem("loaded")
            block = L.block()

            @block.sync
            def _(sp):
                sp.dma_start(w[:, :, :], g.dram["L0_attn_a_W_out"].rearrange("(k p) f -> p k f", p=P)).then_inc(loaded, 16)
                sp.wait_ge(loaded, 16)
        project_and_add(nc, g, name, h, w, g.dram["L0_attn_a_b_out"])


def binarized_weight(nc, g):
    with Layer(nc, "binw") as L:
        w = L.sb("w", [P, DT, D])
        size = L.sb("size", [P, DT, D])
        alpha = L.sb("alpha", [P, DT])
        bw = L.sb("bw", [P, DT, D])
        wt_ps = L.ps("wt_ps", [P, 2, D])
        loaded, chain, w_ready, wt_done, copied = (L.sem(s) for s in ("loaded", "chain", "w_ready", "wt_done", "copied"))
        block = L.block()

        @block.sync
        def _(sp):
            sp.dma_start(w[:, :, :], g.dram["L0_ffn_weight"].rearrange("(c p) i -> p c i", p=P)).then_inc(loaded, 16)
            sp.dma_start(g.ffn_bias[:, :], g.dram["L0_ffn_bias"].partition_broadcast(P)).then_inc(loaded, 16)
            sp.wait_ge(loaded, 32)

        @block.vector
        def _(dve):
            link = Chain(dve, chain)
            dve.wait_ge(loaded, 32)
            link(nc.vector.tensor_scalar(size[:, :, :], w[:, :, :], -1.0, None, ALU.mult))
            link(nc.vector.tensor_tensor(size[:, :, :], size[:, :, :], w[:, :, :], ALU.max))
            link(nc.vector.tensor_reduce(alpha[:, :], size[:, :, :], axis=AX.X, op=ALU.add))
            link(nc.vector.tensor_scalar(alpha[:, :], alpha[:, :], 1.0 / D, None, ALU.mult))
            link(nc.vector.tensor_scalar(bw[:, :, :], w[:, :, :], 0.0, 2.0, ALU.is_ge, ALU.mult))
            link(nc.vector.tensor_scalar(bw[:, :, :], bw[:, :, :], -1.0, None, ALU.add))
            for c in range(DT):
                link(nc.vector.tensor_scalar(bw[:, c, :], bw[:, c, :], alpha[:, c:c + 1], None, ALU.mult))
            link(nc.vector.tensor_tensor(bw[:, :, :], bw[:, :, :], w[:, :, :], ALU.subtract))
            nc.vector.tensor_tensor(bw[:, :, :], bw[:, :, :], w[:, :, :], ALU.add).then_inc(w_ready, 1)

        @block.tensor
        def _(pe):
            pe.wait_ge(w_ready, 1)
            for k in range(DT):
                if k >= 2:
                    pe.wait_ge(copied, k - 1)
                for c in range(DT):
                    last = nc.tensor.transpose(wt_ps[:, k % 2, c * P:(c + 1) * P], bw[:, c, k * P:(k + 1) * P], g.ident[:, :])
                last.then_inc(wt_done, 1)

        @block.scalar
        def _(act):
            for k in range(DT):
                act.wait_ge(wt_done, k + 1)
                nc.scalar.copy(g.ffn_wt[:, k, :], wt_ps[:, k % 2, :]).then_inc(copied, 1)


def ffn(nc, g, name):
    with Layer(nc, name) as L:
        norm = Norm(L, nc, g.X)
        z = L.sb("z", [P, 2, D])
        zt = L.sb("zt", [P, 2, D])
        zt_ps = L.ps("zt_ps", [P, 2, D])
        y_ps = L.ps("y_ps", [P, 2, D])
        z_ready, z_used, zt_done, zt_ready, y_ready, y_used, biased = (
            L.sem(s) for s in ("z_ready", "z_used", "zt_done", "zt_ready", "y_ready", "y_used", "biased"))
        block = L.block()

        @block.vector
        def _(dve):
            norm.on_vector(dve)
            mv, rstd = norm.mv, norm.rstd

            def normalize(i, b):
                nc.vector.tensor_scalar(z[:, b, :], g.X[:, i, :], mv[:, i, 0:1], rstd[:, i:i + 1],
                                        ALU.subtract, ALU.mult).then_inc(z_ready, 1)

            normalize(0, 0)
            normalize(1, 1)
            with dve.Fori(0, TT // 2 - 1) as pair:
                for b in range(2):
                    i = pair * 2 + b
                    dve.wait_ge(y_ready, i + 1)
                    dve.wait_ge(biased, i + 1)
                    nc.vector.tensor_tensor(g.X[:, bass.ds(i, 1), :], g.X[:, bass.ds(i, 1), :], y_ps[:, b:b + 1, :], ALU.add).then_inc(y_used, 1)
                    nc.vector.tensor_scalar(z[:, b:b + 1, :], g.X[:, bass.ds(i + 2, 1), :], mv[:, bass.ds(i + 2, 1), 0:1],
                                            rstd[:, bass.ds(i + 2, 1)], ALU.subtract, ALU.mult).then_inc(z_ready, 1)
            for b in range(2):
                dve.wait_ge(y_ready, TT - 1 + b)
                dve.wait_ge(biased, TT - 1 + b)
                nc.vector.tensor_tensor(g.X[:, TT - 2 + b, :], g.X[:, TT - 2 + b, :], y_ps[:, b, :], ALU.add).then_inc(y_used, 1)

        @block.gpsimd
        def _(pool):
            with pool.Fori(0, TT) as i:
                pool.wait_ge(z_ready, i + 1)
                nc.gpsimd.tensor_tensor(g.X[:, bass.ds(i, 1), :], g.X[:, bass.ds(i, 1), :],
                                        g.ffn_bias[:, :].rearrange("p (o d) -> p o d", o=1), ALU.add).then_inc(biased, 1)

        @block.tensor
        def _(pe):
            with pe.Fori(0, TT // 2) as pair:
                for b in range(2):
                    pe.wait_ge(z_ready, pair * 2 + b + 1)
                    for k in range(DT):
                        last = nc.tensor.transpose(zt_ps[:, b, k * P:(k + 1) * P], z[:, b, k * P:(k + 1) * P], g.ident[:, :])
                    last.then_inc(zt_done, 1)
                for b in range(2):
                    pe.wait_ge(zt_ready, pair * 2 + b + 1)
                    for k in range(DT):
                        last = nc.tensor.matmul(y_ps[:, b, :], zt[:, b, k * P:(k + 1) * P], g.ffn_wt[:, k, :],
                                                start=(k == 0), stop=(k == DT - 1))
                    last.then_inc(y_ready, 1)

        @block.scalar
        def _(act):
            norm.on_scalar(act)
            with act.Fori(0, TT // 2) as pair:
                for b in range(2):
                    act.wait_ge(zt_done, pair * 2 + b + 1)
                    nc.scalar.copy(zt[:, b, :], zt_ps[:, b, :]).then_inc(zt_ready, 1)


N_STATE = 16
Q = 4
DT_MIN = 1e-4


def ssm(nc, g):
    with nc.sbuf_tensor("ssm_u", [P, DT, T], F32) as u:
        normalized_features(nc, g, "ssma", u)
        ssm_scan(nc, g, "ssmb", u)


def ssm_scan(nc, g, name, u):
    with Layer(nc, name) as L:
        bias = L.sb("bias", [P, 4, DT])
        a_raw, b_base, c_base = (L.sb(s, [P, DT, N_STATE]) for s in ("a_raw", "b_base", "c_base"))
        a_pos = L.sb("a_pos", [P, DT, N_STATE])
        rate = L.sb("rate", [P, DT, N_STATE])
        gain = L.sb("gain", [P, DT, N_STATE])
        w = L.sb("w", [P, 2, 3, DT, P])
        raw, soft = L.sb("raw", [P, NB]), L.sb("soft", [P, NB])
        dt, bu, c = (L.sb(s, [P, 2, T]) for s in ("dt", "bu", "c"))
        decay = L.sb("decay", [P, 2, T])
        state = L.sb("state", [P, Q, T])
        diag = L.sb("diag", [P, Q, P])
        zero16 = L.sb("zero16", [P, P], BF16)
        zcol16 = L.sb("zcol16", [P, NB], BF16)
        y = L.sb("y", [P, T])
        y_ps = L.ps("y_ps", [P, TC, NB])
        pr_ps = L.ps("pr_ps", [P, 3, NB])
        tr_ps = L.ps("tr_ps", [P, 4, P])
        (par_loaded, a_abs, consts, zeroed, w_loaded0, w_loaded1, pr_done, raw_out, c_out, b_out, soft_done, dt_done, decay_done,
         state_done, diag_done, summed, y_full, y_read, y_done, tr_done, added, chain, achain, pchain, dt_half, bu_done) = (
            L.sem(s) for s in ("par_loaded", "a_abs", "consts", "zeroed", "w_loaded0", "w_loaded1", "pr_done", "raw_out", "c_out",
                               "b_out", "soft_done", "dt_done", "decay_done", "state_done", "diag_done", "summed", "y_full",
                               "y_read", "y_done", "tr_done", "added", "chain", "achain", "pchain",
                               "dt_half", "bu_done"))
        w_loaded = (w_loaded0, w_loaded1)
        block = L.block()

        @block.sync
        def _(sp):
            for j, n in enumerate(("bdt", "bb", "bc", "D")):
                sp.dma_start(bias[:, j, :], g.dram["L0_attn_b_" + n].rearrange("(c p) -> p c", p=P),
                             allow_slow_non_contiguous=True).then_inc(par_loaded, 16)
            for t, n in ((a_raw, "a_raw"), (b_base, "B_base"), (c_base, "C_base")):
                sp.dma_start(t[:, :, :], g.dram["L0_attn_b_" + n].rearrange("(c p) n -> p c n", p=P)).then_inc(par_loaded, 16)
            for e in range(DT):
                if e >= 2:
                    sp.wait_ge(pr_done, (e - 1) * TC)
                for j, n in enumerate(("Wdt", "Wb", "Wc")):
                    sp.dma_start(w[:, e % 2, j, :, :], g.dram["L0_attn_b_" + n][:, e * P:(e + 1) * P]
                                 .rearrange("(k p) f -> p k f", p=P)).then_inc(w_loaded[e % 2], 16)
            sp.wait_ge(par_loaded, 16 * 7)
            for b in range(2):
                sp.wait_ge(w_loaded[b], 2 * 48)

        @block.gpsimd
        def _(pool):
            pool.memset(zero16[:, :], 0.0).then_inc(zeroed, 1)
            pool.memset(zcol16[:, :], 0.0).then_inc(zeroed, 1)
            pool.wait_ge(par_loaded, 16 * 7)
            pool.tensor_tensor(gain[:, :, :], b_base[:, :, :], c_base[:, :, :], ALU.mult).then_inc(pchain, 1)
            pool.wait_ge(pchain, 1)
            gains = gain[:, :, :].rearrange("p c n -> p (c n)")
            with pool.Fori(0, DT * N_STATE // Q) as r:
                for j in range(Q):
                    pool.wait_ge(summed, r * Q + (j + 1))
                    pool.tensor_tensor(diag[:, j, :], g.ident[:, :], gains[:, bass.ds(r * Q + j, 1)].to_broadcast([P, P]),
                                       ALU.mult).then_inc(diag_done, 1)

        @block.tensor
        def _(pe):
            def products(e, tq):
                m = tq + e * TC
                if e == 0:
                    pe.wait_ge(w_loaded[0], 48)
                else:
                    pe.wait_ge(w_loaded[e % 2], 48 * (e // 2 + 1))
                for j, out in enumerate((raw_out, b_out, c_out)):
                    pe.wait_ge(out, m + 1)
                    for k in range(DT):
                        last = nc.tensor.matmul(pr_ps[:, j, :], w[:, e % 2, j, k, :], u[:, k, bass.ds(tq * NB, NB)],
                                                start=(k == 0), stop=(k == DT - 1))
                last.then_inc(pr_done, 1)

            def back(e):
                pe.wait_ge(y_done, e + 1)
                for t in range(TC):
                    pe.wait_ge(added, t + (e * TC + 1))
                    for s in range(4):
                        last = nc.tensor.transpose(tr_ps[:, s, :], y[:, t * NB + s * P:t * NB + (s + 1) * P], g.ident[:, :])
                    last.then_inc(tr_done, 1)

            pe.sem_inc(summed, Q)
            pe.wait_ge(zeroed, 2)
            with pe.Fori(0, TC) as tq:
                products(0, tq)
            for e in range(DT):
                if e >= 1:
                    pe.wait_ge(y_read, e)
                for t in range(TC):
                    nc.tensor.matmul(y_ps[:, t, :], zero16[:, :], zcol16[:, :], start=True, stop=False)
                if e >= 1:
                    back(e - 1)
                with pe.Fori(0, TC) as tq:
                    if e + 1 < DT:
                        products(e + 1, tq)
                    for j in range(Q):
                        n = tq * Q + (e * N_STATE + j)
                        pe.wait_ge(state_done, n + 3)
                        pe.wait_ge(diag_done, n + 1)
                        for t in range(TC):
                            last = nc.tensor.matmul(y_ps[:, t, :], diag[:, j, :], state[:, j, t * NB:(t + 1) * NB],
                                                    start=False, stop=False)
                        last.then_inc(summed, 1)
                for t in range(TC):
                    last = nc.tensor.matmul(y_ps[:, t, :], zero16[:, :], zcol16[:, :], start=False, stop=True)
                last.then_inc(y_full, 1)
            back(DT - 1)

        @block.scalar
        def _(act):
            link = Chain(act, achain)
            act.wait_ge(par_loaded, 16 * 7)
            act.sem_inc(raw_out, 1)
            act.sem_inc(c_out, 1)
            link(nc.scalar.activation(rate[:, :, :], a_raw[:, :, :], ACT.Abs))
            link(nc.scalar.activation(rate[:, :, :], rate[:, :, :], ACT.Exp, scale=-1.0))
            nc.scalar.activation(a_pos[:, :, :], rate[:, :, :], ACT.Ln, bias=1.0).then_inc(a_abs, 1)
            act.wait_ge(consts, 1)

            def evacuate(e, tq):
                m = tq + e * TC
                cols = bass.ds(tq * NB, NB)
                act.wait_ge(pr_done, m + 1)
                if e >= 2:
                    act.wait_ge(y_read, e - 1)
                act.wait_ge(dt_done, m + 1)
                nc.scalar.activation(raw[:, :], pr_ps[:, 0, :], ACT.Identity, bias=bias[:, 0, e:e + 1]).then_inc(raw_out, 1)
                nc.scalar.activation(c[:, e % 2, cols], pr_ps[:, 2, :], ACT.Identity, bias=bias[:, 2, e:e + 1]).then_inc(c_out, 1)
                act.wait_ge(raw_out, m + 2)
                nc.scalar.activation(soft[:, :], raw[:, :], ACT.Abs).then_inc(achain, 1)
                act.wait_ge(achain, tq * 2 + (2 + e * TC * 2 + 1))
                nc.scalar.activation(soft[:, :], soft[:, :], ACT.Exp, scale=-1.0).then_inc(achain, 1)
                act.wait_ge(achain, tq * 2 + (2 + e * TC * 2 + 2))
                nc.scalar.activation(soft[:, :], soft[:, :], ACT.Ln, bias=1.0).then_inc(soft_done, 1)

            with act.Fori(0, TC) as tq:
                evacuate(0, tq)
            for e in range(DT):
                act.wait_ge(dt_done, e * TC + TC + 1)
                with act.Fori(0, TC) as tq:
                    for j in range(Q):
                        n = tq * Q + (e * N_STATE + j)
                        act.wait_ge(state_done, n + 1)
                        nc.scalar.activation(decay[:, j % 2, :], dt[:, e % 2, :], ACT.Exp,
                                             scale=rate[:, e, bass.ds(tq * Q + j, 1)]).then_inc(decay_done, 1)
                    if e + 1 < DT:
                        evacuate(e + 1, tq)

        @block.vector
        def _(dve):
            link = Chain(dve, chain)
            dve.sem_inc(state_done, 2)
            dve.sem_inc(dt_done, 1)
            dve.sem_inc(b_out, 1)
            dve.sem_inc(added, 1)
            dve.wait_ge(par_loaded, 16 * 7)
            dve.wait_ge(a_abs, 1)
            link(nc.vector.scalar_tensor_tensor(out=a_pos[:, :, :], in0=a_raw[:, :, :], scalar=0.0, in1=a_pos[:, :, :],
                                                op0=ALU.max, op1=ALU.add))
            nc.vector.tensor_scalar(rate[:, :, :], a_pos[:, :, :], -1.0, None, ALU.mult).then_inc(consts, 1)

            def chunk(e, tq):
                m = tq + e * TC
                cols = bass.ds(tq * NB, NB)
                dve.wait_ge(pr_done, m + 1)
                nc.vector.scalar_tensor_tensor(out=bu[:, e % 2, cols], in0=pr_ps[:, 1, :], scalar=bias[:, 1, e:e + 1],
                                               in1=u[:, e, cols], op0=ALU.add, op1=ALU.mult).then_inc(b_out, 1)
                dve.wait_ge(soft_done, m + 1)
                if e >= 2:
                    dve.wait_ge(decay_done, (e - 1) * N_STATE)
                nc.vector.scalar_tensor_tensor(out=dt[:, e % 2, cols], in0=raw[:, :], scalar=0.0, in1=soft[:, :],
                                               op0=ALU.max, op1=ALU.add).then_inc(dt_half, 1)
                dve.wait_ge(dt_half, m + 1)
                dve.wait_ge(b_out, m + 2)
                nc.vector.tensor_scalar(dt[:, e % 2, cols], dt[:, e % 2, cols], DT_MIN, None, ALU.add).then_inc(dt_done, 1)
                dve.wait_ge(dt_done, m + 2)
                nc.vector.tensor_tensor(bu[:, e % 2, cols], bu[:, e % 2, cols], dt[:, e % 2, cols], ALU.mult).then_inc(bu_done, 1)

            def add_back(e, tq):
                dve.wait_ge(tr_done, tq + (e * TC + 1))
                nc.vector.tensor_tensor(g.X[:, bass.ds(tq * 4, 4), e * P:(e + 1) * P], g.X[:, bass.ds(tq * 4, 4), e * P:(e + 1) * P],
                                        tr_ps[:, :, :], ALU.add).then_inc(added, 1)

            with dve.Fori(0, TC) as tq:
                chunk(0, tq)
            for e in range(DT):
                dve.wait_ge(bu_done, (e + 1) * TC)
                if e >= 1:
                    with dve.Fori(0, TC) as tq:
                        add_back(e - 1, tq)
                with dve.Fori(0, TC) as tq:
                    for j in range(Q):
                        n = tq * Q + (e * N_STATE + j)
                        dve.wait_ge(decay_done, n + 1)
                        dve.wait_ge(summed, n + 1)
                        nc.vector.tensor_tensor_scan(state[:, j, :], decay[:, j % 2, :], bu[:, e % 2, :], 0.0,
                                                     ALU.mult, ALU.add).then_inc(state_done, 1)
                    if e + 1 < DT:
                        chunk(e + 1, tq)
                dve.wait_ge(y_full, e + 1)
                nc.vector.tensor_tensor(y[:, :], y_ps[:, :, :].rearrange("p t n -> p (t n)"), c[:, e % 2, :], ALU.mult).then_inc(y_read, 1)
                dve.wait_ge(y_read, e + 1)
                nc.vector.scalar_tensor_tensor(out=y[:, :], in0=u[:, e, :], scalar=bias[:, 3, e:e + 1], in1=y[:, :],
                                               op0=ALU.mult, op1=ALU.add).then_inc(y_done, 1)
            with dve.Fori(0, TC) as tq:
                add_back(DT - 1, tq)


HEADS = 16
DH = D // HEADS
SBLK = 1024
PARTS = 3
STACK = PARTS * DH
ST = SBLK // P


def transpose_weight(nc, g, name, dram_w, wt):
    tiles = dram_w.shape[0] // P
    with Layer(nc, name) as L:
        w = L.sb("w", [P, tiles, D])
        w_ps = L.ps("w_ps", [P, 2, DT, P])
        loaded, done, out = (L.sem(s) for s in ("loaded", "done", "out"))
        block = L.block()

        @block.sync
        def _(sp):
            sp.dma_start(w[:, :, :], dram_w.rearrange("(c p) i -> p c i", p=P)).then_inc(loaded, 16)
            sp.wait_ge(loaded, 16)

        @block.tensor
        def _(pe):
            pe.wait_ge(loaded, 16)
            for c in range(tiles):
                if c >= 2:
                    pe.wait_ge(out, c - 1)
                for k in range(DT):
                    last = nc.tensor.transpose(w_ps[:, c % 2, k, :], w[:, c, k * P:(k + 1) * P], g.ident[:, :])
                last.then_inc(done, 1)

        @block.scalar
        def _(act):
            for c in range(tiles):
                act.wait_ge(done, c + 1)
                nc.scalar.copy(wt[:, :, c * P:(c + 1) * P], w_ps[:, c % 2, :, :]).then_inc(out, 1)


def attention(nc, g):
    with ExitStack() as ctx:
        v = ctx.enter_context(nc.sbuf_tensor("att_v", [P, TT, HEADS, PARTS + 1, DH], BF16))
        with ExitStack() as inner:
            z = inner.enter_context(nc.sbuf_tensor("att_z", [P, DT, T], F32))
            wt = [inner.enter_context(nc.sbuf_tensor(f"att_wt{j}", [P, DT, D], F32)) for j in range(3)]
            normalized_features(nc, g, "atta", z)
            for j, n in enumerate(("Wq", "Wk", "Wv")):
                transpose_weight(nc, g, f"attw{j}", g.dram["L1_attn_a_" + n], wt[j])
            attention_inputs(nc, g, "attb", z, wt, v)
        attention_heads(nc, g, "attc", v)
    with ExitStack() as ctx:
        o = ctx.enter_context(nc.sbuf_tensor("att_o", [P, PARTS, DT, T], F32))
        wo = ctx.enter_context(nc.sbuf_tensor("att_wo", [P, DT, D], F32))
        transpose_weight(nc, g, "attd", g.dram["L1_attn_a_Wo"], wo)
        attention_outputs(nc, g, "atte", o, wo)


def attention_inputs(nc, g, name, z, wt, v):
    with Layer(nc, name) as L:
        b_qk = L.sb("b_qk", [P, 2, DT])
        rot = L.sb("rot", [P, DT])
        tmp = L.sb("tmp", [P, DT])
        scale = L.sb("scale", [P, 2, DT])
        spiral = L.sb("spiral", [P, DT])
        half_pi = L.sb("half_pi", [P, 1])
        bv = L.sb("bv", [P, D])
        whole, rest = L.sb("whole", [P, 2, NB]), L.sb("rest", [P, 2, NB])
        parts = L.sb("parts", [P, 2, PARTS, NB], BF16)
        zt = L.sb("zt", [P, 2, DT, P])
        p_ps = L.ps("p_ps", [P, 2, NB])
        v_ps = L.ps("v_ps", [P, 2, NB])
        (loaded, chain, reduced, angles, consts, prod, whole_out, split_chain, split_done, zt_ready, v_done, v_out, split_step, v_step, ones_set) = (
            L.sem(s) for s in ("loaded", "chain", "reduced", "angles", "consts", "prod", "whole_out", "split_chain", "split_done",
                               "zt_ready", "v_done", "v_out", "split_step", "v_step", "ones_set"))
        saved = [L.sem(f"saved{b}") for b in range(2)]
        block = L.block()
        FT = 2 * DT
        N_PAR = 2 + 1 + 1 + HEADS

        @block.sync
        def _(sp):
            for j, n in enumerate(("bq", "bk")):
                sp.dma_start(b_qk[:, j, :], g.dram["L1_attn_a_" + n].rearrange("(c p) -> p c", p=P),
                             allow_slow_non_contiguous=True).then_inc(loaded, 16)
            sp.dma_start(rot[:, :], g.dram["L1_attn_a_helix_rotation"].rearrange("(c p) -> p c", p=P),
                         allow_slow_non_contiguous=True).then_inc(loaded, 16)
            sp.dma_start(bv[:, :], g.dram["L1_attn_a_bv"].partition_broadcast(P)).then_inc(loaded, 16)
            for h in range(HEADS):
                r = (h % (P // DH)) * DH
                sp.dma_start(spiral[r:r + DH, h // (P // DH):h // (P // DH) + 1],
                             g.dram["L1_attn_a_spiral_weight"][h:h + 1].partition_broadcast(DH)).then_inc(loaded, 16)
            for j in range(2):
                dst = g.qk_dram[j].rearrange("r (c p) t -> p c r t", p=P)
                with sp.Fori(0, TC) as t:
                    for f in range(DT):
                        sp.wait_ge(split_done, t * DT + (j * TC * DT + f + 1))
                        sp.dma_start(dst[:, f, :, bass.ds(t * NB, NB)], parts[:, f % 2, :, :]).then_inc(saved[f % 2], 16)
            for b in range(2):
                sp.wait_ge(saved[b], 16 * (TC * FT // 2 + 1))

        @block.gpsimd
        def _(pool):
            pool.memset(v[:, :, :, PARTS, :], 1.0).then_inc(ones_set, 1)

        @block.tensor
        def _(pe):
            def product(j, f, t, m):
                pe.wait_ge(whole_out, m + 1)
                for k in range(DT):
                    last = nc.tensor.matmul(p_ps[:, f % 2, :], wt[j][:, k, f * P:(f + 1) * P], z[:, k, bass.ds(t * NB, NB)],
                                            start=(k == 0), stop=(k == DT - 1))
                last.then_inc(prod, 1)

            for j in range(2):
                with pe.Fori(0, TC) as t:
                    for f in range(DT):
                        product(j, f, t, t * DT + (j * TC * DT + f))
            pe.sem_inc(v_done, 2)
            with pe.Fori(0, TT // 2) as pair:
                for b in range(2):
                    i = pair * 2 + b
                    pe.wait_ge(zt_ready, i + 1)
                    pe.wait_ge(v_out, i + 1)
                    for k in range(DT):
                        last = nc.tensor.matmul(v_ps[:, b, :], zt[:, b, k, :], wt[2][:, k, :], start=(k == 0), stop=(k == DT - 1))
                    last.then_inc(v_done, 1)

        @block.scalar
        def _(act):
            act.sem_inc(whole_out, 2)
            act.wait_ge(reduced, 1)
            nc.scalar.activation(scale[:, 1, :], rot[:, :], ACT.Sin).then_inc(angles, 1)
            nc.scalar.activation(tmp[:, :], rot[:, :], ACT.Abs).then_inc(angles, 1)
            act.wait_ge(angles, 2)
            nc.scalar.activation(scale[:, 0, :], tmp[:, :], ACT.Sin, scale=-1.0, bias=half_pi[:, 0:1]).then_inc(angles, 1)
            act.wait_ge(consts, 1)
            for j in range(2):
                with act.Fori(0, TC) as t:
                    for f in range(DT):
                        m = t * DT + (j * TC * DT + f)
                        act.wait_ge(prod, m + 1)
                        act.wait_ge(split_chain, m * 2 + 2)
                        nc.scalar.activation(whole[:, f % 2, :], p_ps[:, f % 2, :], ACT.Identity, scale=scale[:, j, f:f + 1],
                                             bias=b_qk[:, j, f:f + 1]).then_inc(whole_out, 1)
            with act.Fori(0, TT // 2) as pair:
                for b in range(2):
                    act.wait_ge(v_done, pair * 2 + (b + 1))
                    nc.scalar.copy(zt[:, b, :, :], z[:, :, bass.ds((pair * 2 + b) * P, P)]).then_inc(zt_ready, 1)

        @block.vector
        def _(dve):
            link = Chain(dve, chain)
            V = nc.vector
            dve.sem_inc(split_chain, 4)
            dve.sem_inc(saved[0], 16)
            dve.sem_inc(saved[1], 16)
            dve.sem_inc(v_out, 2)
            dve.wait_ge(loaded, 16 * N_PAR)
            link(V.memset(half_pi[:, :], math.pi / 2))
            link(V.tensor_scalar(tmp[:, :], rot[:, :], 1.0 / TWO_PI, ROUND, ALU.mult, ALU.add))
            link(V.tensor_scalar(tmp[:, :], tmp[:, :], ROUND, -TWO_PI, ALU.subtract, ALU.mult))
            link(V.tensor_tensor(rot[:, :], rot[:, :], tmp[:, :], ALU.add))
            V.tensor_scalar(rot[:, :], rot[:, :], PI_BELOW, -PI_BELOW, ALU.min, ALU.max).then_inc(reduced, 1)
            dve.wait_ge(angles, 3)
            link(V.tensor_scalar(spiral[:, :], spiral[:, :], 1.0 / math.sqrt(DH), None, ALU.mult))
            link(V.tensor_tensor(scale[:, 0, :], scale[:, 0, :], spiral[:, :], ALU.mult))
            V.tensor_tensor(b_qk[:, :, :], b_qk[:, :, :], scale[:, :, :], ALU.mult).then_inc(consts, 1)
            for j in range(2):
                with dve.Fori(0, TC) as t:
                    for f in range(DT):
                        m = t * DT + (j * TC * DT + f)
                        b = f % 2
                        dve.wait_ge(whole_out, m + 3)
                        dve.wait_ge(saved[b], t * 32 + (j * TC * 32 + (f // 2) * 16 + 16))
                        V.tensor_copy(parts[:, b, 0, :], whole[:, b, :]).then_inc(split_step, 1)
                        dve.wait_ge(split_step, m * 3 + 1)
                        V.tensor_tensor(rest[:, b, :], whole[:, b, :], parts[:, b, 0, :], ALU.subtract).then_inc(split_chain, 2)
                        dve.wait_ge(split_chain, m * 2 + 6)
                        V.tensor_copy(parts[:, b, 1, :], rest[:, b, :]).then_inc(split_step, 2)
                        dve.wait_ge(split_step, m * 3 + 3)
                        V.tensor_tensor(parts[:, b, 2, :], rest[:, b, :], parts[:, b, 1, :], ALU.subtract).then_inc(split_done, 1)
            with dve.Fori(0, TT // 2) as pair:
                for b in range(2):
                    i = pair * 2 + b
                    dve.wait_ge(v_done, i + 3)
                    V.tensor_tensor(whole[:, b, :], v_ps[:, b, :], bv[:, :], ALU.add).then_inc(v_out, 1)
                    dve.wait_ge(v_out, i + 3)
                    heads = whole[:, b, :].rearrange("p (o h d) -> p o h d", o=1, h=HEADS)
                    rests = rest[:, b, :].rearrange("p (o h d) -> p o h d", o=1, h=HEADS)
                    part = [v[:, bass.ds(i, 1), :, r, :] for r in range(PARTS)]
                    V.tensor_copy(part[0], heads).then_inc(v_step, 1)
                    dve.wait_ge(v_step, i * 4 + 1)
                    V.tensor_tensor(rests, heads, part[0], ALU.subtract).then_inc(v_step, 1)
                    dve.wait_ge(v_step, i * 4 + 2)
                    V.tensor_copy(part[1], rests).then_inc(v_step, 1)
                    dve.wait_ge(v_step, i * 4 + 3)
                    V.tensor_tensor(part[2], rests, part[1], ALU.subtract).then_inc(v_step, 1)


def attention_heads(nc, g, name, v):
    with Layer(nc, name) as L:
        NSB = T // SBLK
        HB = SBLK // NB
        UNITS = NSB * TT
        PIECES = TT * TC
        NP = 4
        LAG = 2
        LOADS = 4 * PARTS * 16
        qm, km = L.sb("qm", [STACK, T], BF16), L.sb("km", [STACK, T], BF16)
        q1, k1 = L.sb("q1", [STACK + 3, 2, T], BF16), L.sb("k1", [STACK + 3, 2, T], BF16)
        q2, k2 = L.sb("q2", [STACK, 2, T], BF16), L.sb("k2", [STACK, 2, T], BF16)
        prob = L.sb("prob", [P, NP, SBLK])
        low = L.sb("low", [P, NP, SBLK], BF16)
        peak = L.sb("peak", [P, TT, TC])
        neg, left = L.sb("neg", [P, TT]), L.sb("left", [P, TT])
        negp = L.sb("negp", [P, P // TT, TT], BF16)
        rows = L.sb("rows", [3 * TT, P], BF16)
        out = L.sb("out", [P, 2, SBLK])
        sc_ps = L.ps("sc_ps", [P, 2, HB, NB])
        o_ps = L.ps("o_ps", [P, HB, NB])
        mx_ps = L.ps("mx_ps", [P, 2, NB])
        high = prob[:, :, :].bitcast(BF16).rearrange("p n (s two) -> p n s two", two=2)[:, :, :, 1]
        rows_ps = mx_ps[:, 0, :].bitcast(BF16)[:, 0:P]
        (ones_ready, m_loaded, low_pool, low_vector, sc_done, exp_done, pv_done, o_done, mx_done, mx_used, neg_step, neg_done,
         rows_done, rows_ready, rows_saved, out_ready) = (
            L.sem(s) for s in ("ones_ready", "m_loaded", "low_pool", "low_vector", "sc_done", "exp_done", "pv_done", "o_done",
                               "mx_done", "mx_used", "neg_step", "neg_done", "rows_done", "rows_ready", "rows_saved",
                               "out_ready"))
        taken = L.sem("taken")
        loaded = [L.sem(f"loaded{b}") for b in range(2)]
        out_saved = [L.sem(f"out_saved{b}") for b in range(2)]
        block = L.block()
        PAIRS = HEADS // 2

        RATE = 2.5
        pieces = [range(min(PIECES, math.ceil(RATE * w)), min(PIECES, math.ceil(RATE * (w + 1)))) for w in range(UNITS)]
        NEGATE = next(w for w in range(UNITS) if pieces[w].stop == PIECES)
        ROWS = NEGATE + 3
        pool_units = [w for w in range(UNITS) if w % 3 == 2]
        vector_units = [w for w in range(UNITS) if w % 3 != 2]

        @block.sync
        def _(sp):
            def stack(dst, j, order, h, sem):
                for r, part in enumerate(order):
                    sp.dma_start(dst[r * DH:(r + 1) * DH, :], g.qk_dram[j][part, bass.ds(h * DH, DH), :]).then_inc(sem, 16)

            def load_max(h):
                stack(qm[:, :], 0, (0, 0, 1), h, m_loaded)
                stack(km[:, :], 1, (0, 1, 0), h, m_loaded)

            def load_head(h, b):
                stack(q1[0:STACK, b, :], 0, (0, 0, 1), h, loaded[b])
                stack(k1[0:STACK, b, :], 1, (0, 1, 0), h, loaded[b])
                stack(q2[:, b, :], 0, (1, 0, 2), h, loaded[b])
                stack(k2[:, b, :], 1, (1, 2, 0), h, loaded[b])

            def load_rows(h, b):
                sp.wait_ge(rows_ready, h + 1)
                sp.dma_start(g.row_dram.rearrange("r (i p) -> (r i) p", p=P), rows[:, :]).then_inc(rows_saved, 16)
                sp.wait_ge(rows_saved, h * 16 + 32)
                sp.dma_start(q1[STACK:STACK + 3, b, :], g.row_dram).then_inc(loaded[b], 16)

            def save(h, b, s):
                sp.wait_ge(out_ready, h * NSB + (s + 2))
                sp.sem_inc(taken, 1)
                sp.dma_start(g.o_dram[bass.ds(h, 1), :, s * SBLK:(s + 1) * SBLK].rearrange("h f t -> f h t"),
                             out[:, s:s + 1, :]).then_inc(out_saved[s], 16)

            def body(pair, last):
                for b in range(2):
                    h = pair * 2 + b
                    final = last and b == 1
                    if not final:
                        sp.wait_ge(sc_done, h * UNITS + 1)
                        sp.sem_inc(taken, 1)
                        load_head(h + 1, 1 - b)
                        sp.wait_ge(mx_done, h * PIECES + 2 * PIECES)
                        if not last:
                            sp.sem_inc(taken, 1)
                            load_max(h + 2)
                    save(h, b, 0)
                    if not final:
                        load_rows(h + 1, 1 - b)
                    save(h, b, 1)

            sp.sem_inc(out_saved[0], 16)
            sp.sem_inc(out_saved[1], 16)
            sp.sem_inc(rows_saved, 16)
            load_max(0)
            load_head(0, 0)
            sp.wait_ge(mx_done, PIECES)
            load_max(1)
            load_rows(0, 0)
            with sp.Fori(0, PAIRS - 1) as pair:
                body(pair, False)
            body(PAIRS - 1, True)
            for b in range(2):
                sp.wait_ge(out_saved[b], 16 * (HEADS + 1))

        @block.gpsimd
        def _(pool):
            pool.memset(negp[:, :, :], 0.0).then_inc(ones_ready, 1)
            pool.wait_ge(ones_ready, 1)
            pool.memset(k1[STACK:STACK + 3, :, :], 1.0).then_inc(ones_ready, 1)

            def body(pair):
                for b in range(2):
                    for j, w in enumerate(pool_units):
                        n = pair * 2 + b
                        pool.wait_ge(exp_done, n * UNITS + (w + 3))
                        pool.wait_ge(pv_done, n * UNITS + (w + 1))
                        pool.tensor_tensor(low[:, w % NP, :], prob[:, w % NP, :], high[:, w % NP, :], ALU.subtract).then_inc(low_pool, 1)

            with pool.Fori(0, PAIRS) as pair:
                body(pair)

        @block.tensor
        def _(pe):
            def max_piece(h, i, t):
                n = h * PIECES + (i * TC + t)
                pe.wait_ge(mx_used, n + 1)
                nc.tensor.matmul(mx_ps[:, t % 2, :], qm[:, i * P:(i + 1) * P], km[:, t * NB:(t + 1) * NB],
                                 start=True, stop=True).then_inc(mx_done, 1)

            def max_rows(h):
                pe.wait_ge(neg_done, h + 1)
                nc.tensor.transpose(rows_ps, negp[:, :, :].rearrange("p r i -> p (r i)"), g.ident16[:, :]).then_inc(rows_done, 1)

            def scores(h, b, w):
                s, i = w // TT, w % TT
                pe.wait_ge(exp_done, h * UNITS + (w + 1))
                keys = slice(i * P, (i + 1) * P)
                for c in range(HB):
                    cols = slice(s * SBLK + c * NB, s * SBLK + (c + 1) * NB)
                    nc.tensor.matmul(sc_ps[:, i % 2, c, :], k1[:, b, keys], q1[:, b, cols], start=True, stop=False)
                    last = nc.tensor.matmul(sc_ps[:, i % 2, c, :], k2[:, b, keys], q2[:, b, cols], start=False, stop=True)
                last.then_inc(sc_done, 1)

            def values(h, w):
                s, i = w // TT, w % TT
                if w in pool_units:
                    pe.wait_ge(low_pool, h * len(pool_units) + (pool_units.index(w) + 1))
                else:
                    pe.wait_ge(low_vector, h * len(vector_units) + (vector_units.index(w) + 1))
                if i == 0:
                    pe.wait_ge(out_ready, h * NSB + (s + 1))
                parts = v[:, i, bass.ds(h, 1), :, :].rearrange("p o r d -> p (o r d)")
                for c in range(HB):
                    cols = slice(c * NB, (c + 1) * NB)
                    nc.tensor.matmul(o_ps[:, c, :], parts, high[:, w % NP, cols], start=(i == 0), stop=False)
                    last = nc.tensor.matmul(o_ps[:, c, :], parts, low[:, w % NP, cols], start=False, stop=(i == TT - 1))
                last.then_inc(pv_done, 1)

            def begin(h, b, pair_of_h):
                pe.wait_ge(loaded[b], pair_of_h * (LOADS + 16) + (LOADS + 16))
                pe.wait_ge(rows_ready, h + 1)

            def beside(h, w):
                if w == 0:
                    pe.wait_ge(m_loaded, h * 96 + 96)
                for n in pieces[w]:
                    max_piece(h, n // TC, n % TC)
                if w == ROWS:
                    max_rows(h)

            def body(pair, last):
                for b in range(2):
                    h = pair * 2 + b
                    end = last and b == 1
                    for w in range(LAG, UNITS + LAG):
                        if w < UNITS:
                            scores(h, b, w)
                            if not end:
                                beside(h + 1, w)
                        elif not end:
                            if w == UNITS:
                                begin(h + 1, 1 - b, pair + b)
                            scores(h + 1, 1 - b, w - UNITS)
                            if not (last and b == 0):
                                beside(h + 2, w - UNITS)
                        values(h, w - LAG)

            pe.sem_inc(pv_done, NP)
            pe.wait_ge(ones_ready, 2)
            pe.wait_ge(m_loaded, 96)
            for i in range(TT):
                for t in range(TC):
                    max_piece(0, i, t)
            max_rows(0)
            begin(0, 0, 0)
            for w in range(LAG):
                scores(0, 0, w)
                beside(1, w)
            with pe.Fori(0, PAIRS - 1) as pair:
                body(pair, False)
            body(PAIRS - 1, True)

        @block.scalar
        def _(act):
            act.sem_inc(exp_done, 2)
            act.sem_inc(out_ready, 1)

            def exponentials(h, w):
                act.wait_ge(sc_done, h * UNITS + (w + 1))
                act.wait_ge(pv_done, h * UNITS + (w + 1))
                nc.scalar.activation(prob[:, w % NP, :], sc_ps[:, w % 2, :, :].rearrange("p c n -> p (c n)"),
                                     ACT.Exp).then_inc(exp_done, 1)

            def output(h, s):
                act.wait_ge(pv_done, h * UNITS + ((s + 1) * TT + NP))
                act.wait_ge(out_saved[s], h * 16 + 16)
                nc.scalar.copy(out[:, s, :], o_ps[:, :, :].rearrange("p c n -> p (c n)")).then_inc(out_ready, 1)

            def body(pair, last):
                for b in range(2):
                    h = pair * 2 + b
                    end = last and b == 1
                    for w in range(LAG, UNITS + LAG):
                        if w < UNITS:
                            exponentials(h, w)
                        elif not end:
                            exponentials(h + 1, w - UNITS)
                        if w in (TT + LAG - 1, 2 * TT + LAG - 1):
                            output(h, w // TT - 1)

            for w in range(LAG):
                exponentials(0, w)
            with act.Fori(0, PAIRS - 1) as pair:
                body(pair, False)
            body(PAIRS - 1, True)

        @block.vector
        def _(dve):
            V = nc.vector
            dve.sem_inc(mx_used, 2)

            def peaks(h, n):
                dve.wait_ge(mx_done, h * PIECES + (n + 1))
                V.tensor_reduce(peak[:, n // TC, n % TC:n % TC + 1], mx_ps[:, n % 2, :], axis=AX.X, op=ALU.max).then_inc(mx_used, 1)

            def negate(h):
                dve.wait_ge(mx_used, h * PIECES + (PIECES + 2))
                V.tensor_reduce(neg[:, :], peak[:, :, :], axis=AX.X, op=ALU.max).then_inc(neg_step, 1)
                dve.wait_ge(neg_step, h * 5 + 1)
                V.tensor_scalar(neg[:, :], neg[:, :], -1.0, None, ALU.mult).then_inc(neg_step, 1)
                dve.wait_ge(neg_step, h * 5 + 2)
                V.tensor_copy(negp[:, 0, :], neg[:, :]).then_inc(neg_step, 1)
                dve.wait_ge(neg_step, h * 5 + 3)
                V.tensor_tensor(left[:, :], neg[:, :], negp[:, 0, :], ALU.subtract).then_inc(neg_step, 1)
                dve.wait_ge(neg_step, h * 5 + 4)
                V.tensor_copy(negp[:, 1, :], left[:, :]).then_inc(neg_step, 1)
                dve.wait_ge(neg_step, h * 5 + 5)
                V.tensor_tensor(negp[:, 2, :], left[:, :], negp[:, 1, :], ALU.subtract).then_inc(neg_done, 1)

            def rows_out(h):
                dve.wait_ge(rows_done, h + 1)
                dve.wait_ge(rows_saved, h * 16 + 16)
                V.tensor_copy(rows[:, :], rows_ps[0:3 * TT, :]).then_inc(rows_ready, 1)

            def lower(h, w):
                dve.wait_ge(exp_done, h * UNITS + (w + 3))
                dve.wait_ge(pv_done, h * UNITS + (w + 1))
                V.tensor_tensor(low[:, w % NP, :], prob[:, w % NP, :], high[:, w % NP, :], ALU.subtract).then_inc(low_vector, 1)

            def body(pair, last):
                for b in range(2):
                    h = pair * 2 + b
                    ahead = not (last and b == 1)
                    for w in range(UNITS):
                        if ahead:
                            for n in pieces[w]:
                                peaks(h + 1, n)
                            if w == NEGATE:
                                negate(h + 1)
                        if w in vector_units:
                            lower(h, w)
                        if ahead and w == ROWS:
                            rows_out(h + 1)

            dve.wait_ge(ones_ready, 1)
            for n in range(PIECES):
                peaks(0, n)
            negate(0)
            rows_out(0)
            with dve.Fori(0, PAIRS - 1) as pair:
                body(pair, False)
            body(PAIRS - 1, True)


def attention_outputs(nc, g, name, o, w):
    QH = P // DH
    SEG = T * HEADS // P
    with Layer(nc, name + "l") as L:
        sums = L.sb("sums", [P, SEG])
        inv = L.sb("inv", [P, DT, T])
        sums_loaded, inverted, inv_saved, inv_loaded, chain = (
            L.sem(s) for s in ("sums_loaded", "inverted", "inv_saved", "inv_loaded", "chain"))
        loaded = [L.sem(f"loaded{r}") for r in range(PARTS)]
        block = L.block()
        heads = g.o_dram.rearrange("(c q) f t -> q f c t", q=QH)

        @block.sync
        def _(sp):
            for h in range(HEADS):
                n = P // HEADS
                sp.dma_start(sums[h * n:(h + 1) * n, :], g.o_dram[h, PARTS * DH, :].rearrange("(a b) -> a b", a=n)).then_inc(sums_loaded, 16)
            for r in range(PARTS):
                for q in range(QH):
                    sp.dma_start(o[q * DH:(q + 1) * DH, r, :, :], heads[q, r * DH:(r + 1) * DH, :, :]).then_inc(loaded[r], 16)
            for r in range(PARTS):
                sp.wait_ge(loaded[r], 16 * QH)

        @block.scalar
        def _(act):
            act.wait_ge(inverted, 1)
            act.dma_start(g.inv_dram.rearrange("h (a b) -> (h a) b", b=SEG), sums[:, :]).then_inc(inv_saved, 16)
            act.wait_ge(inv_saved, 16)
            for q in range(QH):
                act.dma_start(inv[q * DH:(q + 1) * DH, :, :],
                              g.inv_dram.rearrange("(c q) t -> q c t", q=QH)[q].partition_broadcast(DH)).then_inc(inv_loaded, 16)
            act.wait_ge(inv_loaded, 16 * QH)

        @block.vector
        def _(dve):
            link = Chain(dve, chain)
            dve.wait_ge(sums_loaded, 16 * HEADS)
            nc.vector.reciprocal(sums[:, :], sums[:, :]).then_inc(inverted, 1)
            for r in range(2):
                dve.wait_ge(loaded[r], 16 * QH)
            link(nc.vector.tensor_tensor(o[:, 0, :, :], o[:, 0, :, :], o[:, 1, :, :], ALU.add))
            dve.wait_ge(loaded[2], 16 * QH)
            link(nc.vector.tensor_tensor(o[:, 0, :, :], o[:, 0, :, :], o[:, 2, :, :], ALU.add))
            dve.wait_ge(inv_loaded, 16 * QH)
            link(nc.vector.tensor_tensor(o[:, 0, :, :], o[:, 0, :, :], inv[:, :, :], ALU.mult))
    project_and_add(nc, g, name, o[:, 0, :, :], w, g.dram["L1_attn_a_bo"])


E_N = 64
TOP = 8
CAP = 256
IN = 192
HALF = IN // 2
GE = 8
GROUPS = E_N // GE
SA = P // GE
SB = CAP // SA
NOWHERE = 4096.0
DROPPED = 65536.0


def moe(nc, g, name):
    with ExitStack() as ctx:
        slot_token = ctx.enter_context(nc.sbuf_tensor(f"{name}_slot_token", [P, GROUPS, SB], U32))
        rows = ctx.enter_context(nc.sbuf_tensor(f"{name}_rows", [P, TT, TOP], U32))
        weights = ctx.enter_context(nc.sbuf_tensor(f"{name}_weights", [P, TT, TOP], F32))
        with nc.sbuf_tensor(f"{name}_logits", [P, TT, E_N], F32) as logits:
            moe_logits(nc, g, name + "a", logits)
            moe_routing(nc, g, name + "b", logits, slot_token, rows, weights)
        moe_experts(nc, g, name + "c", slot_token)
        moe_combine(nc, g, name + "d", rows, weights)


def moe_logits(nc, g, name, logits):
    with Layer(nc, name) as L:
        norm = Norm(L, nc, g.X)
        z = L.sb("z", [P, 2, D])
        zt = L.sb("zt", [P, 2, D])
        rw = L.sb("rw", [E_N, D])
        rwt = L.sb("rwt", [P, DT, E_N])
        zt_ps = L.ps("zt_ps", [P, 2, D])
        rwt_ps = L.ps("rwt_ps", [P, DT, E_N])
        lg_ps = L.ps("lg_ps", [P, 2, NB])
        z_ready, zt_done, zt_ready, lg_ready, lg_used, rw_loaded, rwt_done, rwt_ready = (
            L.sem(s) for s in ("z_ready", "zt_done", "zt_ready", "lg_ready", "lg_used", "rw_loaded", "rwt_done", "rwt_ready"))
        z_saved = [L.sem(f"z_saved{b}") for b in range(2)]
        block = L.block()
        z_rows = g.z_dram.rearrange("(i p) d -> p i d", p=P)

        @block.sync
        def _(sp):
            sp.dma_start(rw[:, :], g.dram["L1_ffn_router_weight"]).then_inc(rw_loaded, 16)
            with sp.Fori(0, TT // 2) as pair:
                for b in range(2):
                    sp.wait_ge(z_ready, pair * 2 + b + 1)
                    sp.dma_start(z_rows[:, bass.ds(pair * 2 + b, 1), :], z[:, b:b + 1, :]).then_inc(z_saved[b], 16)
            for b in range(2):
                sp.wait_ge(z_saved[b], 16 * (TT // 2))

        @block.vector
        def _(dve):
            norm.on_vector(dve)
            for b in range(2):
                nc.vector.tensor_scalar(z[:, b, :], g.X[:, b, :], norm.mv[:, b, 0:1], norm.rstd[:, b:b + 1],
                                        ALU.subtract, ALU.mult).then_inc(z_ready, 1)
            with dve.Fori(0, TT // 2 - 1) as pair:
                for b in range(2):
                    i = pair * 2 + b
                    dve.wait_ge(lg_ready, i + 1)
                    nc.vector.tensor_copy(logits[:, bass.ds(i, 1), :], lg_ps[:, b:b + 1, 0:E_N]).then_inc(lg_used, 1)
                    dve.wait_ge(z_saved[b], pair * 16 + 16)
                    nc.vector.tensor_scalar(z[:, b:b + 1, :], g.X[:, bass.ds(i + 2, 1), :], norm.mv[:, bass.ds(i + 2, 1), 0:1],
                                            norm.rstd[:, bass.ds(i + 2, 1)], ALU.subtract, ALU.mult).then_inc(z_ready, 1)
            for b in range(2):
                dve.wait_ge(lg_ready, TT - 1 + b)
                nc.vector.tensor_copy(logits[:, TT - 2 + b, :], lg_ps[:, b, 0:E_N]).then_inc(lg_used, 1)

        @block.tensor
        def _(pe):
            pe.wait_ge(rw_loaded, 16)
            for k in range(DT):
                last = nc.tensor.transpose(rwt_ps[:, k, :], rw[:, k * P:(k + 1) * P], g.ident[0:E_N, 0:E_N])
            last.then_inc(rwt_done, 1)
            pe.wait_ge(rwt_ready, 1)

            def transposes(b):
                for k in range(DT):
                    last = nc.tensor.transpose(zt_ps[:, b, k * P:(k + 1) * P], z[:, b, k * P:(k + 1) * P], g.ident[:, :])
                last.then_inc(zt_done, 1)

            with pe.Fori(0, TT // 2) as pair:
                for b in range(2):
                    pe.wait_ge(z_ready, pair * 2 + b + 1)
                    transposes(b)
                for b in range(2):
                    pe.wait_ge(zt_ready, pair * 2 + b + 1)
                    for k in range(DT):
                        last = nc.tensor.matmul(lg_ps[:, b, 0:E_N], zt[:, b, k * P:(k + 1) * P], rwt[:, k, :],
                                                start=(k == 0), stop=(k == DT - 1))
                    last.then_inc(lg_ready, 1)

        @block.scalar
        def _(act):
            norm.on_scalar(act)
            act.wait_ge(rwt_done, 1)
            nc.scalar.copy(rwt[:, :, :], rwt_ps[:, :, :]).then_inc(rwt_ready, 1)
            with act.Fori(0, TT // 2) as pair:
                for b in range(2):
                    act.wait_ge(zt_done, pair * 2 + b + 1)
                    nc.scalar.copy(zt[:, b, :], zt_ps[:, b, :]).then_inc(zt_ready, 1)


def moe_routing(nc, g, name, logits, slot_token, rows, weights):
    with Layer(nc, name) as L:
        best = L.sb("best", [P, TT, TOP])
        choice = L.sb("choice", [P, TT, TOP], U32)
        choice_f = L.sb("choice_f", [P, TT, TOP])
        others = L.sb("others", [P, TT, E_N])
        shifted = L.sb("shifted", [P, TT, E_N])
        total = L.sb("total", [P, TT])
        taken = L.sb("taken", [P, TT, E_N])
        taken16 = L.sb("taken16", [P, TT, E_N], BF16)
        before16 = L.sb("before16", [P, TT, E_N], BF16)
        pos = L.sb("pos", [P, TT, E_N])
        pos_i = L.sb("pos_i", [P, TT, E_N], I32)
        pos_a = L.sb("pos_a", [P, TT, E_N], I32)
        pos_af = L.sb("pos_af", [P, TT, E_N])
        pos_bf = L.sb("pos_bf", [P, TT, E_N])
        tri = L.sb("tri", [P, P])
        tri16, ones16 = L.sb("tri16", [P, P], BF16), L.sb("ones16", [P, P], BF16)
        iota_i = L.sb("iota_i", [P, E_N], I32)
        iota = L.sb("iota", [P, E_N])
        base = L.sb("base", [P, E_N])
        part_i, part = L.sb("part_i", [P, 1], I32), L.sb("part", [P, 1])
        own = L.sb("own", [P, GE])
        hot = L.sb("hot", [P, TT // 2, TOP, E_N])
        eq_a = L.sb("eq_a", [P, TT, E_N, SA], BF16)
        by_part = L.sb("by_part", [P, TT, E_N, SB], BF16)
        by_tile = L.sb("by_tile", [P, TT, E_N, SB], BF16)
        diag = L.sb("diag", [P, 2, GE, SB])
        slot_f = L.sb("slot_f", [P, GROUPS, SB])
        pos_ps = L.ps("pos_ps", [P, TT, E_N])
        slot_ps = L.ps("slot_ps", [P, 2, 4, P])
        consts, chain, less_max, exps, counted, pos_done, onehots, slots_done, slots_used = (
            L.sem(s) for s in ("consts", "chain", "less_max", "exps", "counted", "pos_done", "onehots", "slots_done", "slots_used"))
        N_CONSTS = 12
        block = L.block()

        @block.gpsimd
        def _(pool):
            link = Chain(pool, consts)
            link(pool.memset(tri[:, :], 1.0))
            link(pool.memset(ones16[:, :], 1.0))
            link(pool.affine_select(out=tri[:, :], in_=tri[:, :], compare_op=ALU.is_ge, fill=0.0, base=-1,
                                    pattern=[[1, P]], channel_multiplier=-1))
            link(pool.tensor_copy(tri16[:, :], tri[:, :]))
            link(pool.iota(iota_i[:, :], [[1, E_N]], base=0, channel_multiplier=0))
            link(pool.tensor_copy(iota[:, :], iota_i[:, :]))
            link(pool.tensor_scalar(base[:, :], iota[:, :], float(CAP), None, ALU.mult))
            link(pool.iota(part_i[:, :], [[0, 1]], base=0, channel_multiplier=1))
            link(pool.tensor_copy(part[:, :], part_i[:, :]))
            link(pool.memset(own[:, :], 1.0))
            link(pool.affine_select(out=own[:, :], in_=own[:, :], compare_op=ALU.is_ge, fill=0.0, base=0,
                                    pattern=[[-SA, GE]], channel_multiplier=1))
            link(pool.affine_select(out=own[:, :], in_=own[:, :], compare_op=ALU.is_ge, fill=0.0, base=SA - 1,
                                    pattern=[[SA, GE]], channel_multiplier=-1))
            assert link.n == N_CONSTS

        @block.vector
        def _(dve):
            link = Chain(dve, chain)
            for i in range(TT):
                link(nc.vector.max(best[:, i, :], logits[:, i, :]))
            for i in range(TT):
                nc.vector.max_index(choice[:, i, :], best[:, i, :], logits[:, i, :])
            for i in range(TT):
                link(nc.vector.match_replace(others[:, i, :], best[:, i, :], logits[:, i, :], -3.0e38))
            link(nc.vector.tensor_tensor(taken[:, :, :], others[:, :, :], logits[:, :, :], ALU.not_equal))
            link(nc.vector.tensor_copy(taken16[:, :, :], taken[:, :, :]))
            link(nc.vector.memset(before16[:, 0, :], 0.0))
            for i in range(1, TT):
                link(nc.vector.tensor_tensor(before16[:, i, :], before16[:, i - 1, :], taken16[:, i - 1, :], ALU.add))
            nc.vector.tensor_copy(choice_f[:, :, :], choice[:, :, :]).then_inc(counted, 1)
            link(nc.vector.tensor_tensor(shifted[:, :, :], logits[:, :, :], best[:, :, 0:1].to_broadcast([P, TT, E_N]), ALU.subtract))
            nc.vector.tensor_tensor(weights[:, :, :], best[:, :, :], best[:, :, 0:1].to_broadcast([P, TT, TOP]),
                                    ALU.subtract).then_inc(less_max, 1)
            dve.wait_ge(exps, 2)
            link(nc.vector.tensor_reduce(total[:, :], shifted[:, :, :], axis=AX.X, op=ALU.add))
            link(nc.vector.reciprocal(total[:, :], total[:, :]))
            link(nc.vector.tensor_tensor(weights[:, :, :], weights[:, :, :],
                                         total[:, :].rearrange("p (i o) -> p i o", o=1).to_broadcast([P, TT, TOP]), ALU.mult))
            link(nc.vector.tensor_reduce(total[:, :], weights[:, :, :], axis=AX.X, op=ALU.add))
            link(nc.vector.reciprocal(total[:, :], total[:, :]))
            link(nc.vector.tensor_tensor(weights[:, :, :], weights[:, :, :],
                                         total[:, :].rearrange("p (i o) -> p i o", o=1).to_broadcast([P, TT, TOP]), ALU.mult))

            dve.wait_ge(consts, N_CONSTS)
            dve.wait_ge(pos_done, 1)
            link(nc.vector.tensor_copy(pos[:, :, :], pos_ps[:, :, :]))
            link(nc.vector.tensor_scalar(shifted[:, :, :], taken[:, :, :], -NOWHERE, NOWHERE, ALU.mult, ALU.add))
            link(nc.vector.tensor_tensor(shifted[:, :, :], pos[:, :, :], shifted[:, :, :], ALU.add))
            link(nc.vector.tensor_copy(pos_i[:, :, :], shifted[:, :, :]))
            link(nc.vector.tensor_scalar(pos_a[:, :, :], pos_i[:, :, :], SA - 1, None, ALU.bitwise_and))
            link(nc.vector.tensor_copy(pos_af[:, :, :], pos_a[:, :, :]))
            link(nc.vector.tensor_scalar(pos_i[:, :, :], pos_i[:, :, :], int(math.log2(SA)), None, ALU.logical_shift_right))
            link(nc.vector.tensor_copy(pos_bf[:, :, :], pos_i[:, :, :]))

            def digit(x, i, n):
                return x[:, i, :].rearrange("p (e o) -> p e o", o=1).to_broadcast([P, E_N, n])

            def count(n):
                return iota[:, 0:n].rearrange("p (o n) -> p o n", o=1).to_broadcast([P, E_N, n])

            for i in range(TT):
                nc.vector.tensor_tensor(eq_a[:, i, :, :], digit(pos_af, i, SA), count(SA), ALU.is_equal)
                link(nc.vector.tensor_tensor(by_tile[:, i, :, :], digit(pos_bf, i, SB), count(SB), ALU.is_equal))
                link(nc.vector.tensor_scalar(by_part[:, i, :, :], by_tile[:, i, :, :], part[:, 0:1], None, ALU.mult))
                last = nc.vector.tensor_scalar(by_tile[:, i, :, :], by_tile[:, i, :, :], float(i * P), None, ALU.mult)
            last.then_inc(onehots, 1)

            link(nc.vector.tensor_scalar(shifted[:, :, :], pos[:, :, :], float(CAP), DROPPED, ALU.is_ge, ALU.mult))
            link(nc.vector.tensor_scalar(pos[:, :, :], pos[:, :, :], float(CAP - 1), None, ALU.min))
            link(nc.vector.tensor_tensor(pos[:, :, :], pos[:, :, :], shifted[:, :, :], ALU.add))
            link(nc.vector.tensor_tensor(pos[:, :, :], pos[:, :, :],
                                         base[:, :].rearrange("p (o e) -> p o e", o=1).to_broadcast([P, TT, E_N]), ALU.add))
            for h in range(2):
                ts = slice(h * TT // 2, (h + 1) * TT // 2)
                for i in range(TT // 2):
                    t = h * TT // 2 + i
                    link(nc.vector.tensor_tensor(
                        hot[:, i, :, :], choice_f[:, t, :].rearrange("p (k o) -> p k o", o=1).to_broadcast([P, TOP, E_N]),
                        iota[:, :].rearrange("p (o e) -> p o e", o=1).to_broadcast([P, TOP, E_N]), ALU.is_equal))
                    link(nc.vector.tensor_tensor(
                        hot[:, i, :, :], hot[:, i, :, :],
                        pos[:, t, :].rearrange("p (o e) -> p o e", o=1).to_broadcast([P, TOP, E_N]), ALU.mult))
                link(nc.vector.tensor_reduce(best[:, ts, :], hot[:, :, :, :], axis=AX.X, op=ALU.add))
            link(nc.vector.tensor_scalar(choice_f[:, :, :], best[:, :, :], DROPPED, None, ALU.is_lt))
            link(nc.vector.tensor_tensor(weights[:, :, :], weights[:, :, :], choice_f[:, :, :], ALU.mult))
            link(nc.vector.tensor_scalar(choice_f[:, :, :], choice_f[:, :, :], DROPPED, -DROPPED, ALU.mult, ALU.add))
            link(nc.vector.tensor_tensor(best[:, :, :], best[:, :, :], choice_f[:, :, :], ALU.add))
            link(nc.vector.tensor_copy(rows[:, :, :], best[:, :, :]))

            for q in range(GROUPS):
                dve.wait_ge(slots_done, q + 1)
                link(nc.vector.tensor_tensor(diag[:, q % 2, :, :], slot_ps[:, q % 2, 0, :].rearrange("p (e b) -> p e b", e=GE),
                                             own[:, :].rearrange("p (e o) -> p e o", o=1).to_broadcast([P, GE, SB]), ALU.mult))
                dve.sem_inc(slots_used, 1)
                link(nc.vector.tensor_reduce(slot_f[:, q, :], diag[:, q % 2, :, :].rearrange("p e b -> p b e"), axis=AX.X, op=ALU.add))
            link(nc.vector.tensor_copy(slot_token[:, :, :], slot_f[:, :, :]))

        @block.scalar
        def _(act):
            act.wait_ge(less_max, 1)
            nc.scalar.activation(shifted[:, :, :], shifted[:, :, :], ACT.Exp).then_inc(exps, 1)
            nc.scalar.activation(weights[:, :, :], weights[:, :, :], ACT.Exp).then_inc(exps, 1)

        @block.tensor
        def _(pe):
            pe.wait_ge(consts, N_CONSTS)
            pe.wait_ge(counted, 1)
            for h in range(2):
                ts = slice(h * TT // 2, (h + 1) * TT // 2)
                nc.tensor.matmul(pos_ps[:, ts, :], tri16[:, :], taken16[:, ts, :], start=True, stop=False)
                last = nc.tensor.matmul(pos_ps[:, ts, :], ones16[:, :], before16[:, ts, :], start=False, stop=True)
            last.then_inc(pos_done, 1)
            pe.wait_ge(onehots, 1)
            for q in range(GROUPS):
                es = slice(q * GE, (q + 1) * GE)
                if q >= 2:
                    pe.wait_ge(slots_used, q - 1)
                for i in range(TT):
                    for rhs in (by_part, by_tile):
                        last = nc.tensor.matmul(slot_ps[:, q % 2, 0, :], eq_a[:, i, es, :], rhs[:, i, es, :],
                                                start=(i == 0 and rhs is by_part), stop=(i == TT - 1 and rhs is by_tile))
                last.then_inc(slots_done, 1)


def moe_experts(nc, g, name, slot_token):
    with Layer(nc, name) as L:
        NW = 4
        UNITS = 2 * GE
        NY = 4
        token = L.sb("token", [P, 2, SB], U32)
        xg = L.sb("xg", [P, SB, D])
        xt = L.sb("xt", [P, 2, DT, GE, SB, SA])
        wgu = L.sb("wgu", [P, NW, DT, 2 * IN])
        wd = L.sb("wd", [HALF, NW, 2, D])
        sg = L.sb("sg", [P, 2, IN])
        h = L.sb("h", [P, 2, IN])
        ht = L.sb("ht", [HALF, 2, 2, P])
        ye = L.sb("ye", [P, NY, D])
        xt_ps = L.ps("xt_ps", [P, 2, 4, P])
        gu_ps = L.ps("gu_ps", [P, 2, NB])
        ht_ps = L.ps("ht_ps", [P, 2, 4, P])
        ye_ps = L.ps("ye_ps", [P, 2, D])
        token_ready, xt_done, xt_ready, gu_done, sg_ready, h_ready, ht_done, ht_ready, ye_done, ye_ready = (
            L.sem(s) for s in ("token_ready", "xt_done", "xt_ready", "gu_done", "sg_ready", "h_ready", "ht_done", "ht_ready",
                               "ye_done", "ye_ready"))
        passed = L.sem("passed")
        gathered = [L.sem(f"gathered{j}") for j in range(4)]
        w_loaded = [L.sem(f"w_loaded{j}") for j in range(NW)]
        saved = [L.sem(f"saved{j}") for j in range(NY)]
        block = L.block()
        wgu_dram = g.dram["L1_ffn_gate_up_proj"].rearrange("e (k p) f -> p e k f", p=P)
        wd_dram = g.dram["L1_ffn_down_proj"].rearrange("e (j p) d -> p e j d", p=HALF)
        y_rows = g.y_dram.rearrange("(u p) d -> p u d", p=P)

        def over_groups(eng, body):
            body(0, 0, True, False)
            with eng.Fori(0, GROUPS // 2 - 1) as r:
                body(r * 2 + 1, 1, False, False)
                body(r * 2 + 2, 0, False, False)
            body(GROUPS - 1, 1, False, True)

        @block.sync
        def _(sp):
            def load(e, slot):
                sp.dma_start(wgu[:, slot, :, :], wgu_dram[:, e, :, :]).then_inc(w_loaded[slot], 16)
                sp.dma_start(wd[:, slot, :, :], wd_dram[:, e, :, :]).then_inc(w_loaded[slot], 16)

            def save(e, slot):
                for s in range(2):
                    sp.wait_ge(ye_ready, e * 2 + s + 1)
                    y = (2 * slot + s) % NY
                    sp.dma_start(y_rows[:, bass.ds(e * 2 + s, 1), :], ye[:, y:y + 1, :]).then_inc(saved[y], 16)

            for e in range(NW):
                load(e, e)
            with sp.Fori(0, E_N // NW - 1) as r:
                for s in range(NW):
                    e = r * NW + s
                    save(e, s)
                    sp.dma_start(wgu[:, s:s + 1, :, :], wgu_dram[:, bass.ds(e + NW, 1), :, :]).then_inc(w_loaded[s], 16)
                    sp.dma_start(wd[:, s:s + 1, :, :], wd_dram[:, bass.ds(e + NW, 1), :, :]).then_inc(w_loaded[s], 16)
            for s in range(NW):
                save(E_N - NW + s, s)
            for y in range(NY):
                sp.wait_ge(saved[y], 16 * (2 * E_N // NY))

        @block.gpsimd
        def _(pool):
            def gather(n, b, free):
                pool.tensor_copy(token[:, b:b + 1, :], slot_token[:, bass.ds(n, 1), :]).then_inc(token_ready, 1)
                pool.wait_ge(token_ready, n + 1)
                pool.sem_inc(passed, 1)
                for s in range(SB):
                    if s % 4 == 0 and free is not None:
                        pool.wait_ge(xt_done, free + s + 4)
                        pool.sem_inc(passed, 1)
                    pool.indirect_dma_start(out=xg[:, s, :], out_offset=None, in_=g.z_dram,
                                            in_offset=bass.IndirectOffsetOnAxis(ap=token[:, b, s:s + 1], axis=0)
                                            ).then_inc(gathered[s // 4], 16)

            def body(q, b, first, last):
                if not last:
                    if not first:
                        for j in range(4):
                            pool.wait_ge(gathered[j], q * 64)
                        pool.sem_inc(passed, 1)
                    gather(q + 1, 1 - b, q * UNITS)

            gather(0, 0, None)
            over_groups(pool, body)

        @block.tensor
        def _(pe):
            def transposes(n, b, u, first):
                j, k = u // 4, u % 4
                if k == 0:
                    pe.wait_ge(gathered[j], n * 64 + 64)
                if not (first and u < 2):
                    pe.wait_ge(xt_ready, n * UNITS + u - 1)
                for s in range(4):
                    last = nc.tensor.transpose(xt_ps[:, u % 2, s, :], xg[:, 4 * j + s, k * P:(k + 1) * P], g.ident[:, :])
                last.then_inc(xt_done, 1)

            def inner(q, b, u, first):
                n = q * UNITS + u
                e, s = u // 2, u % 2
                if s == 0:
                    pe.wait_ge(w_loaded[e % NW], q * (GE // NW * 32) + (e // NW * 32 + 32))
                if u == 0:
                    pe.wait_ge(xt_ready, q * UNITS + UNITS)
                if not (first and u < 2):
                    pe.wait_ge(h_ready, n - 1)
                for k in range(DT):
                    last = nc.tensor.matmul(gu_ps[:, u % 2, 0:2 * IN], xt[:, b, k, e, s * SB // 2:(s + 1) * SB // 2, :],
                                            wgu[:, e % NW, k, :], start=(k == 0), stop=(k == DT - 1))
                last.then_inc(gu_done, 1)

            def hidden(n, u, first):
                pe.wait_ge(h_ready, n + 1)
                if not (first and u < 2):
                    pe.wait_ge(ht_ready, n - 1)
                for j in range(2):
                    last = nc.tensor.transpose(ht_ps[0:HALF, u % 2, j, :], h[:, u % 2, j * HALF:(j + 1) * HALF], g.ident[:, :])
                last.then_inc(ht_done, 1)

            def outer(n, u, first):
                pe.wait_ge(ht_ready, n + 1)
                if not (first and u < 2):
                    pe.wait_ge(ye_ready, n - 1)
                for j in range(2):
                    last = nc.tensor.matmul(ye_ps[:, u % 2, :], ht[:, u % 2, j, :], wd[:, (u // 2) % NW, j, :],
                                            start=(j == 0), stop=(j == 1))
                last.then_inc(ye_done, 1)

            def body(q, b, first, last):
                for u in range(UNITS):
                    n = q * UNITS + u
                    inner(q, b, u, first)
                    if not (first and u < 1):
                        hidden(n - 1, (u - 1) % UNITS, first)
                    if not (first and u < 2):
                        outer(n - 2, (u - 2) % UNITS, first)
                    if not last:
                        transposes(q + 1, 1 - b, u, False)

            for u in range(UNITS):
                transposes(0, 0, u, True)
            over_groups(pe, body)
            n = GROUPS * UNITS
            hidden(n - 1, UNITS - 1, False)
            outer(n - 2, UNITS - 2, False)
            outer(n - 1, UNITS - 1, False)

        @block.scalar
        def _(act):
            def evacuate(n, b, u):
                j, k = u // 4, u % 4
                act.wait_ge(xt_done, n * UNITS + u + 1)
                nc.scalar.copy(xt[:, b, k, :, 4 * j:4 * j + 4, :],
                               xt_ps[:, u % 2, :, :].rearrange("p s (e a) -> p e s a", e=GE)).then_inc(xt_ready, 1)

            def body(q, b, first, last):
                for u in range(UNITS):
                    n = q * UNITS + u
                    act.wait_ge(gu_done, n + 1)
                    if not (first and u < 2):
                        act.wait_ge(h_ready, n - 1)
                    nc.scalar.activation(sg[:, u % 2, :], gu_ps[:, u % 2, 0:IN], ACT.Silu).then_inc(sg_ready, 1)
                    if not last:
                        evacuate(q + 1, 1 - b, u)

            for u in range(UNITS):
                evacuate(0, 0, u)
            over_groups(act, body)

        @block.vector
        def _(dve):
            def gate(n, u, first):
                dve.wait_ge(sg_ready, n + 1)
                if not (first and u < 2):
                    dve.wait_ge(ht_done, n - 1)
                nc.vector.tensor_tensor(h[:, u % 2, :], sg[:, u % 2, :], gu_ps[:, u % 2, IN:2 * IN], ALU.mult).then_inc(h_ready, 1)

            def hidden_out(n, u, first):
                dve.wait_ge(ht_done, n + 1)
                if not (first and u < 2):
                    dve.wait_ge(ye_done, n - 1)
                nc.vector.tensor_copy(ht[:, u % 2, :, :], ht_ps[0:HALF, u % 2, 0:2, :]).then_inc(ht_ready, 1)

            def output_out(n, q, u, first):
                dve.wait_ge(ye_done, n + 1)
                if not (first and u < NY):
                    dve.wait_ge(saved[u % NY], q * (UNITS // NY * 16) + (u // NY * 16))
                nc.vector.tensor_copy(ye[:, u % NY, :], ye_ps[:, u % 2, :]).then_inc(ye_ready, 1)

            def body(q, b, first, last):
                for u in range(UNITS):
                    n = q * UNITS + u
                    gate(n, u, first)
                    if not (first and u < 1):
                        hidden_out(n - 1, (u - 1) % UNITS, first and u <= 2)
                    if not (first and u < 2):
                        output_out(n - 2, q - (u < 2), (u - 2) % UNITS, first)

            over_groups(dve, body)
            n = GROUPS * UNITS
            hidden_out(n - 1, UNITS - 1, False)
            output_out(n - 2, GROUPS - 1, UNITS - 2, False)
            output_out(n - 1, GROUPS - 1, UNITS - 1, False)


def moe_combine(nc, g, name, rows, weights):
    with Layer(nc, name) as L:
        row = L.sb("row", [P, 2, TOP], U32)
        yg = L.sb("yg", [P, 2, TOP, D])
        row_ready, summed = L.sem("row_ready"), L.sem("summed")
        passed = L.sem("passed")
        gathered = [L.sem(f"gathered{b}") for b in range(2)]
        block = L.block()

        @block.gpsimd
        def _(pool):
            def gather(i, b, first):
                if not first:
                    pool.wait_ge(summed, i * TOP - TOP)
                    pool.sem_inc(passed, 1)
                pool.tensor_copy(row[:, b:b + 1, :], rows[:, bass.ds(i, 1), :]).then_inc(row_ready, 1)
                pool.wait_ge(row_ready, i + 1)
                pool.sem_inc(passed, 1)
                for k in range(TOP):
                    pool.indirect_dma_start(out=yg[:, b, k, :], out_offset=None, in_=g.y_dram,
                                            in_offset=bass.IndirectOffsetOnAxis(ap=row[:, b, k:k + 1], axis=0)
                                            ).then_inc(gathered[b], 16)

            for b in range(2):
                gather(b, b, True)
            with pool.Fori(0, TT // 2 - 1) as pair:
                for b in range(2):
                    gather(pair * 2 + (2 + b), b, False)

        @block.vector
        def _(dve):
            with dve.Fori(0, TT // 2) as pair:
                for b in range(2):
                    i = pair * 2 + b
                    dve.wait_ge(gathered[b], pair * (16 * TOP) + 16 * TOP)
                    for k in range(TOP):
                        nc.vector.scalar_tensor_tensor(
                            out=g.X[:, bass.ds(i, 1), :], in0=yg[:, b, k:k + 1, :], scalar=weights[:, bass.ds(i, 1), k],
                            in1=g.X[:, bass.ds(i, 1), :], op0=ALU.mult, op1=ALU.add).then_inc(summed, 1)
                        dve.wait_ge(summed, i * TOP + (k + 1))


LH = 32
LD = 64
LF = LH * LD
CH = P
NCH = T // CH
PAIRS_L = LH // 2
KINDS = 4
RMS_EPS = 1e-5
FAR = 1.0e9


def head_slopes():
    base = 1.0 / 2.0 ** (8.0 / LH)
    return [base ** (h + 1.0) * (1.0 + 1e-5) for h in range(LH)]


def linear_attention(nc, g):
    with nc.sbuf_tensor("lin_squares", [P, T], F32) as squares:
        with nc.sbuf_tensor("lin_z", [P, DT, T], F32) as z:
            normalized_features(nc, g, "lina", z)
            linear_heads(nc, g, "linb", z, squares)
        linear_outputs(nc, g, "linc", squares)


def linear_heads(nc, g, name, z, squares):
    with Layer(nc, name) as L:
        TQ = NB // CH
        USES = KINDS * (TC + 1)
        wr = L.sb("wr", [P, KINDS, D])
        wt = L.sb("wt", [P, KINDS, DT, P])
        proj = [L.sb(f"proj{b}", [P, KINDS, T]) for b in range(2)]
        qd = L.sb("qd", [P, T])
        dd = L.sb("dd", [P, 2, 2, CH])
        qdec = L.sb("qdec", [P, 2, CH])
        slope_all = L.sb("slope_all", [P, LH])
        slope_own = L.sb("slope_own", [P, PAIRS_L])
        kdec = L.sb("kdec", [P, LH])
        sdec = L.sb("sdec", [P, PAIRS_L])
        norm_w = L.sb("norm_w", [P, PAIRS_L])
        dist_i, dist = L.sb("dist_i", [P, CH], I32), L.sb("dist", [P, CH])
        since_i, since = L.sb("since_i", [P, CH], I32), L.sb("since", [P, CH])
        until_i, until = L.sb("until_i", [P, LH], I32), L.sb("until", [P, LH])
        aw = L.sb("aw", [P, 2, CH])
        kt = L.sb("kt", [P, 2, LD])
        vt = L.sb("vt", [P, P])
        state = L.sb("state", [P, 2, P])
        osb = L.sb("osb", [P, 2, NB])
        sq = L.sb("sq", [P, NB])
        gated = L.sb("gated", [P, 2, NB])
        pr_ps = L.ps("pr_ps", [P, 2, NB])
        s_ps = L.ps("s_ps", [P, 2, 4, CH])
        tr_ps = L.ps("tr_ps", [P, 4, P])
        kv_ps = L.ps("kv_ps", [P, 4, P])
        o_ps = L.ps("o_ps", [P, 2, NB])
        names = ("w_taken", "pr_done", "pr_out", "consts", "tables0", "tables", "qd_done", "s_done", "aw_done", "tr_done",
                 "vt_done", "kv_done", "state_done", "o_done", "o_out", "gated_done", "sq_step", "sq_done",
                 "norm_loaded", "osb_used", "state_step", "act_passed")
        S = {n: L.sem(n) for n in names}
        (w_taken, pr_done, pr_out, consts, tables0, tables, qd_done, s_done, aw_done, tr_done, vt_done, kv_done,
         state_done, o_done, o_out, gated_done, sq_step, sq_done, norm_loaded, osb_used, state_step, act_passed) = (S[n] for n in names)
        w_loaded = [L.sem(f"w_loaded{k}") for k in range(KINDS)]
        saved = [L.sem(f"saved{b}") for b in range(2)]
        block = L.block()
        qkv_rows = g.dram["L1_attn_b_qkv_w"].rearrange("(h c r) i -> h c r i", c=3, r=LD)
        gate_rows = g.dram["L1_attn_b_gate_w"].rearrange("(n p) i -> n p i", p=P)
        out_rows = g.g_dram.rearrange("(n p) t -> p n t", p=P)
        N_CONSTS = 9 + 2 * LH

        def over_pairs(eng, body):
            with eng.Fori(0, PAIRS_L // 2 - 1) as r:
                body(r * 2, 0, False)
                body(r * 2 + 1, 1, False)
            body(PAIRS_L - 2, 0, False)
            body(PAIRS_L - 1, 1, True)

        @block.sync
        def _(sp):
            def load(kind, n):
                if kind < 3:
                    for hh in range(2):
                        sp.dma_start(wr[hh * LD:(hh + 1) * LD, kind:kind + 1, :],
                                     qkv_rows[bass.ds(n * 2 + hh, 1), kind, :, :].rearrange("h r i -> r h i")).then_inc(w_loaded[kind], 16)
                else:
                    sp.dma_start(wr[:, kind:kind + 1, :], gate_rows[bass.ds(n, 1), :, :].rearrange("n p i -> p n i")).then_inc(w_loaded[kind], 32)

            def save(n, b, q):
                sp.wait_ge(gated_done, n * TC + (q + 1))
                sp.sem_inc(w_taken, 1)
                sp.dma_start(out_rows[:, bass.ds(n, 1), q * NB:(q + 1) * NB],
                             gated[:, q % 2:q % 2 + 1, :]).then_inc(saved[q % 2], 16)

            def reload(kind, n):
                if kind == 0:
                    sp.wait_ge(pr_done, (n - 1) * USES + 1)
                else:
                    sp.wait_ge(pr_done, (n - 1) * USES + (5 * (kind - 1) + 6))
                sp.sem_inc(w_taken, 1)
                load(kind, n)

            sp.dma_start(norm_w[:, :], g.dram["L1_attn_b_norm_w"].rearrange("(c p) -> p c", p=P),
                         allow_slow_non_contiguous=True).then_inc(norm_loaded, 16)
            for kind in range(KINDS):
                load(kind, 0)
            for kind in range(KINDS):
                reload(kind, 1)

            with sp.Fori(0, PAIRS_L // 2 - 1) as r:
                for b in range(2):
                    n = r * 2 + b
                    for q in range(TC):
                        reload(q, n + 2)
                        save(n, b, q)
            for b in range(2):
                for q in range(TC):
                    save(PAIRS_L - 2 + b, b, q)
            for b in range(2):
                sp.wait_ge(saved[b], 16 * (PAIRS_L * TC // 2 + 1))
            sp.wait_ge(norm_loaded, 16)

        @block.gpsimd
        def _(pool):
            link = Chain(pool, consts)
            link(pool.iota(dist_i[:, :], [[1, CH]], base=0, channel_multiplier=-1))
            link(pool.tensor_copy(dist[:, :], dist_i[:, :]))
            link(pool.affine_select(out=dist[:, :], in_=dist[:, :], compare_op=ALU.is_ge, fill=FAR, base=0,
                                    pattern=[[1, CH]], channel_multiplier=-1))
            link(pool.iota(since_i[:, :], [[1, CH]], base=1, channel_multiplier=0))
            link(pool.tensor_copy(since[:, :], since_i[:, :]))
            link(pool.iota(until_i[:, :], [[0, LH]], base=CH - 1, channel_multiplier=-1))
            link(pool.tensor_copy(until[:, :], until_i[:, :]))
            link(pool.memset(state[:, :, :], 0.0))
            link(pool.memset(squares[:, :], 0.0))
            for h, s in enumerate(head_slopes()):
                link(pool.memset(slope_all[:, h:h + 1], -s))
                r = (h % 2) * LD
                link(pool.memset(slope_own[r:r + LD, h // 2:h // 2 + 1], -s))
            assert link.n == N_CONSTS

            def body(n, b, last):
                for q in range(TC):
                    m = n * TC + q
                    pool.wait_ge(o_out, m + 3)
                    pool.tensor_tensor(sq[:, :], osb[:, q % 2, :], osb[:, q % 2, :], ALU.mult).then_inc(sq_step, 1)
                    pool.wait_ge(sq_step, m + 1)
                    pool.tensor_tensor(squares[:, q * NB:(q + 1) * NB], squares[:, q * NB:(q + 1) * NB], sq[:, :], ALU.add).then_inc(sq_done, 1)
                    pool.wait_ge(sq_done, m + 3)

            pool.sem_inc(sq_done, 2)
            over_pairs(pool, body)

        @block.tensor
        def _(pe):
            def weight(kind, n, use):
                pe.wait_ge(w_loaded[kind], n * 32 + 32)
                pe.wait_ge(pr_out, use[0] * USES + (use[1] + 1))
                for k in range(DT):
                    last = nc.tensor.transpose(pr_ps[:, use[1] % 2, k * P:(k + 1) * P], wr[:, kind, k * P:(k + 1) * P], g.ident[:, :])
                last.then_inc(pr_done, 1)

            def piece(kind, t, n):
                use = 5 * kind + t + 1
                pe.wait_ge(pr_out, n * USES + (5 * kind + 2))
                pe.wait_ge(pr_out, n * USES + (use + 1))
                if t == 0:
                    pe.wait_ge(pr_out, n * USES + (5 * kind + 3))
                for k in range(DT):
                    last = nc.tensor.matmul(pr_ps[:, use % 2, :], wt[:, kind, k, :], z[:, k, t * NB:(t + 1) * NB],
                                            start=(k == 0), stop=(k == DT - 1))
                last.then_inc(pr_done, 1)

            def chunk_first(n, b, c):
                m = n * NCH + c
                cols = slice(c * CH, (c + 1) * CH)
                if c == 0:
                    pe.wait_ge(pr_out, n * USES + (USES + 2))
                pe.wait_ge(aw_done, m + 1)
                for hh in range(2):
                    rows = slice(hh * LD, (hh + 1) * LD)
                    last = nc.tensor.matmul(s_ps[:, hh, 0, :], proj[b][rows, 1, cols], proj[b][rows, 0, cols], start=True, stop=True)
                last.then_inc(s_done, 1)
                pe.wait_ge(vt_done, m + 1)
                nc.tensor.transpose(tr_ps[:, 0, :], proj[b][:, 1, cols], g.ident[:, :])
                nc.tensor.transpose(tr_ps[:, 1, :], proj[b][:, 2, cols], g.ident[:, :]).then_inc(tr_done, 1)

            def chunk_second(n, b, c):
                m = n * NCH + c
                q, r = c // TQ, c % TQ
                out = o_ps[:, q % 2, r * CH:(r + 1) * CH]
                if r == 0:
                    pe.wait_ge(o_out, n * TC + (q + 1))
                pe.wait_ge(aw_done, m + 2)
                pe.wait_ge(vt_done, m + 2)
                for hh in range(2):
                    rows = slice(hh * LD, (hh + 1) * LD)
                    last = nc.tensor.matmul(out[rows, :], vt[:, rows], aw[:, hh, :], start=True, stop=(c == 0),
                                            skip_group_check=True)
                if c >= 1:
                    if c == 1:
                        pe.wait_ge(qd_done, n + 1)
                    pe.wait_ge(state_done, m + 1)
                    last = nc.tensor.matmul(out, state[:, c % 2, :], qd[:, c * CH:(c + 1) * CH], start=False, stop=True,
                                            skip_group_check=True)
                last.then_inc(o_done, 1)
                if c < NCH - 1:
                    pe.wait_ge(state_done, m + 1)
                    nc.tensor.matmul(kv_ps[:, 0, :], kt[:, :, :].rearrange("p h d -> p (h d)"), vt[:, :], start=True, stop=True).then_inc(kv_done, 1)
                else:
                    pe.sem_inc(kv_done, 1)

            pe.sem_inc(kv_done, 1)
            pe.wait_ge(consts, N_CONSTS)
            weight(0, 0, (0, 0))
            for kind in range(KINDS):
                for t in range(TC):
                    piece(kind, t, 0)
                if kind < KINDS - 1:
                    weight(kind + 1, 0, (0, 5 * kind + 5))
                else:
                    weight(0, 1, (1, 0))

            def body(n, b, last):
                for c in range(NCH):
                    chunk_first(n, b, c)
                    if not last:
                        kind, t = c // TC, c % TC
                        piece(kind, t, n + 1)
                        if t == TC - 1 and kind < KINDS - 1:
                            weight(kind + 1, n + 1, (n + 1, 5 * kind + 5))
                        elif t == TC - 1 and prefetch[0]:
                            weight(0, n + 2, (n + 2, 0))
                    chunk_second(n, b, c)

            prefetch = [True]
            with pe.Fori(0, PAIRS_L // 2 - 1) as r:
                body(r * 2, 0, False)
                body(r * 2 + 1, 1, False)
            prefetch[0] = False
            body(PAIRS_L - 2, 0, False)
            body(PAIRS_L - 1, 1, True)

        @block.scalar
        def _(act):
            def table(n, b):
                for hh in range(2):
                    nc.scalar.activation(dd[:, b, hh, :], dist[:, :], ACT.Exp, scale=slope_all[:, bass.ds(n * 2 + hh, 1)]).then_inc(tables, 1)
                nc.scalar.activation(qdec[:, b, :], since[:, :], ACT.Exp, scale=slope_own[:, bass.ds(n, 1)]).then_inc(tables, 1)

            def weight_out(kind, use):
                act.wait_ge(pr_done, use[0] * USES + (use[1] + 1))
                nc.scalar.copy(wt[:, kind, :, :].rearrange("p k f -> p (k f)"), pr_ps[:, use[1] % 2, :]).then_inc(pr_out, 1)

            def piece_out(kind, t, n, b):
                use = 5 * kind + t + 1
                act.wait_ge(pr_done, n * USES + (use + 1))
                nc.scalar.activation(proj[b][:, kind, t * NB:(t + 1) * NB], pr_ps[:, use % 2, :],
                                     ACT.Sigmoid if kind == 3 else ACT.Silu).then_inc(pr_out, 1)

            def chunk_out(n, c):
                m = n * NCH + c
                act.wait_ge(tr_done, m + 1)
                act.wait_ge(kv_done, m + 1)
                act.sem_inc(act_passed, 1)
                for hh in range(2):
                    nc.scalar.activation(kt[:, hh, :], tr_ps[:, 0, hh * LD:(hh + 1) * LD], ACT.Copy,
                                         scale=kdec[:, bass.ds(n * 2 + hh, 1)])
                nc.scalar.copy(vt[:, :], tr_ps[:, 1, :]).then_inc(vt_done, 1)

            def quarter_out(n, q):
                act.wait_ge(o_done, n * NCH + (q + 1) * TQ)
                act.wait_ge(sq_done, n * TC + (q + 1))
                act.wait_ge(osb_used, n * TC + (q + 1))
                nc.scalar.copy(osb[:, q % 2, :], o_ps[:, q % 2, :]).then_inc(o_out, 1)

            act.sem_inc(pr_out, 2)
            act.sem_inc(vt_done, 1)
            act.sem_inc(o_out, 2)
            act.wait_ge(consts, N_CONSTS)
            nc.scalar.activation(sdec[:, :], slope_own[:, :], ACT.Exp, scale=float(CH)).then_inc(tables0, 1)
            for h in range(LH):
                nc.scalar.activation(kdec[:, h:h + 1], until[:, h:h + 1], ACT.Exp, scale=slope_all[:, h:h + 1]).then_inc(tables0, 1)
            table(0, 0)
            weight_out(0, (0, 0))
            for kind in range(KINDS):
                for t in range(TC):
                    piece_out(kind, t, 0, 0)
                if kind < KINDS - 1:
                    weight_out(kind + 1, (0, 5 * kind + 5))
                else:
                    weight_out(0, (1, 0))

            def body(n, b, last):
                for c in range(NCH):
                    chunk_out(n, c)
                    if not last:
                        kind, t = c // TC, c % TC
                        if kind == 3 and t == 0:
                            act.wait_ge(gated_done, n * TC + 1)
                        piece_out(kind, t, n + 1, 1 - b)
                        if t == TC - 1 and kind < KINDS - 1:
                            weight_out(kind + 1, (n + 1, 5 * kind + 5))
                        elif t == TC - 1 and prefetch[0]:
                            weight_out(0, (n + 2, 0))
                        if c == NCH // 2:
                            table(n + 1, 1 - b)
                    if c % TQ == TQ - 1:
                        quarter_out(n, c // TQ)

            prefetch = [True]
            with act.Fori(0, PAIRS_L // 2 - 1) as r:
                body(r * 2, 0, False)
                body(r * 2 + 1, 1, False)
            prefetch[0] = False
            body(PAIRS_L - 2, 0, False)
            body(PAIRS_L - 1, 1, True)

        @block.vector
        def _(dve):
            V = nc.vector
            dve.sem_inc(aw_done, 1)
            dve.sem_inc(state_done, 1)
            dve.sem_inc(osb_used, 2)
            dve.sem_inc(saved[0], 16)
            dve.sem_inc(saved[1], 16)
            dve.wait_ge(tables0, 1 + LH)
            dve.wait_ge(norm_loaded, 16)

            def update(n, b, c):
                m = n * NCH + c
                dve.wait_ge(kv_done, m + 2)
                if c == NCH - 1:
                    dve.sem_inc(state_done, 1)
                    return
                for hh in range(2):
                    rows = slice(hh * LD, (hh + 1) * LD)
                    new, old = state[rows, (c + 1) % 2, rows], state[rows, c % 2, rows]
                    if c == 0:
                        ins = V.tensor_copy(new, kv_ps[rows, 0, rows])
                    else:
                        ins = V.scalar_tensor_tensor(out=new, in0=old, scalar=sdec[rows, bass.ds(n, 1)], in1=kv_ps[rows, 0, rows],
                                                     op0=ALU.mult, op1=ALU.add)
                    ins.then_inc(state_step, 1)
                dve.wait_ge(state_step, n * (2 * NCH - 2) + (2 * c + 2))
                dve.sem_inc(state_done, 1)

            def body(n, b, last):
                q_all = proj[b][:, 0, :].rearrange("p (c i) -> p c i", i=CH)
                dve.wait_ge(pr_out, n * USES + (USES + 2))
                dve.wait_ge(tables, n * 3 + 3)
                V.tensor_tensor(qd[:, :].rearrange("p (c i) -> p c i", i=CH), q_all,
                                qdec[:, b, :].rearrange("p (o i) -> p o i", o=1).to_broadcast([P, NCH, CH]), ALU.mult).then_inc(qd_done, 1)
                for c in range(NCH):
                    m = n * NCH + c
                    dve.wait_ge(s_done, m + 1)
                    dve.wait_ge(kv_done, m + 1)
                    V.tensor_tensor(aw[:, :, :], s_ps[:, :, 0, :], dd[:, b, :, :], ALU.mult).then_inc(aw_done, 1)
                    update(n, b, c)
                    if c % TQ == TQ - 1:
                        q = c // TQ
                        dve.wait_ge(o_out, n * TC + (q + 3))
                        dve.wait_ge(saved[q % 2], n * 32 + (q // 2 * 16 + 16))
                        V.scalar_tensor_tensor(out=gated[:, q % 2, :], in0=osb[:, q % 2, :], scalar=norm_w[:, bass.ds(n, 1)],
                                               in1=proj[b][:, 3, q * NB:(q + 1) * NB], op0=ALU.mult, op1=ALU.mult).then_inc(gated_done, 1)
                        dve.wait_ge(gated_done, n * TC + (q + 1))
                        dve.sem_inc(osb_used, 1)

            over_pairs(dve, body)


def linear_outputs(nc, g, name, squares):
    FT = LF // P
    TOK = 2 * P
    with Layer(nc, name) as L:
        w = L.sb("w", [P, 2, LF])
        wt = L.sb("wt", [P, FT, D])
        ones = L.sb("ones", [P, 1])
        ms, rms, inv = L.sb("ms", [P, TT]), L.sb("rms", [P, TT]), L.sb("inv", [P, TT])
        gt = L.sb("gt", [P, 2, FT, TOK])
        w_ps = L.ps("w_ps", [P, 2, 4, P])
        y_ps = L.ps("y_ps", [P, 2, NB])
        ss_ps = L.ps("ss_ps", [P, NB])
        (w_done, w_out, ones_ready, ss_done, ms_ready, rms_ready, inv_ready, y_done, y_used, taken) = (
            L.sem(s) for s in ("w_done", "w_out", "ones_ready", "ss_done", "ms_ready", "rms_ready", "inv_ready", "y_done", "y_used",
                            "taken"))
        w_loaded = [L.sem(f"w_loaded{b}") for b in range(2)]
        loaded = [L.sem(f"loaded{b}") for b in range(2)]
        block = L.block()
        w_rows = g.dram["L1_attn_b_out_w"].rearrange("(c p) f -> p c f", p=P)
        g_rows = g.g_dram.rearrange("(c p) t -> p c t", p=P)

        @block.sync
        def _(sp):
            for c in range(DT):
                if c >= 2:
                    sp.wait_ge(w_done, (c - 1) * 4)
                sp.dma_start(w[:, c % 2, :], w_rows[:, c, :]).then_inc(w_loaded[c % 2], 16)
                if c < 2:
                    sp.dma_start(gt[:, c, :, :], g_rows[:, :, c * TOK:(c + 1) * TOK]).then_inc(loaded[c], 16)
            with sp.Fori(0, T // TOK // 2 - 1) as r:
                for b in range(2):
                    sp.wait_ge(y_done, r * 4 + (2 * b + 2))
                    sp.sem_inc(taken, 1)
                    sp.dma_start(gt[:, b, :, :], g_rows[:, :, bass.ds(r * (2 * TOK) + (2 + b) * TOK, TOK)]).then_inc(loaded[b], 16)
            for b in range(2):
                sp.wait_ge(w_loaded[b], 32)
                sp.wait_ge(loaded[b], 16 * (T // TOK // 2))

        @block.tensor
        def _(pe):
            pe.wait_ge(ones_ready, 1)
            for i in range(TT):
                last = nc.tensor.matmul(ss_ps[:, i:i + 1], squares[:, i * P:(i + 1) * P], ones[:, :], start=True, stop=True)
            last.then_inc(ss_done, 1)
            for c in range(DT):
                pe.wait_ge(w_loaded[c % 2], 16 * (c // 2 + 1))
                for q in range(FT // 4):
                    u = c * 4 + q
                    if u >= 2:
                        pe.wait_ge(w_out, u - 1)
                    for s in range(4):
                        last = nc.tensor.transpose(w_ps[:, u % 2, s, :], w[:, c % 2, (4 * q + s) * P:(4 * q + s + 1) * P], g.ident[:, :])
                    last.then_inc(w_done, 1)
            pe.wait_ge(w_out, DT * 4)
            with pe.Fori(0, T // TOK // 2) as r:
                for b in range(2):
                    pe.wait_ge(loaded[b], r * 16 + 16)
                    for s in range(2):
                        pe.wait_ge(y_used, r * 4 + (2 * b + s + 1))
                        for f in range(FT):
                            last = nc.tensor.matmul(y_ps[:, s, :], gt[:, b, f, s * P:(s + 1) * P], wt[:, f, :],
                                                    start=(f == 0), stop=(f == FT - 1))
                        last.then_inc(y_done, 1)

        @block.scalar
        def _(act):
            for c in range(DT):
                for q in range(FT // 4):
                    u = c * 4 + q
                    act.wait_ge(w_done, u + 1)
                    nc.scalar.copy(wt[:, 4 * q:4 * q + 4, c * P:(c + 1) * P], w_ps[:, u % 2, :, :]).then_inc(w_out, 1)
            act.wait_ge(ms_ready, 1)
            nc.scalar.activation(rms[:, :], ms[:, :], ACT.Sqrt).then_inc(rms_ready, 1)

        @block.vector
        def _(dve):
            V = nc.vector
            dve.sem_inc(y_used, 2)
            V.memset(ones[:, :], 1.0).then_inc(ones_ready, 1)
            dve.wait_ge(ss_done, 1)
            V.tensor_scalar(ms[:, :], ss_ps[:, 0:TT], 1.0 / LF, RMS_EPS, ALU.mult, ALU.add).then_inc(ms_ready, 1)
            dve.wait_ge(rms_ready, 1)
            V.reciprocal(inv[:, :], rms[:, :]).then_inc(inv_ready, 1)
            dve.wait_ge(inv_ready, 1)
            with dve.Fori(0, TT // 2) as pair:
                for s in range(2):
                    i = pair * 2 + s
                    dve.wait_ge(y_done, i + 1)
                    V.scalar_tensor_tensor(out=g.X[:, bass.ds(i, 1), :], in0=y_ps[:, s:s + 1, :], scalar=inv[:, bass.ds(i, 1)],
                                           in1=g.X[:, bass.ds(i, 1), :], op0=ALU.mult, op1=ALU.add).then_inc(y_used, 1)


class Shared:
    pass


LAYERS = {
    1: lambda nc, g: lru(nc, g),
    2: lambda nc, g: ffn(nc, g, "ffn1"),
    3: lambda nc, g: ssm(nc, g),
    4: lambda nc, g: ffn(nc, g, "ffn2"),
    5: lambda nc, g: attention(nc, g),
    6: lambda nc, g: moe(nc, g, "moe1"),
    7: lambda nc, g: linear_attention(nc, g),
    8: lambda nc, g: moe(nc, g, "moe2"),
}
ORDER = (1, 2, 3, 4, 5, 6, 7, 8)


def program(nc, dram):
    with ExitStack() as ctx:
        g = Shared()
        g.dram = dram
        g.X = ctx.enter_context(nc.sbuf_tensor("residual", [P, TT, D], F32))
        g.ident = ctx.enter_context(nc.sbuf_tensor("ident", [P, P], F32))
        g.ident16 = ctx.enter_context(nc.sbuf_tensor("ident16", [P, P], BF16))
        g.z_dram = nc.dram_tensor("normalized_rows", [T, D], F32, kind="Internal").ap()
        g.y_dram = nc.dram_tensor("expert_rows", [E_N * CAP, D], F32, kind="Internal").ap()
        g.qk_dram = [nc.dram_tensor(f"{n}_parts", [PARTS, D, T], BF16, kind="Internal").ap() for n in "qk"]
        g.row_dram = nc.dram_tensor("maximum_rows", [3, T], BF16, kind="Internal").ap()
        g.o_dram = nc.dram_tensor("attention_out", [HEADS, P, T], F32, kind="Internal").ap()
        g.inv_dram = nc.dram_tensor("inverse_sums", [HEADS, T], F32, kind="Internal").ap()
        g.g_dram = nc.dram_tensor("gated_features", [LF, T], F32, kind="Internal").ap()
        setup(nc, g)
        for n in ORDER:
            if n == 2:
                g.ffn_wt = ctx.enter_context(nc.sbuf_tensor("ffn_wt", [P, DT, D], F32))
                g.ffn_bias = ctx.enter_context(nc.sbuf_tensor("ffn_bias", [P, D], F32))
                binarized_weight(nc, g)
            LAYERS[n](nc, g)
        store(nc, g)


_OUT_SHAPE = (1, T, D)


def kernel(**inputs):
    import numpy as _np
    import concourse.bacc as _bacc
    from concourse.bass_utils import run_bass_kernel_spmd as _run

    nc = _bacc.Bacc("TRN2", target_bir_lowering=False, num_devices=1)
    arrays, dram = {}, {}
    for name, value in inputs.items():
        a = _np.ascontiguousarray(value)
        arrays[f"in_{name}"] = a
        dram[name] = nc.dram_tensor(f"in_{name}", a.shape, mybir.dt.from_np(a.dtype), kind="ExternalInput").ap()
    dram["out"] = nc.dram_tensor("out_0", _OUT_SHAPE, F32, kind="ExternalOutput").ap()
    program(nc, dram)
    r = _run(nc, [arrays], core_ids=[0])
    return r.results[0]["out_0"]
```

```python
import math
from contextlib import ExitStack

import concourse.bass as bass
import concourse.mybir as mybir

F32 = mybir.dt.float32
BF16 = mybir.dt.bfloat16
I32 = mybir.dt.int32
U32 = mybir.dt.uint32
ALU = mybir.AluOpType
ACT = mybir.ActivationFunctionType
AX = mybir.AxisListType

P = 128
T = 2048
D = 512
TT = T // P
DT = D // P
NB = 512
TC = T // NB
LN_EPS = 1e-5


class Chain:

    def __init__(self, eng, sem):
        self.eng, self.sem, self.n = eng, sem, 0

    def __call__(self, ins):
        self.n += 1
        ins.then_inc(self.sem, 1)
        self.eng.wait_ge(self.sem, self.n)
        return ins


class Layer:

    def __init__(self, nc, name):
        self.nc, self.name, self.ctx, self.sems = nc, name, ExitStack(), []

    def __enter__(self):
        self.ctx.__enter__()
        return self

    def __exit__(self, *a):
        done = self.ctx.__exit__(*a)
        if a[0] is None:
            self.nc.clear_and_free_semaphores(self.sems)
            self.nc.all_engine_barrier()
        return done

    def sb(self, name, shape, dt=F32):
        return self.ctx.enter_context(self.nc.sbuf_tensor(f"{self.name}_{name}", shape, dt))

    def ps(self, name, shape, dt=F32):
        return self.ctx.enter_context(self.nc.psum_tensor(f"{self.name}_{name}", shape, dt))

    def sem(self, name):
        self.sems.append(self.nc.alloc_semaphore(f"{self.name}_{name}"))
        return self.sems[-1]

    def block(self):
        return self.ctx.enter_context(self.nc.Block())


def setup(nc, g):
    with Layer(nc, "setup") as L:
        loaded, zeroed = L.sem("loaded"), L.sem("zeroed")
        block = L.block()

        @block.sync
        def _(sp):
            sp.dma_start(g.X[:, :, :], g.dram["L0_attn_a_x"][0].rearrange("(i p) d -> p i d", p=P)).then_inc(loaded, 16)
            sp.wait_ge(loaded, 16)

        @block.gpsimd
        def _(pool):
            pool.memset(g.ident[:, :], 0.0).then_inc(zeroed, 1)
            pool.wait_ge(zeroed, 1)
            pool.affine_select(out=g.ident[:, :], in_=g.ident[:, :], compare_op=ALU.not_equal, fill=1.0, base=0,
                               pattern=[[-1, P]], channel_multiplier=1).then_inc(zeroed, 1)
            pool.wait_ge(zeroed, 2)
            pool.tensor_copy(g.ident16[:, :], g.ident[:, :]).then_inc(zeroed, 1)


def store(nc, g):
    with Layer(nc, "store") as L:
        stored = L.sem("stored")
        block = L.block()

        @block.sync
        def _(sp):
            sp.dma_start(g.dram["out"][0].rearrange("(i p) d -> p i d", p=P), g.X[:, :, :]).then_inc(stored, 16)
            sp.wait_ge(stored, 16)


class Norm:

    def __init__(self, L, nc, X):
        self.nc, self.X = nc, X
        self.stats, self.mv = L.sb("norm_stats", [P, TT, 6]), L.sb("norm_mv", [P, TT, 2])
        self.dev, self.rstd = L.sb("norm_dev", [P, TT]), L.sb("norm_rstd", [P, TT])
        self.summed, self.have_var, self.have_dev, self.have_rstd = (
            L.sem(n) for n in ("norm_summed", "norm_have_var", "norm_have_dev", "norm_have_rstd"))

    def on_vector(self, dve):
        nc = self.nc
        for i in range(TT):
            nc.vector.bn_stats(self.stats[:, i, :], self.X[:, i, :]).then_inc(self.summed, 1)
        for i in range(TT):
            dve.wait_ge(self.summed, i + 1)
            nc.vector.bn_aggr(self.mv[:, i, :], self.stats[:, i, :]).then_inc(self.summed, 1)
        dve.wait_ge(self.summed, 2 * TT)
        nc.vector.tensor_scalar(self.dev[:, :], self.mv[:, :, 1], LN_EPS, None, ALU.add).then_inc(self.have_var, 1)
        dve.wait_ge(self.have_dev, 1)
        nc.vector.reciprocal(self.rstd[:, :], self.dev[:, :]).then_inc(self.have_rstd, 1)
        dve.wait_ge(self.have_rstd, 1)

    def on_scalar(self, act):
        act.wait_ge(self.have_var, 1)
        self.nc.scalar.activation(self.dev[:, :], self.dev[:, :], ACT.Sqrt).then_inc(self.have_dev, 1)


def normalized_features(nc, g, name, zt):
    with Layer(nc, name) as L:
        norm = Norm(L, nc, g.X)
        z = L.sb("z", [P, 2, D])
        zt_ps = L.ps("zt_ps", [P, 2, DT, P])
        z_ready, zt_done, zt_ready = (L.sem(s) for s in ("z_ready", "zt_done", "zt_ready"))
        block = L.block()

        @block.vector
        def _(dve):
            norm.on_vector(dve)

            def normalize(i, b):
                nc.vector.tensor_scalar(z[:, b:b + 1, :], g.X[:, bass.ds(i, 1), :], norm.mv[:, bass.ds(i, 1), 0:1],
                                        norm.rstd[:, bass.ds(i, 1)], ALU.subtract, ALU.mult).then_inc(z_ready, 1)

            for b in range(2):
                normalize(b, b)
            with dve.Fori(0, TT // 2 - 1) as pair:
                for b in range(2):
                    dve.wait_ge(zt_done, pair * 2 + (b + 1))
                    normalize(pair * 2 + (2 + b), b)

        @block.tensor
        def _(pe):
            def transposes(i, b, first):
                pe.wait_ge(z_ready, i + 1)
                if not first:
                    pe.wait_ge(zt_ready, i - 1)
                for k in range(DT):
                    last = nc.tensor.transpose(zt_ps[:, b, k, :], z[:, b, k * P:(k + 1) * P], g.ident[:, :])
                last.then_inc(zt_done, 1)

            for b in range(2):
                transposes(b, b, True)
            with pe.Fori(0, TT // 2 - 1) as pair:
                for b in range(2):
                    transposes(pair * 2 + (2 + b), b, False)

        @block.scalar
        def _(act):
            norm.on_scalar(act)
            with act.Fori(0, TT // 2) as pair:
                for b in range(2):
                    act.wait_ge(zt_done, pair * 2 + b + 1)
                    nc.scalar.copy(zt[:, :, bass.ds((pair * 2 + b) * P, P)], zt_ps[:, b, :, :]).then_inc(zt_ready, 1)


def project_and_add(nc, g, name, h, w, bias_dram):
    with Layer(nc, name) as L:
        bias = L.sb("bias", [P, D])
        ht = L.sb("ht", [P, 2, DT, P])
        y_ps = L.ps("y_ps", [P, 2, D])
        loaded, h_ready, y_ready, y_used, biased = (L.sem(s) for s in ("loaded", "h_ready", "y_ready", "y_used", "biased"))
        block = L.block()

        @block.sync
        def _(sp):
            sp.dma_start(bias[:, :], bias_dram.partition_broadcast(P)).then_inc(loaded, 16)
            sp.wait_ge(loaded, 16)

        @block.scalar
        def _(act):
            with act.Fori(0, TT // 2) as pair:
                for b in range(2):
                    i = pair * 2 + b
                    act.wait_ge(y_ready, i + 1)
                    nc.scalar.copy(ht[:, b, :, :], h[:, :, bass.ds(i * P, P)]).then_inc(h_ready, 1)

        @block.tensor
        def _(pe):
            pe.sem_inc(y_ready, 2)
            pe.wait_ge(loaded, 16)
            with pe.Fori(0, TT // 2) as pair:
                for b in range(2):
                    i = pair * 2 + b
                    pe.wait_ge(h_ready, i + 1)
                    pe.wait_ge(y_used, i + 1)
                    for k in range(DT):
                        last = nc.tensor.matmul(y_ps[:, b, :], ht[:, b, k, :], w[:, k, :], start=(k == 0), stop=(k == DT - 1))
                    last.then_inc(y_ready, 1)

        @block.gpsimd
        def _(pool):
            pool.wait_ge(loaded, 16)
            with pool.Fori(0, TT) as i:
                pool.tensor_tensor(g.X[:, bass.ds(i, 1), :], g.X[:, bass.ds(i, 1), :],
                                   bias[:, :].rearrange("p (o d) -> p o d", o=1), ALU.add).then_inc(biased, 1)

        @block.vector
        def _(dve):
            dve.sem_inc(y_used, 2)
            with dve.Fori(0, TT // 2) as pair:
                for b in range(2):
                    i = pair * 2 + b
                    dve.wait_ge(y_ready, i + 3)
                    dve.wait_ge(biased, i + 1)
                    nc.vector.tensor_tensor(g.X[:, bass.ds(i, 1), :], g.X[:, bass.ds(i, 1), :], y_ps[:, b:b + 1, :],
                                            ALU.add).then_inc(y_used, 1)


GATES = D // 2
GT = GATES // P
BLK = 8
BI, BO = D // BLK, GATES // BLK
TWO_PI = 2.0 * math.pi
CUT = T * 11 // 16
ROUND = 1.5 * 2.0 ** 23
PI_BELOW = 3.1415925


def lru(nc, g):
    with ExitStack() as ctx:
        xh = ctx.enter_context(nc.sbuf_tensor("lru_xh", [P, DT, T], F32))
        z = ctx.enter_context(nc.sbuf_tensor("lru_z", [P, DT, T], F32))
        gates = ctx.enter_context(nc.sbuf_tensor("lru_gates", [P, 2, GT, T], F32))
        normalized_features(nc, g, "lrua", z)
        lru_inputs(nc, g, "lrub", z, xh, gates)
        lru_recurrence(nc, g, "lruc", z, xh, gates)
        lru_outputs(nc, g, "lrud", xh)


def lru_inputs(nc, g, name, z, xh, gates):
    with Layer(nc, name) as L:
        w_in = L.sb("w_in", [P, DT, D])
        wg = L.sb("wg", [P, 2, DT, P])
        b_in = L.sb("b_in", [P, DT])
        b_g = L.sb("b_g", [P, 2, GT])
        x_ps = L.ps("x_ps", [P, 4, NB])
        g_ps = L.ps("g_ps", [P, 4, NB])
        cleared, loaded, blocks_loaded, x_done, x_out, g_done, g_out = (
            L.sem(s) for s in ("cleared", "loaded", "blocks_loaded", "x_done", "x_out", "g_done", "g_out"))
        block = L.block()

        @block.sync
        def _(sp):
            sp.dma_start(w_in[:, :, :], g.dram["L0_attn_a_W_in"].rearrange("(k p) f -> p k f", p=P)).then_inc(loaded, 16)
            sp.dma_start(b_in[:, :], g.dram["L0_attn_a_b_in"].rearrange("(c p) -> p c", p=P),
                         allow_slow_non_contiguous=True).then_inc(loaded, 16)
            for j, n in enumerate(("b_gx", "b_ga")):
                for r in range(GT):
                    for b in range(P // BO):
                        sp.dma_start(b_g[b * BO:(b + 1) * BO, j, r:r + 1], g.dram["L0_attn_a_" + n][r * (P // BO) + b, :].rearrange("(f o) -> f o", o=1),
                                     allow_slow_non_contiguous=True).then_inc(loaded, 16)
            sp.wait_ge(cleared, 1)
            for j, n in enumerate(("W_gx", "W_ga")):
                for k in range(DT):
                    for r in range(2):
                        col = (k % 2) * (2 * BO) + r * BO
                        sp.dma_start(wg[r * BI:(r + 1) * BI, j, k, col:col + BO],
                                     g.dram["L0_attn_a_" + n][2 * k + r, :, :]).then_inc(blocks_loaded, 16)
            sp.wait_ge(loaded, 16 * (2 + 2 * BLK))
            sp.wait_ge(blocks_loaded, 16 * 4 * DT)

        @block.gpsimd
        def _(pool):
            pool.memset(wg[:, :, :, :], 0.0).then_inc(cleared, 1)

        @block.tensor
        def _(pe):
            pe.sem_inc(g_done, 1)
            pe.wait_ge(loaded, 16 * (2 + 2 * BLK))
            pe.wait_ge(blocks_loaded, 16 * 4 * DT)
            with pe.Fori(0, TC) as t:
                for f in range(DT):
                    pe.wait_ge(x_out, t * DT + (f + 1))
                    for k in range(DT):
                        last = nc.tensor.matmul(x_ps[:, f, :], w_in[:, k, f * P:(f + 1) * P], z[:, k, bass.ds(t * NB, NB)],
                                                start=(k == 0), stop=(k == DT - 1))
                    last.then_inc(x_done, 1)
                for j in range(2):
                    for r in range(GT):
                        n = 2 * j + r
                        if j == 0:
                            pe.wait_ge(x_out, t * DT + (2 * r + 2 + DT))
                        pe.wait_ge(g_out, t * 4 + (n + 1))
                        for k in range(2):
                            last = nc.tensor.matmul(g_ps[:, n, :], wg[:, j, 2 * r + k, :], xh[:, 2 * r + k, bass.ds(t * NB, NB)],
                                                    start=(k == 0), stop=(k == 1))
                        last.then_inc(g_done, 1)

        @block.scalar
        def _(act):
            act.sem_inc(x_out, DT)
            act.sem_inc(g_out, 4)
            act.wait_ge(loaded, 16 * (2 + 2 * BLK))
            with act.Fori(0, TC) as t:
                for f in range(DT):
                    act.wait_ge(x_done, t * DT + (f + 1))
                    nc.scalar.activation(xh[:, f, bass.ds(t * NB, NB)], x_ps[:, f, :], ACT.Identity,
                                         bias=b_in[:, f:f + 1]).then_inc(x_out, 1)
                for n in range(4):
                    act.wait_ge(g_done, t * 4 + (n + 2))
                    nc.scalar.activation(gates[:, n // 2, n % 2, bass.ds(t * NB, NB)], g_ps[:, n, :], ACT.Sigmoid,
                                         bias=b_g[:, n // 2, n % 2:n % 2 + 1]).then_inc(g_out, 1)


def lru_recurrence(nc, g, name, z, xh, gates):
    with Layer(nc, name) as L:
        a_real, a_imag, fall = L.sb("a_real", [P, GT]), L.sb("a_imag", [P, GT]), L.sb("fall", [P, GT])
        half_pi = L.sb("half_pi", [P, 1])
        ones = L.sb("ones", [P, NB])
        start = L.sb("start", [P, 4])
        t4, t5, t6, t7 = (L.sb(f"t{n}", [P, T]) for n in range(4, 8))
        t0, t1, t2, t3 = (z[:, k, :] for k in range(4))
        loaded, chain, asked, answered, shared, pool_chain, pool_done = (
            L.sem(s) for s in ("loaded", "chain", "asked", "answered", "shared", "pool_chain", "pool_done"))
        block = L.block()

        @block.sync
        def _(sp):
            for t, n in ((a_real, "a_real"), (a_imag, "a_imag")):
                sp.dma_start(t[:, :], g.dram["L0_attn_a_" + n].rearrange("(c p) -> p c", p=P),
                             allow_slow_non_contiguous=True).then_inc(loaded, 16)
            sp.wait_ge(loaded, 32)

        def rotations(eng, link, r, cols):
            xr, xi, s0, s1 = xh[:, r, cols], xh[:, GT + r, cols], t0[:, cols], t1[:, cols]
            for cr, ci, sign in ((t2[:, cols], t5[:, cols], 1), (t4[:, cols], t3[:, cols], -1)):
                link(eng.tensor_tensor(s0, ci, xi, ALU.mult))
                link(eng.tensor_tensor(s1, ci, xr, ALU.mult))
                link(eng.tensor_tensor(xr, cr, xr, ALU.mult))
                link(eng.tensor_tensor(xi, cr, xi, ALU.mult))
                link(eng.tensor_tensor(xr, xr, s0, ALU.subtract if sign > 0 else ALU.add))
                link(eng.tensor_tensor(xi, xi, s1, ALU.add if sign > 0 else ALU.subtract))

        def back(eng, link, r, cols):
            xr, xi, tmp = xh[:, r, cols], xh[:, GT + r, cols], t2[:, cols]
            sr, si, cr, ci = t0[:, cols], t1[:, cols], t4[:, cols], t3[:, cols]
            link(eng.tensor_tensor(xr, cr, sr, ALU.mult))
            link(eng.tensor_tensor(tmp, ci, si, ALU.mult))
            link(eng.tensor_tensor(xr, xr, tmp, ALU.subtract))
            link(eng.tensor_tensor(xi, cr, si, ALU.mult))
            link(eng.tensor_tensor(tmp, ci, sr, ALU.mult))
            link(eng.tensor_tensor(xi, xi, tmp, ALU.add))

        @block.gpsimd
        def _(pool):
            link = Chain(pool, pool_chain)
            for r in range(GT):
                pool.wait_ge(shared, 2 * r + 1)
                rotations(nc.gpsimd, link, r, slice(CUT, T))
                pool.sem_inc(pool_done, 1)
                pool.wait_ge(shared, 2 * r + 2)
                back(nc.gpsimd, link, r, slice(CUT, T))
                pool.sem_inc(pool_done, 1)

        @block.scalar
        def _(act):
            link = Chain(act, answered)
            act.wait_ge(loaded, 32)
            act.wait_ge(asked, 1)
            link(nc.scalar.activation(fall[:, :], a_real[:, :], ACT.Abs))
            link(nc.scalar.activation(fall[:, :], fall[:, :], ACT.Exp, scale=-1.0))
            link(nc.scalar.activation(fall[:, :], fall[:, :], ACT.Ln, bias=1.0))
            for r in range(GT):
                act.wait_ge(asked, 5 * r + 2)
                link(nc.scalar.activation(t7[:, :], gates[:, 1, r, :], ACT.Exp, scale=fall[:, r:r + 1]))
                act.wait_ge(asked, 5 * r + 3)
                link(nc.scalar.activation(t2, t1, ACT.Abs))
                link(nc.scalar.activation(t1, t1, ACT.Sin))
                link(nc.scalar.activation(t2, t2, ACT.Sin, scale=-1.0, bias=half_pi[:, 0:1]))
                act.wait_ge(asked, 5 * r + 4)
                link(nc.scalar.activation(t4[:, :], t3, ACT.Abs))
                link(nc.scalar.activation(t3, t3, ACT.Sin))
                link(nc.scalar.activation(t4[:, :], t4[:, :], ACT.Sin, scale=-1.0, bias=half_pi[:, 0:1]))
                act.wait_ge(asked, 5 * r + 5)
                link(nc.scalar.activation(t2, t2, ACT.Sqrt))
                act.wait_ge(asked, 5 * r + 6)
                link(nc.scalar.activation(t0, t2, ACT.Ln, scale=0.5))
                link(nc.scalar.activation(t0, t0, ACT.Exp, scale=-0.5))
                link(nc.scalar.activation(t2, t2, ACT.Sqrt, scale=0.5))

        @block.vector
        def _(dve):
            link = Chain(dve, chain)
            V = nc.vector

            def mul(out, a, b):
                link(V.tensor_tensor(out, a, b, ALU.mult))

            def add(out, a, b, op=ALU.add):
                link(V.tensor_tensor(out, a, b, op))

            def ask():
                dve.sem_inc(asked, 1)

            def reduce_angle(out, angle, tmp):
                link(V.tensor_scalar(tmp, angle, 1.0 / TWO_PI, ROUND, ALU.mult, ALU.add))
                link(V.tensor_scalar(tmp, tmp, ROUND, -TWO_PI, ALU.subtract, ALU.mult))
                add(out, angle, tmp)
                link(V.tensor_scalar(out, out, PI_BELOW, -PI_BELOW, ALU.min, ALU.max))

            link(V.memset(half_pi[:, :], math.pi / 2))
            link(V.memset(ones[:, :], 1.0))
            ask()
            dve.wait_ge(loaded, 32)
            dve.wait_ge(answered, 3)
            link(V.scalar_tensor_tensor(out=fall[:, :], in0=a_real[:, :], scalar=0.0, in1=fall[:, :], op0=ALU.max, op1=ALU.add))
            link(V.tensor_scalar(fall[:, :], fall[:, :], -8.0, None, ALU.mult))
            got = 3
            for r in range(GT):
                gx, ga = gates[:, 0, r, :], gates[:, 1, r, :]
                xr, xi = xh[:, r, :], xh[:, GT + r, :]
                ask()
                link(V.tensor_scalar(t0, ga, a_imag[:, r:r + 1], None, ALU.mult))
                reduce_angle(t1, t0, t2)
                ask()
                for c in range(TC):
                    cols = slice(c * NB, (c + 1) * NB)
                    if c:
                        reduce_angle(start[:, 0:1], t3[:, c * NB - 1:c * NB], start[:, 1:2])
                    link(V.tensor_tensor_scan(t3[:, cols], ones[:, :], t0[:, cols], start[:, 0:1] if c else 0.0, ALU.mult, ALU.add))
                reduce_angle(t3, t3, t0)
                ask()
                dve.wait_ge(answered, got + 4)
                mul(t0, t7[:, :], t7[:, :])
                mul(t2, t1, t2)
                link(V.scalar_tensor_tensor(out=t5[:, :], in0=t2, scalar=-2.0, in1=t0, op0=ALU.mult, op1=ALU.mult))
                mul(t1, t1, t1)
                link(V.tensor_scalar(t1, t1, 2.0, -1.0, ALU.mult, ALU.add))
                mul(t1, t1, t0)
                link(V.tensor_scalar(t6[:, :], t1, 1.0, None, ALU.add))
                mul(t0, t6[:, :], t6[:, :])
                mul(t1, t5[:, :], t5[:, :])
                link(V.scalar_tensor_tensor(out=t2, in0=t0, scalar=1e-30, in1=t1, op0=ALU.max, op1=ALU.add))
                ask()
                dve.wait_ge(answered, got + 8)
                link(V.scalar_tensor_tensor(out=t2, in0=t6[:, :], scalar=0.0, in1=t2, op0=ALU.max, op1=ALU.add))
                ask()
                mul(xr, xr, gx)
                mul(xi, xi, gx)
                dve.wait_ge(answered, got + 11)
                link(V.scalar_tensor_tensor(out=t5[:, :], in0=t5[:, :], scalar=0.5, in1=t0, op0=ALU.mult, op1=ALU.mult))

                dve.sem_inc(shared, 1)
                rotations(V, link, r, slice(0, CUT))
                dve.wait_ge(pool_done, 2 * r + 1)
                link(V.tensor_tensor_scan(t0, t7[:, :], xr, 0.0, ALU.mult, ALU.add))
                link(V.tensor_tensor_scan(t1, t7[:, :], xi, 0.0, ALU.mult, ALU.add))
                dve.sem_inc(shared, 1)
                back(V, link, r, slice(0, CUT))
                dve.wait_ge(pool_done, 2 * r + 2)
                got += 11


def lru_outputs(nc, g, name, h):
    with nc.sbuf_tensor(f"{name}_w", [P, DT, D], F32) as w:
        with Layer(nc, name + "l") as L:
            loaded = L.sem("loaded")
            block = L.block()

            @block.sync
            def _(sp):
                sp.dma_start(w[:, :, :], g.dram["L0_attn_a_W_out"].rearrange("(k p) f -> p k f", p=P)).then_inc(loaded, 16)
                sp.wait_ge(loaded, 16)
        project_and_add(nc, g, name, h, w, g.dram["L0_attn_a_b_out"])


def binarized_weight(nc, g):
    with Layer(nc, "binw") as L:
        w = L.sb("w", [P, DT, D])
        size = L.sb("size", [P, DT, D])
        alpha = L.sb("alpha", [P, DT])
        bw = L.sb("bw", [P, DT, D])
        wt_ps = L.ps("wt_ps", [P, 2, D])
        loaded, chain, w_ready, wt_done, copied = (L.sem(s) for s in ("loaded", "chain", "w_ready", "wt_done", "copied"))
        block = L.block()

        @block.sync
        def _(sp):
            sp.dma_start(w[:, :, :], g.dram["L0_ffn_weight"].rearrange("(c p) i -> p c i", p=P)).then_inc(loaded, 16)
            sp.dma_start(g.ffn_bias[:, :], g.dram["L0_ffn_bias"].partition_broadcast(P)).then_inc(loaded, 16)
            sp.wait_ge(loaded, 32)

        @block.vector
        def _(dve):
            link = Chain(dve, chain)
            dve.wait_ge(loaded, 32)
            link(nc.vector.tensor_scalar(size[:, :, :], w[:, :, :], -1.0, None, ALU.mult))
            link(nc.vector.tensor_tensor(size[:, :, :], size[:, :, :], w[:, :, :], ALU.max))
            link(nc.vector.tensor_reduce(alpha[:, :], size[:, :, :], axis=AX.X, op=ALU.add))
            link(nc.vector.tensor_scalar(alpha[:, :], alpha[:, :], 1.0 / D, None, ALU.mult))
            link(nc.vector.tensor_scalar(bw[:, :, :], w[:, :, :], 0.0, 2.0, ALU.is_ge, ALU.mult))
            link(nc.vector.tensor_scalar(bw[:, :, :], bw[:, :, :], -1.0, None, ALU.add))
            for c in range(DT):
                link(nc.vector.tensor_scalar(bw[:, c, :], bw[:, c, :], alpha[:, c:c + 1], None, ALU.mult))
            link(nc.vector.tensor_tensor(bw[:, :, :], bw[:, :, :], w[:, :, :], ALU.subtract))
            nc.vector.tensor_tensor(bw[:, :, :], bw[:, :, :], w[:, :, :], ALU.add).then_inc(w_ready, 1)

        @block.tensor
        def _(pe):
            pe.wait_ge(w_ready, 1)
            for k in range(DT):
                if k >= 2:
                    pe.wait_ge(copied, k - 1)
                for c in range(DT):
                    last = nc.tensor.transpose(wt_ps[:, k % 2, c * P:(c + 1) * P], bw[:, c, k * P:(k + 1) * P], g.ident[:, :])
                last.then_inc(wt_done, 1)

        @block.scalar
        def _(act):
            for k in range(DT):
                act.wait_ge(wt_done, k + 1)
                nc.scalar.copy(g.ffn_wt[:, k, :], wt_ps[:, k % 2, :]).then_inc(copied, 1)


def ffn(nc, g, name):
    with Layer(nc, name) as L:
        norm = Norm(L, nc, g.X)
        z = L.sb("z", [P, 2, D])
        zt = L.sb("zt", [P, 2, D])
        zt_ps = L.ps("zt_ps", [P, 2, D])
        y_ps = L.ps("y_ps", [P, 2, D])
        z_ready, zt_done, zt_ready, y_ready, y_used, biased = (
            L.sem(s) for s in ("z_ready", "zt_done", "zt_ready", "y_ready", "y_used", "biased"))
        block = L.block()

        @block.vector
        def _(dve):
            norm.on_vector(dve)
            mv, rstd = norm.mv, norm.rstd

            def normalize(i, b):
                nc.vector.tensor_scalar(z[:, b, :], g.X[:, i, :], mv[:, i, 0:1], rstd[:, i:i + 1],
                                        ALU.subtract, ALU.mult).then_inc(z_ready, 1)

            dve.sem_inc(y_used, 2)
            normalize(0, 0)
            normalize(1, 1)
            with dve.Fori(0, TT // 2 - 1) as pair:
                for b in range(2):
                    i = pair * 2 + b
                    dve.wait_ge(zt_done, i + 1)
                    nc.vector.tensor_scalar(z[:, b:b + 1, :], g.X[:, bass.ds(i + 2, 1), :], mv[:, bass.ds(i + 2, 1), 0:1],
                                            rstd[:, bass.ds(i + 2, 1)], ALU.subtract, ALU.mult).then_inc(z_ready, 1)
                    dve.wait_ge(y_ready, i + 1)
                    dve.wait_ge(biased, i + 1)
                    nc.vector.tensor_tensor(g.X[:, bass.ds(i, 1), :], g.X[:, bass.ds(i, 1), :], y_ps[:, b:b + 1, :], ALU.add).then_inc(y_used, 1)
            for b in range(2):
                dve.wait_ge(y_ready, TT - 1 + b)
                dve.wait_ge(biased, TT - 1 + b)
                nc.vector.tensor_tensor(g.X[:, TT - 2 + b, :], g.X[:, TT - 2 + b, :], y_ps[:, b, :], ALU.add).then_inc(y_used, 1)

        @block.gpsimd
        def _(pool):
            with pool.Fori(0, TT) as i:
                pool.wait_ge(z_ready, i + 1)
                nc.gpsimd.tensor_tensor(g.X[:, bass.ds(i, 1), :], g.X[:, bass.ds(i, 1), :],
                                        g.ffn_bias[:, :].rearrange("p (o d) -> p o d", o=1), ALU.add).then_inc(biased, 1)

        @block.tensor
        def _(pe):
            def transposes(i, b):
                pe.wait_ge(z_ready, i + 1)
                for k in range(DT):
                    last = nc.tensor.transpose(zt_ps[:, b, k * P:(k + 1) * P], z[:, b, k * P:(k + 1) * P], g.ident[:, :])
                last.then_inc(zt_done, 1)

            def product(i, b):
                pe.wait_ge(zt_ready, i + 1)
                pe.wait_ge(y_used, i + 1)
                for k in range(DT):
                    last = nc.tensor.matmul(y_ps[:, b, :], zt[:, b, k * P:(k + 1) * P], g.ffn_wt[:, k, :],
                                            start=(k == 0), stop=(k == DT - 1))
                last.then_inc(y_ready, 1)

            for b in range(2):
                transposes(b, b)
            with pe.Fori(0, TT // 2 - 1) as pair:
                for b in range(2):
                    product(pair * 2 + b, b)
                    transposes(pair * 2 + (2 + b), b)
            for b in range(2):
                product(TT - 2 + b, b)

        @block.scalar
        def _(act):
            norm.on_scalar(act)
            with act.Fori(0, TT // 2) as pair:
                for b in range(2):
                    act.wait_ge(zt_done, pair * 2 + b + 1)
                    nc.scalar.copy(zt[:, b, :], zt_ps[:, b, :]).then_inc(zt_ready, 1)


N_STATE = 16
Q = 4
QP = Q - 1
DT_MIN = 1e-4


def ssm(nc, g):
    with nc.sbuf_tensor("ssm_u", [P, DT, T], F32) as u:
        normalized_features(nc, g, "ssma", u)
        ssm_scan(nc, g, "ssmb", u)


def ssm_scan(nc, g, name, u):
    with Layer(nc, name) as L:
        bias = L.sb("bias", [P, 4, DT])
        a_raw, b_base, c_base = (L.sb(s, [P, DT, N_STATE]) for s in ("a_raw", "b_base", "c_base"))
        a_pos = L.sb("a_pos", [P, DT, N_STATE])
        rate = L.sb("rate", [P, DT, N_STATE])
        gain = L.sb("gain", [P, DT, N_STATE])
        w = L.sb("w", [P, 2, 3, DT, P])
        raw, soft = L.sb("raw", [P, NB]), L.sb("soft", [P, NB])
        dt, bu, c = (L.sb(s, [P, 2, T]) for s in ("dt", "bu", "c"))
        decay = L.sb("decay", [P, 2, T])
        state = L.sb("state", [P, Q, T])
        acc = L.sb("acc", [P, T])
        diag = L.sb("diag", [P, QP, P])
        zero16 = L.sb("zero16", [P, P], BF16)
        zcol16 = L.sb("zcol16", [P, NB], BF16)
        y = L.sb("y", [P, T])
        y_ps = L.ps("y_ps", [P, TC, NB])
        pr_ps = L.ps("pr_ps", [P, 3, NB])
        tr_ps = L.ps("tr_ps", [P, 4, P])
        (par_loaded, a_abs, consts, zeroed, w_loaded0, w_loaded1, pr_done, raw_out, c_out, b_out, soft_done, dt_done, decay_done,
         state_done, diag_done, summed, y_full, y_read, y_done, tr_done, added, chain, achain, pchain, dt_half, bu_done,
         scaled, acc_done, y_summed) = (
            L.sem(s) for s in ("par_loaded", "a_abs", "consts", "zeroed", "w_loaded0", "w_loaded1", "pr_done", "raw_out", "c_out",
                               "b_out", "soft_done", "dt_done", "decay_done", "state_done", "diag_done", "summed", "y_full",
                               "y_read", "y_done", "tr_done", "added", "chain", "achain", "pchain",
                               "dt_half", "bu_done", "scaled", "acc_done", "y_summed"))
        w_loaded = (w_loaded0, w_loaded1)
        block = L.block()

        @block.sync
        def _(sp):
            for j, n in enumerate(("bdt", "bb", "bc", "D")):
                sp.dma_start(bias[:, j, :], g.dram["L0_attn_b_" + n].rearrange("(c p) -> p c", p=P),
                             allow_slow_non_contiguous=True).then_inc(par_loaded, 16)
            for t, n in ((a_raw, "a_raw"), (b_base, "B_base"), (c_base, "C_base")):
                sp.dma_start(t[:, :, :], g.dram["L0_attn_b_" + n].rearrange("(c p) n -> p c n", p=P)).then_inc(par_loaded, 16)
            for e in range(DT):
                if e >= 2:
                    sp.wait_ge(pr_done, (e - 1) * TC)
                for j, n in enumerate(("Wdt", "Wb", "Wc")):
                    sp.dma_start(w[:, e % 2, j, :, :], g.dram["L0_attn_b_" + n][:, e * P:(e + 1) * P]
                                 .rearrange("(k p) f -> p k f", p=P)).then_inc(w_loaded[e % 2], 16)
            sp.wait_ge(par_loaded, 16 * 7)
            for b in range(2):
                sp.wait_ge(w_loaded[b], 2 * 48)

        @block.gpsimd
        def _(pool):
            pool.memset(zero16[:, :], 0.0).then_inc(zeroed, 1)
            pool.memset(zcol16[:, :], 0.0).then_inc(zeroed, 1)
            pool.wait_ge(par_loaded, 16 * 7)
            pool.tensor_tensor(gain[:, :, :], b_base[:, :, :], c_base[:, :, :], ALU.mult).then_inc(pchain, 1)
            pool.wait_ge(pchain, 1)
            gains = gain[:, :, :].rearrange("p c n -> p (c n)")

            def quarter(e, tq, first):
                m = tq + e * TC
                for j in range(QP):
                    pool.wait_ge(summed, m * QP + (j + 1))
                    pool.tensor_tensor(diag[:, j, :], g.ident[:, :], gains[:, bass.ds(m * Q + (1 + j), 1)].to_broadcast([P, P]),
                                       ALU.mult).then_inc(diag_done, 1)
                pool.wait_ge(state_done, m * Q + 3)
                if first and e >= 1:
                    pool.wait_ge(y_summed, e)
                own, own_gain = state[:, 0, :], gains[:, bass.ds(m * Q, 1)].to_broadcast([P, T])
                if first:
                    pool.tensor_tensor(acc[:, :], own, own_gain, ALU.mult).then_inc(scaled, 1)
                    pool.wait_ge(scaled, m + 1)
                    pool.sem_inc(acc_done, 1)
                else:
                    pool.tensor_tensor(own, own, own_gain, ALU.mult).then_inc(scaled, 1)
                    pool.wait_ge(scaled, m + 1)
                    pool.tensor_tensor(acc[:, :], acc[:, :], own, ALU.add).then_inc(acc_done, 1)

            pool.sem_inc(acc_done, 1)
            for e in range(DT):
                quarter(e, 0, True)
                with pool.Fori(0, TC - 1) as r:
                    quarter(e, r + 1, False)

        @block.tensor
        def _(pe):
            def products(e, tq):
                m = tq + e * TC
                if e == 0:
                    pe.wait_ge(w_loaded[0], 48)
                else:
                    pe.wait_ge(w_loaded[e % 2], 48 * (e // 2 + 1))
                for j, out in enumerate((raw_out, b_out, c_out)):
                    pe.wait_ge(out, m + 1)
                    for k in range(DT):
                        last = nc.tensor.matmul(pr_ps[:, j, :], w[:, e % 2, j, k, :], u[:, k, bass.ds(tq * NB, NB)],
                                                start=(k == 0), stop=(k == DT - 1))
                last.then_inc(pr_done, 1)

            def back(e):
                pe.wait_ge(y_done, e + 1)
                for t in range(TC):
                    pe.wait_ge(added, t + (e * TC + 1))
                    for s in range(4):
                        last = nc.tensor.transpose(tr_ps[:, s, :], y[:, t * NB + s * P:t * NB + (s + 1) * P], g.ident[:, :])
                    last.then_inc(tr_done, 1)

            pe.sem_inc(summed, QP)
            pe.wait_ge(zeroed, 2)
            with pe.Fori(0, TC) as tq:
                products(0, tq)
            for e in range(DT):
                if e >= 1:
                    pe.wait_ge(y_summed, e)
                for t in range(TC):
                    nc.tensor.matmul(y_ps[:, t, :], zero16[:, :], zcol16[:, :], start=True, stop=False)
                if e >= 1:
                    back(e - 1)
                with pe.Fori(0, TC) as tq:
                    if e + 1 < DT:
                        products(e + 1, tq)
                    for j in range(QP):
                        pe.wait_ge(state_done, tq * Q + (e * N_STATE + j + 4))
                        pe.wait_ge(diag_done, tq * QP + (e * TC * QP + j + 1))
                        for t in range(TC):
                            last = nc.tensor.matmul(y_ps[:, t, :], diag[:, j, :], state[:, j + 1, t * NB:(t + 1) * NB],
                                                    start=False, stop=False)
                        last.then_inc(summed, 1)
                for t in range(TC):
                    last = nc.tensor.matmul(y_ps[:, t, :], zero16[:, :], zcol16[:, :], start=False, stop=True)
                last.then_inc(y_full, 1)
            back(DT - 1)

        @block.scalar
        def _(act):
            link = Chain(act, achain)
            act.wait_ge(par_loaded, 16 * 7)
            act.sem_inc(raw_out, 1)
            act.sem_inc(c_out, 1)
            link(nc.scalar.activation(rate[:, :, :], a_raw[:, :, :], ACT.Abs))
            link(nc.scalar.activation(rate[:, :, :], rate[:, :, :], ACT.Exp, scale=-1.0))
            nc.scalar.activation(a_pos[:, :, :], rate[:, :, :], ACT.Ln, bias=1.0).then_inc(a_abs, 1)
            act.wait_ge(consts, 1)

            def evacuate(e, tq):
                m = tq + e * TC
                cols = bass.ds(tq * NB, NB)
                act.wait_ge(pr_done, m + 1)
                if e >= 2:
                    act.wait_ge(y_read, e - 1)
                act.wait_ge(dt_done, m + 1)
                nc.scalar.activation(raw[:, :], pr_ps[:, 0, :], ACT.Identity, bias=bias[:, 0, e:e + 1]).then_inc(raw_out, 1)
                nc.scalar.activation(c[:, e % 2, cols], pr_ps[:, 2, :], ACT.Identity, bias=bias[:, 2, e:e + 1]).then_inc(c_out, 1)
                act.wait_ge(raw_out, m + 2)
                nc.scalar.activation(soft[:, :], raw[:, :], ACT.Abs).then_inc(achain, 1)
                act.wait_ge(achain, tq * 2 + (2 + e * TC * 2 + 1))
                nc.scalar.activation(soft[:, :], soft[:, :], ACT.Exp, scale=-1.0).then_inc(achain, 1)
                act.wait_ge(achain, tq * 2 + (2 + e * TC * 2 + 2))
                nc.scalar.activation(soft[:, :], soft[:, :], ACT.Ln, bias=1.0).then_inc(soft_done, 1)

            with act.Fori(0, TC) as tq:
                evacuate(0, tq)
            for e in range(DT):
                act.wait_ge(dt_done, e * TC + TC + 1)
                with act.Fori(0, TC) as tq:
                    for j in range(Q):
                        n = tq * Q + (e * N_STATE + j)
                        act.wait_ge(state_done, n + 1)
                        nc.scalar.activation(decay[:, j % 2, :], dt[:, e % 2, :], ACT.Exp,
                                             scale=rate[:, e, bass.ds(tq * Q + j, 1)]).then_inc(decay_done, 1)
                    if e + 1 < DT:
                        evacuate(e + 1, tq)

        @block.vector
        def _(dve):
            link = Chain(dve, chain)
            dve.sem_inc(state_done, 2)
            dve.sem_inc(dt_done, 1)
            dve.sem_inc(b_out, 1)
            dve.sem_inc(added, 1)
            dve.wait_ge(par_loaded, 16 * 7)
            dve.wait_ge(a_abs, 1)
            link(nc.vector.scalar_tensor_tensor(out=a_pos[:, :, :], in0=a_raw[:, :, :], scalar=0.0, in1=a_pos[:, :, :],
                                                op0=ALU.max, op1=ALU.add))
            nc.vector.tensor_scalar(rate[:, :, :], a_pos[:, :, :], -1.0, None, ALU.mult).then_inc(consts, 1)

            def chunk(e, tq):
                m = tq + e * TC
                cols = bass.ds(tq * NB, NB)
                dve.wait_ge(pr_done, m + 1)
                nc.vector.scalar_tensor_tensor(out=bu[:, e % 2, cols], in0=pr_ps[:, 1, :], scalar=bias[:, 1, e:e + 1],
                                               in1=u[:, e, cols], op0=ALU.add, op1=ALU.mult).then_inc(b_out, 1)
                dve.wait_ge(soft_done, m + 1)
                if e >= 2:
                    dve.wait_ge(decay_done, (e - 1) * N_STATE)
                nc.vector.scalar_tensor_tensor(out=dt[:, e % 2, cols], in0=raw[:, :], scalar=0.0, in1=soft[:, :],
                                               op0=ALU.max, op1=ALU.add).then_inc(dt_half, 1)
                dve.wait_ge(dt_half, m + 1)
                dve.wait_ge(b_out, m + 2)
                nc.vector.tensor_scalar(dt[:, e % 2, cols], dt[:, e % 2, cols], DT_MIN, None, ALU.add).then_inc(dt_done, 1)
                dve.wait_ge(dt_done, m + 2)
                nc.vector.tensor_tensor(bu[:, e % 2, cols], bu[:, e % 2, cols], dt[:, e % 2, cols], ALU.mult).then_inc(bu_done, 1)

            def add_back(e, tq):
                dve.wait_ge(tr_done, tq + (e * TC + 1))
                nc.vector.tensor_tensor(g.X[:, bass.ds(tq * 4, 4), e * P:(e + 1) * P], g.X[:, bass.ds(tq * 4, 4), e * P:(e + 1) * P],
                                        tr_ps[:, :, :], ALU.add).then_inc(added, 1)

            with dve.Fori(0, TC) as tq:
                chunk(0, tq)
            for e in range(DT):
                dve.wait_ge(bu_done, (e + 1) * TC)
                if e >= 1:
                    with dve.Fori(0, TC) as tq:
                        add_back(e - 1, tq)
                with dve.Fori(0, TC) as tq:
                    for j in range(Q):
                        n = tq * Q + (e * N_STATE + j)
                        dve.wait_ge(decay_done, n + 1)
                        if j == 0:
                            dve.wait_ge(acc_done, tq + (e * TC + 1))
                        else:
                            dve.wait_ge(summed, tq * QP + (e * TC * QP + j))
                        nc.vector.tensor_tensor_scan(state[:, j, :], decay[:, j % 2, :], bu[:, e % 2, :], 0.0,
                                                     ALU.mult, ALU.add).then_inc(state_done, 1)
                    if e + 1 < DT:
                        chunk(e + 1, tq)
                dve.wait_ge(y_full, e + 1)
                dve.wait_ge(acc_done, (e + 1) * TC + 1)
                nc.vector.tensor_tensor(y[:, :], y_ps[:, :, :].rearrange("p t n -> p (t n)"), acc[:, :], ALU.add).then_inc(y_summed, 1)
                dve.wait_ge(y_summed, e + 1)
                nc.vector.tensor_tensor(y[:, :], y[:, :], c[:, e % 2, :], ALU.mult).then_inc(y_read, 1)
                dve.wait_ge(y_read, e + 1)
                nc.vector.scalar_tensor_tensor(out=y[:, :], in0=u[:, e, :], scalar=bias[:, 3, e:e + 1], in1=y[:, :],
                                               op0=ALU.mult, op1=ALU.add).then_inc(y_done, 1)
            with dve.Fori(0, TC) as tq:
                add_back(DT - 1, tq)


HEADS = 16
DH = D // HEADS
SBLK = 1024
PARTS = 3
STACK = PARTS * DH


class WeightTranspose:

    def __init__(self, L, nc, g, weights):
        self.nc, self.g, self.weights = nc, g, weights
        self.w = L.sb("w", [P, len(weights), DT, D])
        self.w_ps = L.ps("w_ps", [P, 2, DT, P])
        self.loaded = [L.sem(f"w_loaded{j}") for j in range(len(weights))]
        self.done, self.out = L.sem("w_done"), L.sem("w_out")
        self.steps = [(j, c) for j in range(len(weights)) for c in range(DT)]

    def on_sync(self, sp):
        for j, (dram_w, _) in enumerate(self.weights):
            sp.dma_start(self.w[:, j, :, :], dram_w.rearrange("(c p) i -> p c i", p=P)).then_inc(self.loaded[j], 16)

    def on_tensor(self, pe):
        for n, (j, c) in enumerate(self.steps):
            pe.wait_ge(self.loaded[j], 16)
            if n >= 2:
                pe.wait_ge(self.out, n - 1)
            for k in range(DT):
                last = self.nc.tensor.transpose(self.w_ps[:, n % 2, k, :], self.w[:, j, c, k * P:(k + 1) * P], self.g.ident[:, :])
            last.then_inc(self.done, 1)

    def on_scalar(self, act):
        for n, (j, c) in enumerate(self.steps):
            act.wait_ge(self.done, n + 1)
            self.nc.scalar.copy(self.weights[j][1][:, :, c * P:(c + 1) * P], self.w_ps[:, n % 2, :, :]).then_inc(self.out, 1)


def transpose_weights(nc, g, name, weights):
    with Layer(nc, name) as L:
        turn = WeightTranspose(L, nc, g, weights)
        block = L.block()

        @block.sync
        def _(sp):
            turn.on_sync(sp)

        @block.tensor
        def _(pe):
            turn.on_tensor(pe)

        @block.scalar
        def _(act):
            turn.on_scalar(act)


def attention(nc, g):
    with ExitStack() as ctx:
        v = ctx.enter_context(nc.sbuf_tensor("att_v", [P, TT, HEADS, PARTS + 1, DH], BF16))
        with ExitStack() as inner:
            z = inner.enter_context(nc.sbuf_tensor("att_z", [P, DT, T], F32))
            wt = [inner.enter_context(nc.sbuf_tensor(f"att_wt{j}", [P, DT, D], F32)) for j in range(3)]
            normalized_features(nc, g, "atta", z)
            transpose_weights(nc, g, "attw", [(g.dram["L1_attn_a_" + n], wt[j]) for j, n in enumerate(("Wq", "Wk", "Wv"))])
            attention_inputs(nc, g, "attb", z, wt, v)
        attention_heads(nc, g, "attc", v)
    with ExitStack() as ctx:
        o = ctx.enter_context(nc.sbuf_tensor("att_o", [P, PARTS, DT, T], F32))
        wo = ctx.enter_context(nc.sbuf_tensor("att_wo", [P, DT, D], F32))
        attention_outputs(nc, g, "atte", o, wo)


def attention_inputs(nc, g, name, z, wt, v):
    with Layer(nc, name) as L:
        b_qk = L.sb("b_qk", [P, 2, DT])
        rot = L.sb("rot", [P, DT])
        tmp = L.sb("tmp", [P, DT])
        scale = L.sb("scale", [P, 2, DT])
        spiral = L.sb("spiral", [P, DT])
        half_pi = L.sb("half_pi", [P, 1])
        bv = L.sb("bv", [P, D])
        whole, rest = L.sb("whole", [P, 2, NB]), L.sb("rest", [P, 2, NB])
        parts = L.sb("parts", [P, 2, PARTS, NB], BF16)
        zt = L.sb("zt", [P, 2, DT, P])
        p_ps = L.ps("p_ps", [P, 2, NB])
        v_ps = L.ps("v_ps", [P, 2, NB])
        (loaded, chain, reduced, angles, consts, prod, whole_out, split_chain, split_done, zt_ready, v_done, v_out, split_step, v_step, ones_set) = (
            L.sem(s) for s in ("loaded", "chain", "reduced", "angles", "consts", "prod", "whole_out", "split_chain", "split_done",
                               "zt_ready", "v_done", "v_out", "split_step", "v_step", "ones_set"))
        saved = [L.sem(f"saved{b}") for b in range(2)]
        block = L.block()
        FT = 2 * DT
        N_PAR = 2 + 1 + 1 + HEADS

        @block.sync
        def _(sp):
            for j, n in enumerate(("bq", "bk")):
                sp.dma_start(b_qk[:, j, :], g.dram["L1_attn_a_" + n].rearrange("(c p) -> p c", p=P),
                             allow_slow_non_contiguous=True).then_inc(loaded, 16)
            sp.dma_start(rot[:, :], g.dram["L1_attn_a_helix_rotation"].rearrange("(c p) -> p c", p=P),
                         allow_slow_non_contiguous=True).then_inc(loaded, 16)
            sp.dma_start(bv[:, :], g.dram["L1_attn_a_bv"].partition_broadcast(P)).then_inc(loaded, 16)
            for h in range(HEADS):
                r = (h % (P // DH)) * DH
                sp.dma_start(spiral[r:r + DH, h // (P // DH):h // (P // DH) + 1],
                             g.dram["L1_attn_a_spiral_weight"][h:h + 1].partition_broadcast(DH)).then_inc(loaded, 16)
            for j in range(2):
                dst = g.qk_dram[j].rearrange("r (c p) t -> p c r t", p=P)
                with sp.Fori(0, TC) as t:
                    for f in range(DT):
                        sp.wait_ge(split_done, t * DT + (j * TC * DT + f + 1))
                        sp.dma_start(dst[:, f, :, bass.ds(t * NB, NB)], parts[:, f % 2, :, :]).then_inc(saved[f % 2], 16)
            for b in range(2):
                sp.wait_ge(saved[b], 16 * (TC * FT // 2 + 1))

        @block.gpsimd
        def _(pool):
            pool.memset(v[:, :, :, PARTS, :], 1.0).then_inc(ones_set, 1)

        @block.tensor
        def _(pe):
            def product(j, f, t, m):
                pe.wait_ge(whole_out, m + 1)
                for k in range(DT):
                    last = nc.tensor.matmul(p_ps[:, f % 2, :], wt[j][:, k, f * P:(f + 1) * P], z[:, k, bass.ds(t * NB, NB)],
                                            start=(k == 0), stop=(k == DT - 1))
                last.then_inc(prod, 1)

            for j in range(2):
                with pe.Fori(0, TC) as t:
                    for f in range(DT):
                        product(j, f, t, t * DT + (j * TC * DT + f))
            pe.sem_inc(v_done, 2)
            with pe.Fori(0, TT // 2) as pair:
                for b in range(2):
                    i = pair * 2 + b
                    pe.wait_ge(zt_ready, i + 1)
                    pe.wait_ge(v_out, i + 1)
                    for k in range(DT):
                        last = nc.tensor.matmul(v_ps[:, b, :], zt[:, b, k, :], wt[2][:, k, :], start=(k == 0), stop=(k == DT - 1))
                    last.then_inc(v_done, 1)

        @block.scalar
        def _(act):
            act.sem_inc(whole_out, 2)
            act.wait_ge(reduced, 1)
            nc.scalar.activation(scale[:, 1, :], rot[:, :], ACT.Sin).then_inc(angles, 1)
            nc.scalar.activation(tmp[:, :], rot[:, :], ACT.Abs).then_inc(angles, 1)
            act.wait_ge(angles, 2)
            nc.scalar.activation(scale[:, 0, :], tmp[:, :], ACT.Sin, scale=-1.0, bias=half_pi[:, 0:1]).then_inc(angles, 1)
            act.wait_ge(consts, 1)
            for j in range(2):
                with act.Fori(0, TC) as t:
                    for f in range(DT):
                        m = t * DT + (j * TC * DT + f)
                        act.wait_ge(prod, m + 1)
                        act.wait_ge(split_chain, m * 2 + 2)
                        nc.scalar.activation(whole[:, f % 2, :], p_ps[:, f % 2, :], ACT.Identity, scale=scale[:, j, f:f + 1],
                                             bias=b_qk[:, j, f:f + 1]).then_inc(whole_out, 1)
            with act.Fori(0, TT // 2) as pair:
                for b in range(2):
                    act.wait_ge(v_done, pair * 2 + (b + 1))
                    nc.scalar.copy(zt[:, b, :, :], z[:, :, bass.ds((pair * 2 + b) * P, P)]).then_inc(zt_ready, 1)

        @block.vector
        def _(dve):
            link = Chain(dve, chain)
            V = nc.vector
            dve.sem_inc(split_chain, 4)
            dve.sem_inc(saved[0], 16)
            dve.sem_inc(saved[1], 16)
            dve.sem_inc(v_out, 2)
            dve.wait_ge(loaded, 16 * N_PAR)
            link(V.memset(half_pi[:, :], math.pi / 2))
            link(V.tensor_scalar(tmp[:, :], rot[:, :], 1.0 / TWO_PI, ROUND, ALU.mult, ALU.add))
            link(V.tensor_scalar(tmp[:, :], tmp[:, :], ROUND, -TWO_PI, ALU.subtract, ALU.mult))
            link(V.tensor_tensor(rot[:, :], rot[:, :], tmp[:, :], ALU.add))
            V.tensor_scalar(rot[:, :], rot[:, :], PI_BELOW, -PI_BELOW, ALU.min, ALU.max).then_inc(reduced, 1)
            dve.wait_ge(angles, 3)
            link(V.tensor_scalar(spiral[:, :], spiral[:, :], 1.0 / math.sqrt(DH), None, ALU.mult))
            link(V.tensor_tensor(scale[:, 0, :], scale[:, 0, :], spiral[:, :], ALU.mult))
            V.tensor_tensor(b_qk[:, :, :], b_qk[:, :, :], scale[:, :, :], ALU.mult).then_inc(consts, 1)
            for j in range(2):
                with dve.Fori(0, TC) as t:
                    for f in range(DT):
                        m = t * DT + (j * TC * DT + f)
                        b = f % 2
                        dve.wait_ge(whole_out, m + 3)
                        dve.wait_ge(saved[b], t * 32 + (j * TC * 32 + (f // 2) * 16 + 16))
                        V.tensor_copy(parts[:, b, 0, :], whole[:, b, :]).then_inc(split_step, 1)
                        dve.wait_ge(split_step, m * 3 + 1)
                        V.tensor_tensor(rest[:, b, :], whole[:, b, :], parts[:, b, 0, :], ALU.subtract).then_inc(split_chain, 2)
                        dve.wait_ge(split_chain, m * 2 + 6)
                        V.tensor_copy(parts[:, b, 1, :], rest[:, b, :]).then_inc(split_step, 2)
                        dve.wait_ge(split_step, m * 3 + 3)
                        V.tensor_tensor(parts[:, b, 2, :], rest[:, b, :], parts[:, b, 1, :], ALU.subtract).then_inc(split_done, 1)
            with dve.Fori(0, TT // 2) as pair:
                for b in range(2):
                    i = pair * 2 + b
                    dve.wait_ge(v_done, i + 3)
                    V.tensor_tensor(whole[:, b, :], v_ps[:, b, :], bv[:, :], ALU.add).then_inc(v_out, 1)
                    dve.wait_ge(v_out, i + 3)
                    heads = whole[:, b, :].rearrange("p (o h d) -> p o h d", o=1, h=HEADS)
                    rests = rest[:, b, :].rearrange("p (o h d) -> p o h d", o=1, h=HEADS)
                    part = [v[:, bass.ds(i, 1), :, r, :] for r in range(PARTS)]
                    V.tensor_copy(part[0], heads).then_inc(v_step, 1)
                    dve.wait_ge(v_step, i * 4 + 1)
                    V.tensor_tensor(rests, heads, part[0], ALU.subtract).then_inc(v_step, 1)
                    dve.wait_ge(v_step, i * 4 + 2)
                    V.tensor_copy(part[1], rests).then_inc(v_step, 1)
                    dve.wait_ge(v_step, i * 4 + 3)
                    V.tensor_tensor(part[2], rests, part[1], ALU.subtract).then_inc(v_step, 1)


def attention_heads(nc, g, name, v):
    with Layer(nc, name) as L:
        NSB = T // SBLK
        HB = SBLK // NB
        UNITS = NSB * TT
        PIECES = TT * TC
        NP = 4
        LAG = 3
        LOADS = 4 * PARTS * 16
        qm, km = L.sb("qm", [STACK, T], BF16), L.sb("km", [STACK, T], BF16)
        q1, k1 = L.sb("q1", [STACK + 3, 2, T], BF16), L.sb("k1", [STACK + 3, 2, T], BF16)
        q2, k2 = L.sb("q2", [STACK, 2, T], BF16), L.sb("k2", [STACK, 2, T], BF16)
        prob = L.sb("prob", [P, NP, SBLK])
        low = L.sb("low", [P, NP, SBLK], BF16)
        peak = L.sb("peak", [P, TT, TC])
        neg, left = L.sb("neg", [P, TT]), L.sb("left", [P, TT])
        negp = L.sb("negp", [P, P // TT, TT], BF16)
        rows = L.sb("rows", [3 * TT, P], BF16)
        out = L.sb("out", [P, 2, SBLK])
        sc_ps = L.ps("sc_ps", [P, 2, HB, NB])
        o_ps = L.ps("o_ps", [P, HB, NB])
        mx_ps = L.ps("mx_ps", [P, 2, NB])
        high = prob[:, :, :].bitcast(BF16).rearrange("p n (s two) -> p n s two", two=2)[:, :, :, 1]
        rows_ps = mx_ps[:, 0, :].bitcast(BF16)[:, 0:P]
        (ones_ready, m_loaded, low_pool, low_vector, sc_done, exp_done, pv_done, o_done, mx_done, mx_used, neg_step, neg_done,
         rows_done, rows_ready, rows_saved, out_ready) = (
            L.sem(s) for s in ("ones_ready", "m_loaded", "low_pool", "low_vector", "sc_done", "exp_done", "pv_done", "o_done",
                               "mx_done", "mx_used", "neg_step", "neg_done", "rows_done", "rows_ready", "rows_saved",
                               "out_ready"))
        taken = L.sem("taken")
        loaded = [L.sem(f"loaded{b}") for b in range(2)]
        out_saved = [L.sem(f"out_saved{b}") for b in range(2)]
        block = L.block()
        PAIRS = HEADS // 2

        RATE = 2.5
        pieces = [range(min(PIECES, math.ceil(RATE * w)), min(PIECES, math.ceil(RATE * (w + 1)))) for w in range(UNITS)]
        NEGATE = next(w for w in range(UNITS) if pieces[w].stop == PIECES)
        ROWS = NEGATE + 3
        pool_units = [w for w in range(UNITS) if w % 2 == 1]
        vector_units = [w for w in range(UNITS) if w % 2 == 0]
        assert UNITS - 1 not in vector_units

        @block.sync
        def _(sp):
            def stack(dst, j, order, h, sem):
                for r, part in enumerate(order):
                    sp.dma_start(dst[r * DH:(r + 1) * DH, :], g.qk_dram[j][part, bass.ds(h * DH, DH), :]).then_inc(sem, 16)

            def load_max(h):
                stack(qm[:, :], 0, (0, 0, 1), h, m_loaded)
                stack(km[:, :], 1, (0, 1, 0), h, m_loaded)

            def load_head(h, b):
                stack(q1[0:STACK, b, :], 0, (0, 0, 1), h, loaded[b])
                stack(k1[0:STACK, b, :], 1, (0, 1, 0), h, loaded[b])
                stack(q2[:, b, :], 0, (1, 0, 2), h, loaded[b])
                stack(k2[:, b, :], 1, (1, 2, 0), h, loaded[b])

            def load_rows(h, b):
                sp.wait_ge(rows_ready, h + 1)
                sp.dma_start(g.row_dram.rearrange("r (i p) -> (r i) p", p=P), rows[:, :]).then_inc(rows_saved, 16)
                sp.wait_ge(rows_saved, h * 16 + 32)
                sp.dma_start(q1[STACK:STACK + 3, b, :], g.row_dram).then_inc(loaded[b], 16)

            def save(h, b, s):
                sp.wait_ge(out_ready, h * NSB + (s + 2))
                sp.sem_inc(taken, 1)
                sp.dma_start(g.o_dram[bass.ds(h, 1), :, s * SBLK:(s + 1) * SBLK].rearrange("h f t -> f h t"),
                             out[:, s:s + 1, :]).then_inc(out_saved[s], 16)

            def body(pair, last):
                for b in range(2):
                    h = pair * 2 + b
                    final = last and b == 1
                    if not final:
                        sp.wait_ge(sc_done, h * UNITS + 1)
                        sp.sem_inc(taken, 1)
                        load_head(h + 1, 1 - b)
                        sp.wait_ge(mx_done, h * PIECES + 2 * PIECES)
                        if not last:
                            sp.sem_inc(taken, 1)
                            load_max(h + 2)
                    save(h, b, 0)
                    if not final:
                        load_rows(h + 1, 1 - b)
                    save(h, b, 1)

            sp.sem_inc(out_saved[0], 16)
            sp.sem_inc(out_saved[1], 16)
            sp.sem_inc(rows_saved, 16)
            load_max(0)
            load_head(0, 0)
            sp.wait_ge(mx_done, PIECES)
            load_max(1)
            load_rows(0, 0)
            with sp.Fori(0, PAIRS - 1) as pair:
                body(pair, False)
            body(PAIRS - 1, True)
            for b in range(2):
                sp.wait_ge(out_saved[b], 16 * (HEADS + 1))

        @block.gpsimd
        def _(pool):
            pool.memset(negp[:, :, :], 0.0).then_inc(ones_ready, 1)
            pool.wait_ge(ones_ready, 1)
            pool.memset(k1[STACK:STACK + 3, :, :], 1.0).then_inc(ones_ready, 1)

            def body(pair):
                for b in range(2):
                    for j, w in enumerate(pool_units):
                        n = pair * 2 + b
                        pool.wait_ge(exp_done, n * UNITS + (w + 3))
                        pool.wait_ge(pv_done, n * UNITS + (w + 1))
                        pool.tensor_tensor(low[:, w % NP, :], prob[:, w % NP, :], high[:, w % NP, :], ALU.subtract).then_inc(low_pool, 1)

            with pool.Fori(0, PAIRS) as pair:
                body(pair)

        @block.tensor
        def _(pe):
            def max_piece(h, i, t):
                n = h * PIECES + (i * TC + t)
                pe.wait_ge(mx_used, n + 1)
                nc.tensor.matmul(mx_ps[:, t % 2, :], qm[:, i * P:(i + 1) * P], km[:, t * NB:(t + 1) * NB],
                                 start=True, stop=True).then_inc(mx_done, 1)

            def max_rows(h):
                pe.wait_ge(neg_done, h + 1)
                nc.tensor.transpose(rows_ps, negp[:, :, :].rearrange("p r i -> p (r i)"), g.ident16[:, :]).then_inc(rows_done, 1)

            def scores(h, b, w):
                s, i = w // TT, w % TT
                pe.wait_ge(exp_done, h * UNITS + (w + 1))
                keys = slice(i * P, (i + 1) * P)
                for c in range(HB):
                    cols = slice(s * SBLK + c * NB, s * SBLK + (c + 1) * NB)
                    nc.tensor.matmul(sc_ps[:, i % 2, c, :], k1[:, b, keys], q1[:, b, cols], start=True, stop=False)
                    last = nc.tensor.matmul(sc_ps[:, i % 2, c, :], k2[:, b, keys], q2[:, b, cols], start=False, stop=True)
                last.then_inc(sc_done, 1)

            def values(h, w):
                s, i = w // TT, w % TT
                if w in pool_units:
                    pe.wait_ge(low_pool, h * len(pool_units) + (pool_units.index(w) + 1))
                else:
                    pe.wait_ge(low_vector, h * len(vector_units) + (vector_units.index(w) + 1))
                if i == 0:
                    pe.wait_ge(out_ready, h * NSB + (s + 1))
                parts = v[:, i, bass.ds(h, 1), :, :].rearrange("p o r d -> p (o r d)")
                for c in range(HB):
                    cols = slice(c * NB, (c + 1) * NB)
                    nc.tensor.matmul(o_ps[:, c, :], parts, high[:, w % NP, cols], start=(i == 0), stop=False)
                    last = nc.tensor.matmul(o_ps[:, c, :], parts, low[:, w % NP, cols], start=False, stop=(i == TT - 1))
                last.then_inc(pv_done, 1)

            def begin(h, b, pair_of_h):
                pe.wait_ge(loaded[b], pair_of_h * (LOADS + 16) + (LOADS + 16))
                pe.wait_ge(rows_ready, h + 1)

            def beside(h, w, place):
                if w == 0 and place == 0:
                    pe.wait_ge(m_loaded, h * 96 + 96)
                for n in pieces[w][place:place + 1 if place < 2 else None]:
                    max_piece(h, n // TC, n % TC)
                if w == ROWS and place == 2:
                    max_rows(h)

            def body(pair, last):
                for b in range(2):
                    h = pair * 2 + b
                    end = last and b == 1
                    for w in range(LAG, UNITS + LAG):
                        if w < UNITS:
                            scored, unit, buf, more = h, w, b, not end
                        else:
                            scored, unit, buf, more = h + 1, w - UNITS, 1 - b, not (last and b == 0)
                        if w < UNITS or not end:
                            if w == UNITS:
                                begin(h + 1, 1 - b, pair + b)
                            if more:
                                beside(scored + 1, unit, 0)
                            scores(scored, buf, unit)
                            if more:
                                beside(scored + 1, unit, 1)
                        values(h, w - LAG)
                        if more and (w < UNITS or not end):
                            beside(scored + 1, unit, 2)

            pe.sem_inc(pv_done, NP)
            pe.wait_ge(ones_ready, 2)
            pe.wait_ge(m_loaded, 96)
            for i in range(TT):
                for t in range(TC):
                    max_piece(0, i, t)
            max_rows(0)
            begin(0, 0, 0)
            for w in range(LAG):
                beside(1, w, 0)
                scores(0, 0, w)
                beside(1, w, 1)
                beside(1, w, 2)
            with pe.Fori(0, PAIRS - 1) as pair:
                body(pair, False)
            body(PAIRS - 1, True)

        @block.scalar
        def _(act):
            act.sem_inc(exp_done, 2)
            act.sem_inc(out_ready, 1)

            def exponentials(h, w):
                act.wait_ge(sc_done, h * UNITS + (w + 1))
                act.wait_ge(pv_done, h * UNITS + (w + 1))
                nc.scalar.activation(prob[:, w % NP, :], sc_ps[:, w % 2, :, :].rearrange("p c n -> p (c n)"),
                                     ACT.Exp).then_inc(exp_done, 1)

            def output(h, s):
                act.wait_ge(pv_done, h * UNITS + ((s + 1) * TT + NP))
                act.wait_ge(out_saved[s], h * 16 + 16)
                nc.scalar.copy(out[:, s, :], o_ps[:, :, :].rearrange("p c n -> p (c n)")).then_inc(out_ready, 1)

            def body(pair, last):
                for b in range(2):
                    h = pair * 2 + b
                    end = last and b == 1
                    for w in range(LAG, UNITS + LAG):
                        if w < UNITS:
                            exponentials(h, w)
                        elif not end:
                            exponentials(h + 1, w - UNITS)
                        if w in (TT + LAG - 1, 2 * TT + LAG - 1):
                            output(h, w // TT - 1)

            for w in range(LAG):
                exponentials(0, w)
            with act.Fori(0, PAIRS - 1) as pair:
                body(pair, False)
            body(PAIRS - 1, True)

        @block.vector
        def _(dve):
            V = nc.vector
            dve.sem_inc(mx_used, 2)

            def peaks(h, n):
                dve.wait_ge(mx_done, h * PIECES + (n + 1))
                V.tensor_reduce(peak[:, n // TC, n % TC:n % TC + 1], mx_ps[:, n % 2, :], axis=AX.X, op=ALU.max).then_inc(mx_used, 1)

            def negate(h):
                dve.wait_ge(mx_used, h * PIECES + (PIECES + 2))
                V.tensor_reduce(neg[:, :], peak[:, :, :], axis=AX.X, op=ALU.max).then_inc(neg_step, 1)
                dve.wait_ge(neg_step, h * 5 + 1)
                V.tensor_scalar(neg[:, :], neg[:, :], -1.0, None, ALU.mult).then_inc(neg_step, 1)
                dve.wait_ge(neg_step, h * 5 + 2)
                V.tensor_copy(negp[:, 0, :], neg[:, :]).then_inc(neg_step, 1)
                dve.wait_ge(neg_step, h * 5 + 3)
                V.tensor_tensor(left[:, :], neg[:, :], negp[:, 0, :], ALU.subtract).then_inc(neg_step, 1)
                dve.wait_ge(neg_step, h * 5 + 4)
                V.tensor_copy(negp[:, 1, :], left[:, :]).then_inc(neg_step, 1)
                dve.wait_ge(neg_step, h * 5 + 5)
                V.tensor_tensor(negp[:, 2, :], left[:, :], negp[:, 1, :], ALU.subtract).then_inc(neg_done, 1)

            def rows_out(h):
                dve.wait_ge(rows_done, h + 1)
                dve.wait_ge(rows_saved, h * 16 + 16)
                V.tensor_copy(rows[:, :], rows_ps[0:3 * TT, :]).then_inc(rows_ready, 1)

            def lower(h, w):
                dve.wait_ge(exp_done, h * UNITS + (w + 3))
                dve.wait_ge(pv_done, h * UNITS + (w + 1))
                V.tensor_tensor(low[:, w % NP, :], prob[:, w % NP, :], high[:, w % NP, :], ALU.subtract).then_inc(low_vector, 1)

            def body(pair, last):
                for b in range(2):
                    h = pair * 2 + b
                    ahead = not (last and b == 1)
                    for w in range(UNITS):
                        if ahead:
                            for n in pieces[w][:2]:
                                peaks(h + 1, n)
                        if w - 1 in vector_units:
                            lower(h, w - 1)
                        if ahead:
                            for n in pieces[w][2:]:
                                peaks(h + 1, n)
                            if w == NEGATE:
                                negate(h + 1)
                        if ahead and w == ROWS:
                            rows_out(h + 1)

            dve.wait_ge(ones_ready, 1)
            for n in range(PIECES):
                peaks(0, n)
            negate(0)
            rows_out(0)
            with dve.Fori(0, PAIRS - 1) as pair:
                body(pair, False)
            body(PAIRS - 1, True)


def attention_outputs(nc, g, name, o, w):
    QH = P // DH
    SEG = T * HEADS // P
    with Layer(nc, name + "l") as L:
        sums = L.sb("sums", [P, SEG])
        inv = L.sb("inv", [P, DT, T])
        sums_loaded, inverted, inv_saved, inv_loaded, chain = (
            L.sem(s) for s in ("sums_loaded", "inverted", "inv_saved", "inv_loaded", "chain"))
        loaded = [L.sem(f"loaded{r}") for r in range(PARTS)]
        turn = WeightTranspose(L, nc, g, [(g.dram["L1_attn_a_Wo"], w)])
        block = L.block()
        heads = g.o_dram.rearrange("(c q) f t -> q f c t", q=QH)

        @block.sync
        def _(sp):
            for h in range(HEADS):
                n = P // HEADS
                sp.dma_start(sums[h * n:(h + 1) * n, :], g.o_dram[h, PARTS * DH, :].rearrange("(a b) -> a b", a=n)).then_inc(sums_loaded, 16)
            turn.on_sync(sp)
            for r in range(PARTS):
                for q in range(QH):
                    sp.dma_start(o[q * DH:(q + 1) * DH, r, :, :], heads[q, r * DH:(r + 1) * DH, :, :]).then_inc(loaded[r], 16)
            for r in range(PARTS):
                sp.wait_ge(loaded[r], 16 * QH)

        @block.tensor
        def _(pe):
            turn.on_tensor(pe)

        @block.scalar
        def _(act):
            turn.on_scalar(act)
            act.wait_ge(inverted, 1)
            act.dma_start(g.inv_dram.rearrange("h (a b) -> (h a) b", b=SEG), sums[:, :]).then_inc(inv_saved, 16)
            act.wait_ge(inv_saved, 16)
            for q in range(QH):
                act.dma_start(inv[q * DH:(q + 1) * DH, :, :],
                              g.inv_dram.rearrange("(c q) t -> q c t", q=QH)[q].partition_broadcast(DH)).then_inc(inv_loaded, 16)
            act.wait_ge(inv_loaded, 16 * QH)

        @block.vector
        def _(dve):
            link = Chain(dve, chain)
            dve.wait_ge(sums_loaded, 16 * HEADS)
            nc.vector.reciprocal(sums[:, :], sums[:, :]).then_inc(inverted, 1)
            for r in range(2):
                dve.wait_ge(loaded[r], 16 * QH)
            link(nc.vector.tensor_tensor(o[:, 0, :, :], o[:, 0, :, :], o[:, 1, :, :], ALU.add))
            dve.wait_ge(loaded[2], 16 * QH)
            link(nc.vector.tensor_tensor(o[:, 0, :, :], o[:, 0, :, :], o[:, 2, :, :], ALU.add))
            dve.wait_ge(inv_loaded, 16 * QH)
            link(nc.vector.tensor_tensor(o[:, 0, :, :], o[:, 0, :, :], inv[:, :, :], ALU.mult))
    project_and_add(nc, g, name, o[:, 0, :, :], w, g.dram["L1_attn_a_bo"])


E_N = 64
TOP = 8
CAP = 256
IN = 192
TAIL = IN - P
GE = 8
GROUPS = E_N // GE
SA = P // GE
SB = CAP // SA
NOWHERE = 4096.0
DROPPED = 65536.0


def moe(nc, g, name):
    with ExitStack() as ctx:
        slot_token = ctx.enter_context(nc.sbuf_tensor(f"{name}_slot_token", [P, GROUPS, SB], U32))
        rows = ctx.enter_context(nc.sbuf_tensor(f"{name}_rows", [P, TT, TOP], U32))
        weights = ctx.enter_context(nc.sbuf_tensor(f"{name}_weights", [P, TT, TOP], F32))
        choice_f = ctx.enter_context(nc.sbuf_tensor(f"{name}_choice_f", [P, TT, TOP], F32))
        pos = ctx.enter_context(nc.sbuf_tensor(f"{name}_pos", [P, TT, E_N], F32))
        iota = ctx.enter_context(nc.sbuf_tensor(f"{name}_iota", [P, E_N], F32))
        with nc.sbuf_tensor(f"{name}_logits", [P, TT, E_N], F32) as logits:
            moe_logits(nc, g, name + "a", logits)
            moe_routing(nc, g, name + "b", logits, slot_token, choice_f, pos, iota, weights)
        moe_experts(nc, g, name + "c", slot_token, choice_f, pos, iota, rows, weights)
        moe_combine(nc, g, name + "d", rows, weights)


def moe_logits(nc, g, name, logits):
    NZ = 4
    with Layer(nc, name) as L:
        norm = Norm(L, nc, g.X)
        z = L.sb("z", [P, NZ, D])
        zt = L.sb("zt", [P, 2, D])
        rw = L.sb("rw", [E_N, D])
        rwt = L.sb("rwt", [P, DT, E_N])
        zt_ps = L.ps("zt_ps", [P, 2, D])
        rwt_ps = L.ps("rwt_ps", [P, DT, E_N])
        lg_ps = L.ps("lg_ps", [P, 2, NB])
        z_ready, zt_done, zt_ready, lg_ready, lg_used, rw_loaded, rwt_done, rwt_ready = (
            L.sem(s) for s in ("z_ready", "zt_done", "zt_ready", "lg_ready", "lg_used", "rw_loaded", "rwt_done", "rwt_ready"))
        z_saved = [L.sem(f"z_saved{b}") for b in range(NZ)]
        block = L.block()
        z_rows = g.z_dram.rearrange("(i p) d -> p i d", p=P)

        @block.sync
        def _(sp):
            sp.dma_start(rw[:, :], g.dram["L1_ffn_router_weight"]).then_inc(rw_loaded, 16)
            with sp.Fori(0, TT // NZ) as r:
                for b in range(NZ):
                    sp.wait_ge(z_ready, r * NZ + b + 1)
                    sp.dma_start(z_rows[:, bass.ds(r * NZ + b, 1), :], z[:, b:b + 1, :]).then_inc(z_saved[b], 16)
            for b in range(NZ):
                sp.wait_ge(z_saved[b], 16 * (TT // NZ))

        @block.vector
        def _(dve):
            norm.on_vector(dve)
            dve.sem_inc(lg_used, 2)
            for b in range(NZ):
                nc.vector.tensor_scalar(z[:, b, :], g.X[:, b, :], norm.mv[:, b, 0:1], norm.rstd[:, b:b + 1],
                                        ALU.subtract, ALU.mult).then_inc(z_ready, 1)
            with dve.Fori(0, TT // NZ - 1) as r:
                for b in range(NZ):
                    i = r * NZ + b
                    dve.wait_ge(lg_ready, i + 1)
                    nc.vector.tensor_copy(logits[:, bass.ds(i, 1), :], lg_ps[:, b % 2:b % 2 + 1, 0:E_N]).then_inc(lg_used, 1)
                    dve.wait_ge(z_saved[b], r * 16 + 16)
                    nc.vector.tensor_scalar(z[:, b:b + 1, :], g.X[:, bass.ds(i + NZ, 1), :], norm.mv[:, bass.ds(i + NZ, 1), 0:1],
                                            norm.rstd[:, bass.ds(i + NZ, 1)], ALU.subtract, ALU.mult).then_inc(z_ready, 1)
            for b in range(NZ):
                i = TT - NZ + b
                dve.wait_ge(lg_ready, i + 1)
                nc.vector.tensor_copy(logits[:, i, :], lg_ps[:, b % 2, 0:E_N]).then_inc(lg_used, 1)

        @block.tensor
        def _(pe):
            pe.wait_ge(rw_loaded, 16)
            for k in range(DT):
                last = nc.tensor.transpose(rwt_ps[:, k, :], rw[:, k * P:(k + 1) * P], g.ident[0:E_N, 0:E_N])
            last.then_inc(rwt_done, 1)
            pe.wait_ge(rwt_ready, 1)

            def transposes(i, b):
                pe.wait_ge(z_ready, i + 1)
                for k in range(DT):
                    last = nc.tensor.transpose(zt_ps[:, b % 2, k * P:(k + 1) * P], z[:, b, k * P:(k + 1) * P], g.ident[:, :])
                last.then_inc(zt_done, 1)

            def product(i, b):
                pe.wait_ge(zt_ready, i + 1)
                pe.wait_ge(lg_used, i + 1)
                for k in range(DT):
                    last = nc.tensor.matmul(lg_ps[:, b % 2, 0:E_N], zt[:, b % 2, k * P:(k + 1) * P], rwt[:, k, :],
                                            start=(k == 0), stop=(k == DT - 1))
                last.then_inc(lg_ready, 1)

            with pe.Fori(0, TT // NZ) as r:
                for b in range(0, NZ, 2):
                    transposes(r * NZ + b, b)
                    transposes(r * NZ + (b + 1), b + 1)
                    product(r * NZ + b, b)
                    product(r * NZ + (b + 1), b + 1)

        @block.scalar
        def _(act):
            norm.on_scalar(act)
            act.wait_ge(rwt_done, 1)
            nc.scalar.copy(rwt[:, :, :], rwt_ps[:, :, :]).then_inc(rwt_ready, 1)
            with act.Fori(0, TT // 2) as pair:
                for b in range(2):
                    act.wait_ge(zt_done, pair * 2 + b + 1)
                    nc.scalar.copy(zt[:, b, :], zt_ps[:, b, :]).then_inc(zt_ready, 1)


def moe_routing(nc, g, name, logits, slot_token, choice_f, pos, iota, weights):
    with Layer(nc, name) as L:
        best = L.sb("best", [P, TT, TOP])
        choice = L.sb("choice", [P, TT, TOP], U32)
        others = L.sb("others", [P, TT, E_N])
        shifted = L.sb("shifted", [P, TT, E_N])
        total = L.sb("total", [P, TT])
        taken = L.sb("taken", [P, TT, E_N])
        taken16 = L.sb("taken16", [P, TT, E_N], BF16)
        before16 = L.sb("before16", [P, TT, E_N], BF16)
        pos_i = L.sb("pos_i", [P, TT, E_N], I32)
        pos_a = L.sb("pos_a", [P, TT, E_N], I32)
        pos_a16 = L.sb("pos_a16", [P, TT, E_N], BF16)
        pos_b16 = L.sb("pos_b16", [P, TT, E_N], BF16)
        tri = L.sb("tri", [P, P])
        tri16, ones16 = L.sb("tri16", [P, P], BF16), L.sb("ones16", [P, P], BF16)
        iota_i = L.sb("iota_i", [P, E_N], I32)
        iota16 = L.sb("iota16", [P, SA], BF16)
        part_i, part = L.sb("part_i", [P, 1], I32), L.sb("part", [P, 1])
        own = L.sb("own", [P, GE])
        hot = L.sb("hot", [P, TT // 2, TOP, E_N])
        tile_i, tile16 = L.sb("tile_i", [P, TT], I32), L.sb("tile16", [P, TT], BF16)
        eq_a = L.sb("eq_a", [P, 2, TT, GE, SA], BF16)
        eq_b = L.sb("eq_b", [P, 2, TT, GE, SB], BF16)
        by_part = L.sb("by_part", [P, 2, TT, GE, SB], BF16)
        by_tile = L.sb("by_tile", [P, 2, TT, GE, SB], BF16)
        diag = L.sb("diag", [P, 2, GE, SB])
        slot_f = L.sb("slot_f", [P, GROUPS, SB])
        pos_ps = L.ps("pos_ps", [P, TT, E_N])
        slot_ps = L.ps("slot_ps", [P, 2, 4, P])
        consts, chain, less_max, exps, counted, pos_done, eq_a_ready, eq_b_ready, by_part_ready, by_tile_ready, slots_done, slots_used = (
            L.sem(s) for s in ("consts", "chain", "less_max", "exps", "counted", "pos_done", "eq_a_ready", "eq_b_ready",
                           "by_part_ready", "by_tile_ready", "slots_done", "slots_used"))
        N_CONSTS = 14
        block = L.block()

        @block.gpsimd
        def _(pool):
            link = Chain(pool, consts)
            link(pool.memset(tri[:, :], 1.0))
            link(pool.memset(ones16[:, :], 1.0))
            link(pool.affine_select(out=tri[:, :], in_=tri[:, :], compare_op=ALU.is_ge, fill=0.0, base=-1,
                                    pattern=[[1, P]], channel_multiplier=-1))
            link(pool.tensor_copy(tri16[:, :], tri[:, :]))
            link(pool.iota(iota_i[:, :], [[1, E_N]], base=0, channel_multiplier=0))
            link(pool.tensor_copy(iota[:, :], iota_i[:, :]))
            link(pool.tensor_copy(iota16[:, :], iota_i[:, 0:SA]))
            link(pool.iota(part_i[:, :], [[0, 1]], base=0, channel_multiplier=1))
            link(pool.tensor_copy(part[:, :], part_i[:, :]))
            link(pool.iota(tile_i[:, :], [[P, TT]], base=0, channel_multiplier=0))
            link(pool.tensor_copy(tile16[:, :], tile_i[:, :]))
            link(pool.memset(own[:, :], 1.0))
            link(pool.affine_select(out=own[:, :], in_=own[:, :], compare_op=ALU.is_ge, fill=0.0, base=0,
                                    pattern=[[-SA, GE]], channel_multiplier=1))
            link(pool.affine_select(out=own[:, :], in_=own[:, :], compare_op=ALU.is_ge, fill=0.0, base=SA - 1,
                                    pattern=[[SA, GE]], channel_multiplier=-1))
            assert link.n == N_CONSTS

            for q in range(GROUPS):
                pool.wait_ge(eq_b_ready, q + 1)
                pool.tensor_tensor(by_tile[:, q % 2, :, :, :].rearrange("p i e b -> p i (e b)"),
                                   eq_b[:, q % 2, :, :, :].rearrange("p i e b -> p i (e b)"),
                                   tile16[:, :].rearrange("p (i o) -> p i o", o=1).to_broadcast([P, TT, GE * SB]),
                                   ALU.mult).then_inc(by_tile_ready, 1)

        @block.vector
        def _(dve):
            link = Chain(dve, chain)
            for i in range(TT):
                link(nc.vector.max(best[:, i, :], logits[:, i, :]))
            for i in range(TT):
                nc.vector.max_index(choice[:, i, :], best[:, i, :], logits[:, i, :])
            for i in range(TT):
                link(nc.vector.match_replace(others[:, i, :], best[:, i, :], logits[:, i, :], -3.0e38))
            link(nc.vector.tensor_tensor(taken[:, :, :], others[:, :, :], logits[:, :, :], ALU.not_equal))
            link(nc.vector.tensor_copy(taken16[:, :, :], taken[:, :, :]))
            link(nc.vector.memset(before16[:, 0, :], 0.0))
            for i in range(1, TT):
                link(nc.vector.tensor_tensor(before16[:, i, :], before16[:, i - 1, :], taken16[:, i - 1, :], ALU.add))
            link(nc.vector.tensor_copy(choice_f[:, :, :], choice[:, :, :]))
            dve.sem_inc(counted, 1)
            link(nc.vector.tensor_tensor(shifted[:, :, :], logits[:, :, :], best[:, :, 0:1].to_broadcast([P, TT, E_N]), ALU.subtract))
            nc.vector.tensor_tensor(weights[:, :, :], best[:, :, :], best[:, :, 0:1].to_broadcast([P, TT, TOP]),
                                    ALU.subtract).then_inc(less_max, 1)
            dve.wait_ge(exps, 2)
            link(nc.vector.tensor_reduce(total[:, :], shifted[:, :, :], axis=AX.X, op=ALU.add))
            link(nc.vector.reciprocal(total[:, :], total[:, :]))
            link(nc.vector.tensor_tensor(weights[:, :, :], weights[:, :, :],
                                         total[:, :].rearrange("p (i o) -> p i o", o=1).to_broadcast([P, TT, TOP]), ALU.mult))
            link(nc.vector.tensor_reduce(total[:, :], weights[:, :, :], axis=AX.X, op=ALU.add))
            link(nc.vector.reciprocal(total[:, :], total[:, :]))
            link(nc.vector.tensor_tensor(weights[:, :, :], weights[:, :, :],
                                         total[:, :].rearrange("p (i o) -> p i o", o=1).to_broadcast([P, TT, TOP]), ALU.mult))

            dve.wait_ge(consts, N_CONSTS)
            dve.wait_ge(pos_done, 1)
            link(nc.vector.tensor_copy(pos[:, :, :], pos_ps[:, :, :]))
            link(nc.vector.tensor_scalar(shifted[:, :, :], taken[:, :, :], -NOWHERE, NOWHERE, ALU.mult, ALU.add))
            link(nc.vector.tensor_tensor(shifted[:, :, :], pos[:, :, :], shifted[:, :, :], ALU.add))
            link(nc.vector.tensor_copy(pos_i[:, :, :], shifted[:, :, :]))
            link(nc.vector.tensor_scalar(pos_a[:, :, :], pos_i[:, :, :], SA - 1, None, ALU.bitwise_and))
            link(nc.vector.tensor_copy(pos_a16[:, :, :], pos_a[:, :, :]))
            link(nc.vector.tensor_scalar(pos_i[:, :, :], pos_i[:, :, :], int(math.log2(SA)), None, ALU.logical_shift_right))
            link(nc.vector.tensor_copy(pos_b16[:, :, :], pos_i[:, :, :]))

            def digit(x, q, n):
                return x[:, :, q * GE:(q + 1) * GE].rearrange("p i (e o) -> p i e o", o=1).to_broadcast([P, TT, GE, n])

            def count(n):
                return iota16[:, 0:n].rearrange("p (i e n) -> p i e n", i=1, e=1).to_broadcast([P, TT, GE, n])

            def slots_out(q):
                link(nc.vector.tensor_tensor(diag[:, q % 2, :, :], slot_ps[:, q % 2, 0, :].rearrange("p (e b) -> p e b", e=GE),
                                             own[:, :].rearrange("p (e o) -> p e o", o=1).to_broadcast([P, GE, SB]), ALU.mult))
                dve.sem_inc(slots_used, 1)
                link(nc.vector.tensor_reduce(slot_f[:, q, :], diag[:, q % 2, :, :].rearrange("p e b -> p b e"), axis=AX.X, op=ALU.add))

            for q in range(GROUPS):
                if q >= 2:
                    dve.wait_ge(slots_done, q - 1)
                nc.vector.tensor_tensor(eq_b[:, q % 2, :, :, :], digit(pos_b16, q, SB), count(SB), ALU.is_equal).then_inc(eq_b_ready, 1)
                nc.vector.tensor_tensor(eq_a[:, q % 2, :, :, :], digit(pos_a16, q, SA), count(SA), ALU.is_equal).then_inc(eq_a_ready, 1)
                if q >= 2:
                    slots_out(q - 2)
            for q in range(GROUPS - 2, GROUPS):
                dve.wait_ge(slots_done, q + 1)
                slots_out(q)
            link(nc.vector.tensor_copy(slot_token[:, :, :], slot_f[:, :, :]))

        @block.scalar
        def _(act):
            act.wait_ge(less_max, 1)
            nc.scalar.activation(shifted[:, :, :], shifted[:, :, :], ACT.Exp).then_inc(exps, 1)
            nc.scalar.activation(weights[:, :, :], weights[:, :, :], ACT.Exp).then_inc(exps, 1)
            act.wait_ge(consts, N_CONSTS)
            for q in range(GROUPS):
                act.wait_ge(eq_b_ready, q + 1)
                nc.scalar.activation(by_part[:, q % 2, :, :, :].rearrange("p i e b -> p (i e b)"),
                                     eq_b[:, q % 2, :, :, :].rearrange("p i e b -> p (i e b)"), ACT.Copy,
                                     scale=part[:, 0:1]).then_inc(by_part_ready, 1)

        @block.tensor
        def _(pe):
            pe.wait_ge(consts, N_CONSTS)
            pe.wait_ge(counted, 1)
            for h in range(2):
                ts = slice(h * TT // 2, (h + 1) * TT // 2)
                nc.tensor.matmul(pos_ps[:, ts, :], tri16[:, :], taken16[:, ts, :], start=True, stop=False)
                last = nc.tensor.matmul(pos_ps[:, ts, :], ones16[:, :], before16[:, ts, :], start=False, stop=True)
            last.then_inc(pos_done, 1)
            for q in range(GROUPS):
                for sem in (eq_a_ready, by_part_ready, by_tile_ready):
                    pe.wait_ge(sem, q + 1)
                if q >= 2:
                    pe.wait_ge(slots_used, q - 1)
                for i in range(TT):
                    for rhs in (by_part, by_tile):
                        last = nc.tensor.matmul(slot_ps[:, q % 2, 0, :], eq_a[:, q % 2, i, :, :], rhs[:, q % 2, i, :, :],
                                                start=(i == 0 and rhs is by_part), stop=(i == TT - 1 and rhs is by_tile))
                last.then_inc(slots_done, 1)


def moe_experts(nc, g, name, slot_token, choice_f, pos, iota, rows, weights):
    with Layer(nc, name) as L:
        NW = 4
        UNITS = 2 * GE
        NY = 4
        token = L.sb("token", [P, 2, SB], U32)
        xg = L.sb("xg", [P, SB, D])
        xt = L.sb("xt", [P, 2, DT, GE, SB, SA])
        wgu = L.sb("wgu", [P, NW, DT, 2 * IN])
        wd = L.sb("wd", [P, NW, D])
        wd_tail = L.sb("wd_tail", [P, NW, D])
        sg = L.sb("sg", [P, 2, IN])
        h = L.sb("h", [P, 2, 2 * P + 2 * TAIL])
        ht = L.sb("ht", [P, 2, 3, P])
        ye = L.sb("ye", [P, NY, D])
        xt_ps = L.ps("xt_ps", [P, 2, 4, P])
        gu_ps = L.ps("gu_ps", [P, 2, NB])
        ht_ps = L.ps("ht_ps", [P, 2, 4, P])
        ye_ps = L.ps("ye_ps", [P, 2, D])
        token_ready, xt_done, xt_ready, gu_done, sg_ready, h_ready, ht_done, ht_ready, ye_done, ye_ready = (
            L.sem(s) for s in ("token_ready", "xt_done", "xt_ready", "gu_done", "sg_ready", "h_ready", "ht_done", "ht_ready",
                               "ye_done", "ye_ready"))
        best = L.sb("best", [P, TT, TOP])
        in_time = L.sb("in_time", [P, TT, TOP])
        chain = L.sem("chain")
        passed = L.sem("passed")
        gathered = [L.sem(f"gathered{j}") for j in range(4)]
        w_loaded = [L.sem(f"w_loaded{j}") for j in range(NW)]
        saved = [L.sem(f"saved{j}") for j in range(NY)]
        block = L.block()
        wgu_dram = g.dram["L1_ffn_gate_up_proj"].rearrange("e (k p) f -> p e k f", p=P)
        wd_dram = g.dram["L1_ffn_down_proj"].rearrange("e p d -> p e d")
        W_LOADS = 4 * 16
        y_rows = g.y_dram.rearrange("(u p) d -> p u d", p=P)

        def over_groups(eng, body):
            body(0, 0, True, False)
            with eng.Fori(0, GROUPS // 2 - 1) as r:
                body(r * 2 + 1, 1, False, False)
                body(r * 2 + 2, 0, False, False)
            body(GROUPS - 1, 1, False, True)

        @block.sync
        def _(sp):
            def load(e, slot):
                one = bass.ds(e, 1)
                at = slice(slot, slot + 1)
                sp.dma_start(wgu[:, at, :, :], wgu_dram[:, one, :, :]).then_inc(w_loaded[slot], 16)
                sp.dma_start(wd[:, at, :], wd_dram[0:P, one, :]).then_inc(w_loaded[slot], 16)
                for half in range(2):
                    sp.dma_start(wd_tail[half * TAIL:(half + 1) * TAIL, at, :], wd_dram[P:IN, one, :]).then_inc(w_loaded[slot], 16)

            def save(e, slot):
                for s in range(2):
                    sp.wait_ge(ye_ready, e * 2 + s + 1)
                    y = (2 * slot + s) % NY
                    sp.dma_start(y_rows[:, bass.ds(e * 2 + s, 1), :], ye[:, y:y + 1, :]).then_inc(saved[y], 16)

            for e in range(NW):
                load(e, e)
            with sp.Fori(0, E_N // NW - 1) as r:
                for s in range(NW):
                    e = r * NW + s
                    save(e, s)
                    load(e + NW, s)
            for s in range(NW):
                save(E_N - NW + s, s)
            for y in range(NY):
                sp.wait_ge(saved[y], 16 * (2 * E_N // NY))

        @block.gpsimd
        def _(pool):
            def gather(n, b, free):
                pool.tensor_copy(token[:, b:b + 1, :], slot_token[:, bass.ds(n, 1), :]).then_inc(token_ready, 1)
                pool.wait_ge(token_ready, n + 1)
                pool.sem_inc(passed, 1)
                for s in range(SB):
                    if s % 4 == 0 and free is not None:
                        pool.wait_ge(xt_done, free + s + 4)
                        pool.sem_inc(passed, 1)
                    pool.indirect_dma_start(out=xg[:, s, :], out_offset=None, in_=g.z_dram,
                                            in_offset=bass.IndirectOffsetOnAxis(ap=token[:, b, s:s + 1], axis=0)
                                            ).then_inc(gathered[s // 4], 16)

            def body(q, b, first, last):
                if not last:
                    if not first:
                        for j in range(4):
                            pool.wait_ge(gathered[j], q * 64)
                        pool.sem_inc(passed, 1)
                    gather(q + 1, 1 - b, q * UNITS)

            gather(0, 0, None)
            over_groups(pool, body)

        @block.tensor
        def _(pe):
            def transposes(n, b, u, first):
                j, k = u // 4, u % 4
                if k == 0:
                    pe.wait_ge(gathered[j], n * 64 + 64)
                if not (first and u < 2):
                    pe.wait_ge(xt_ready, n * UNITS + u - 1)
                for s in range(4):
                    last = nc.tensor.transpose(xt_ps[:, u % 2, s, :], xg[:, 4 * j + s, k * P:(k + 1) * P], g.ident[:, :])
                last.then_inc(xt_done, 1)

            def inner(q, b, u, first):
                n = q * UNITS + u
                e, s = u // 2, u % 2
                if s == 0:
                    pe.wait_ge(w_loaded[e % NW], q * (GE // NW * W_LOADS) + (e // NW + 1) * W_LOADS)
                if u == 0:
                    pe.wait_ge(xt_ready, q * UNITS + UNITS)
                if not (first and u < 2):
                    pe.wait_ge(h_ready, n - 1)
                for k in range(DT):
                    last = nc.tensor.matmul(gu_ps[:, u % 2, 0:2 * IN], xt[:, b, k, e, s * SB // 2:(s + 1) * SB // 2, :],
                                            wgu[:, e % NW, k, :], start=(k == 0), stop=(k == DT - 1))
                last.then_inc(gu_done, 1)

            def hidden(e, b):
                pe.wait_ge(h_ready, e * 2 + 2)
                for j in range(3):
                    last = nc.tensor.transpose(ht_ps[:, b, j, :], h[:, b, j * P:(j + 1) * P], g.ident[:, :])
                last.then_inc(ht_done, 1)

            def outer(e, slot, first):
                b = slot % 2
                pe.wait_ge(ht_ready, e + 1)
                if not first:
                    pe.wait_ge(ye_ready, e * 2)
                for s in range(2):
                    nc.tensor.matmul(ye_ps[:, s, :], ht[:, b, s, :], wd[:, slot, :], start=True, stop=False)
                for s in range(2):
                    rows = slice(s * TAIL, (s + 1) * TAIL)
                    nc.tensor.matmul(ye_ps[:, s, :], ht[rows, b, 2, :], wd_tail[rows, slot, :], start=False, stop=True).then_inc(ye_done, 1)

            def body(q, b, first, last):
                for u in range(UNITS):
                    inner(q, b, u, first)
                    before = u // 2 - 1
                    if not (first and before < 0):
                        if u % 2 == 0:
                            hidden(q * GE + before, before % 2)
                        else:
                            outer(q * GE + before, before % NW, first and before == 0)
                    if not last:
                        transposes(q + 1, 1 - b, u, False)

            for u in range(UNITS):
                transposes(0, 0, u, True)
            over_groups(pe, body)
            hidden(E_N - 1, (E_N - 1) % 2)
            outer(E_N - 1, (E_N - 1) % NW, False)

        @block.scalar
        def _(act):
            def evacuate(n, b, u):
                j, k = u // 4, u % 4
                act.wait_ge(xt_done, n * UNITS + u + 1)
                nc.scalar.copy(xt[:, b, k, :, 4 * j:4 * j + 4, :],
                               xt_ps[:, u % 2, :, :].rearrange("p s (e a) -> p e s a", e=GE)).then_inc(xt_ready, 1)

            def body(q, b, first, last):
                for u in range(UNITS):
                    n = q * UNITS + u
                    act.wait_ge(gu_done, n + 1)
                    if not (first and u < 2):
                        act.wait_ge(h_ready, n - 1)
                    nc.scalar.activation(sg[:, u % 2, :], gu_ps[:, u % 2, 0:IN], ACT.Silu).then_inc(sg_ready, 1)
                    if not last:
                        evacuate(q + 1, 1 - b, u)

            for u in range(UNITS):
                evacuate(0, 0, u)
            over_groups(act, body)

        @block.vector
        def _(dve):
            def choice_rows(dve):
                link = Chain(dve, chain)
                late = ye[:, 0:2, :].rearrange("p b (i e) -> p (b i) e", e=E_N)
                link(nc.vector.tensor_scalar(late, pos[:, :, :], float(CAP), DROPPED, ALU.is_ge, ALU.mult))
                link(nc.vector.tensor_scalar(pos[:, :, :], pos[:, :, :], float(CAP - 1), None, ALU.min))
                link(nc.vector.tensor_tensor(pos[:, :, :], pos[:, :, :], late, ALU.add))
                QT = NY * D // (TOP * E_N)
                hot = ye[:, :, :].rearrange("p b (k e) -> p b k e", e=E_N)
                for t0 in range(0, TT, QT):
                    for i in range(QT):
                        link(nc.vector.tensor_tensor(
                            hot[:, i, :, :], choice_f[:, t0 + i, :].rearrange("p (k o) -> p k o", o=1).to_broadcast([P, TOP, E_N]),
                            iota[:, :].rearrange("p (o e) -> p o e", o=1).to_broadcast([P, TOP, E_N]), ALU.is_equal))
                    for i in range(QT):
                        link(nc.vector.tensor_tensor(
                            hot[:, i, :, :], hot[:, i, :, :],
                            pos[:, t0 + i, :].rearrange("p (o e) -> p o e", o=1).to_broadcast([P, TOP, E_N]), ALU.mult))
                    link(nc.vector.tensor_reduce(best[:, t0:t0 + QT, :], hot, axis=AX.X, op=ALU.add))
                link(nc.vector.tensor_scalar(in_time[:, :, :], best[:, :, :], DROPPED, None, ALU.is_lt))
                link(nc.vector.tensor_tensor(weights[:, :, :], weights[:, :, :], in_time[:, :, :], ALU.mult))
                link(nc.vector.tensor_scalar(in_time[:, :, :], in_time[:, :, :], DROPPED, -DROPPED, ALU.mult, ALU.add))
                link(nc.vector.tensor_tensor(best[:, :, :], best[:, :, :], in_time[:, :, :], ALU.add))
                link(nc.vector.scalar_tensor_tensor(out=best[:, :, :], in0=choice_f[:, :, :], scalar=float(CAP), in1=best[:, :, :],
                                                    op0=ALU.mult, op1=ALU.add))
                link(nc.vector.tensor_copy(rows[:, :, :], best[:, :, :]))

            def gate(n, e, u, first):
                dve.wait_ge(sg_ready, n + 1)
                if not (first and u < 4):
                    dve.wait_ge(ht_done, e - 1)
                s, b = u % 2, u // 2 % 2
                for part, to in ((slice(0, P), s * P), (slice(P, IN), 2 * P + s * TAIL)):
                    n_cols = part.stop - part.start
                    last = nc.vector.tensor_tensor(h[:, b, to:to + n_cols], sg[:, s, part],
                                                   gu_ps[:, s, IN + part.start:IN + part.stop], ALU.mult)
                last.then_inc(h_ready, 1)

            def hidden_out(e, b):
                dve.wait_ge(ht_done, e + 1)
                nc.vector.tensor_copy(ht[:, b, :, :], ht_ps[:, b, 0:3, :]).then_inc(ht_ready, 1)

            def outputs_out(e, q, u, first):
                for s in range(2):
                    y = (u + s) % NY
                    dve.wait_ge(ye_done, e * 2 + (s + 1))
                    if not (first and u < NY):
                        dve.wait_ge(saved[y], q * (UNITS // NY * 16) + (u // NY * 16))
                    nc.vector.tensor_copy(ye[:, y, :], ye_ps[:, s, :]).then_inc(ye_ready, 1)

            def body(q, b, first, last):
                for u in range(UNITS):
                    gate(q * UNITS + u, q * GE + u // 2, u, first)
                    before = u // 2 - 1
                    if not (first and before < 0):
                        e = q * GE + before
                        if u % 2 == 0:
                            hidden_out(e, before % 2)
                        else:
                            outputs_out(e, q - (before < 0), before % GE * 2, first)

            choice_rows(dve)
            over_groups(dve, body)
            hidden_out(E_N - 1, (E_N - 1) % 2)
            outputs_out(E_N - 1, GROUPS - 1, UNITS - 2, False)


def moe_combine(nc, g, name, rows, weights):
    NG = 4
    with Layer(nc, name) as L:
        row = L.sb("row", [P, NG, TOP], U32)
        yg = L.sb("yg", [P, NG, TOP, D])
        row_ready, summed = L.sem("row_ready"), L.sem("summed")
        passed = L.sem("passed")
        gathered = [L.sem(f"gathered{b}") for b in range(NG)]
        block = L.block()

        @block.gpsimd
        def _(pool):
            def gather(i, b, first):
                if not first:
                    pool.wait_ge(summed, (i - NG + 1) * TOP)
                    pool.sem_inc(passed, 1)
                pool.tensor_copy(row[:, b:b + 1, :], rows[:, bass.ds(i, 1), :]).then_inc(row_ready, 1)
                pool.wait_ge(row_ready, i + 1)
                pool.sem_inc(passed, 1)
                for k in range(TOP):
                    pool.indirect_dma_start(out=yg[:, b, k, :], out_offset=None, in_=g.y_dram,
                                            in_offset=bass.IndirectOffsetOnAxis(ap=row[:, b, k:k + 1], axis=0)
                                            ).then_inc(gathered[b], 16)

            for b in range(NG):
                gather(b, b, True)
            with pool.Fori(0, TT // NG - 1) as r:
                for b in range(NG):
                    gather(r * NG + (NG + b), b, False)

        @block.vector
        def _(dve):
            with dve.Fori(0, TT // NG) as r:
                for b in range(NG):
                    i = r * NG + b
                    dve.wait_ge(gathered[b], r * (16 * TOP) + 16 * TOP)
                    for k in range(TOP):
                        nc.vector.scalar_tensor_tensor(
                            out=g.X[:, bass.ds(i, 1), :], in0=yg[:, b, k:k + 1, :], scalar=weights[:, bass.ds(i, 1), k],
                            in1=g.X[:, bass.ds(i, 1), :], op0=ALU.mult, op1=ALU.add).then_inc(summed, 1)
                        dve.wait_ge(summed, i * TOP + (k + 1))


LH = 32
LD = 64
LF = LH * LD
CH = P
NCH = T // CH
PAIRS_L = LH // 2
KINDS = 4
RMS_EPS = 1e-5
FAR = 1.0e9


def head_slopes():
    base = 1.0 / 2.0 ** (8.0 / LH)
    return [base ** (h + 1.0) * (1.0 + 1e-5) for h in range(LH)]


def linear_attention(nc, g):
    with nc.sbuf_tensor("lin_squares", [P, T], F32) as squares:
        with nc.sbuf_tensor("lin_z", [P, DT, T], F32) as z:
            normalized_features(nc, g, "lina", z)
            linear_heads(nc, g, "linb", z, squares)
        linear_outputs(nc, g, "linc", squares)


def linear_heads(nc, g, name, z, squares):
    with Layer(nc, name) as L:
        TQ = NB // CH
        USES = KINDS * (TC + 1)
        wr = L.sb("wr", [P, KINDS, D])
        wt = L.sb("wt", [P, KINDS, DT, P])
        proj = [L.sb(f"proj{b}", [P, KINDS, T]) for b in range(2)]
        qd = L.sb("qd", [P, T])
        dd = L.sb("dd", [P, 2, 2, CH])
        qdec = L.sb("qdec", [P, 2, CH])
        slope_all = L.sb("slope_all", [P, LH])
        slope_own = L.sb("slope_own", [P, PAIRS_L])
        kdec = L.sb("kdec", [P, LH])
        sdec = L.sb("sdec", [P, PAIRS_L])
        norm_w = L.sb("norm_w", [P, PAIRS_L])
        dist_i, dist = L.sb("dist_i", [P, CH], I32), L.sb("dist", [P, CH])
        since_i, since = L.sb("since_i", [P, CH], I32), L.sb("since", [P, CH])
        until_i, until = L.sb("until_i", [P, LH], I32), L.sb("until", [P, LH])
        aw = L.sb("aw", [P, 2, CH])
        kt = L.sb("kt", [P, 2, LD])
        vt = L.sb("vt", [P, P])
        state = L.sb("state", [P, 2, P])
        osb = L.sb("osb", [P, 2, NB])
        sq = L.sb("sq", [P, NB])
        gated = L.sb("gated", [P, 2, NB])
        pr_ps = L.ps("pr_ps", [P, 2, NB])
        s_ps = L.ps("s_ps", [P, 2, 4, CH])
        tr_ps = L.ps("tr_ps", [P, 4, P])
        kv_ps = L.ps("kv_ps", [P, 4, P])
        o_ps = L.ps("o_ps", [P, 2, NB])
        names = ("w_taken", "pr_done", "pr_out", "consts", "tables0", "tables", "qd_done", "s_done", "aw_done", "tr_done",
                 "vt_done", "kv_done", "state_done", "o_done", "o_out", "gated_done", "sq_step", "sq_done",
                 "norm_loaded", "osb_used", "state_step", "act_passed")
        S = {n: L.sem(n) for n in names}
        (w_taken, pr_done, pr_out, consts, tables0, tables, qd_done, s_done, aw_done, tr_done, vt_done, kv_done,
         state_done, o_done, o_out, gated_done, sq_step, sq_done, norm_loaded, osb_used, state_step, act_passed) = (S[n] for n in names)
        w_loaded = [L.sem(f"w_loaded{k}") for k in range(KINDS)]
        saved = [L.sem(f"saved{b}") for b in range(2)]
        block = L.block()
        qkv_rows = g.dram["L1_attn_b_qkv_w"].rearrange("(h c r) i -> h c r i", c=3, r=LD)
        gate_rows = g.dram["L1_attn_b_gate_w"].rearrange("(n p) i -> n p i", p=P)
        out_rows = g.g_dram.rearrange("(n p) t -> p n t", p=P)
        N_CONSTS = 9 + 2 * LH

        def over_pairs(eng, body):
            with eng.Fori(0, PAIRS_L // 2 - 1) as r:
                body(r * 2, 0, False)
                body(r * 2 + 1, 1, False)
            body(PAIRS_L - 2, 0, False)
            body(PAIRS_L - 1, 1, True)

        @block.sync
        def _(sp):
            def load(kind, n):
                if kind < 3:
                    for hh in range(2):
                        sp.dma_start(wr[hh * LD:(hh + 1) * LD, kind:kind + 1, :],
                                     qkv_rows[bass.ds(n * 2 + hh, 1), kind, :, :].rearrange("h r i -> r h i")).then_inc(w_loaded[kind], 16)
                else:
                    sp.dma_start(wr[:, kind:kind + 1, :], gate_rows[bass.ds(n, 1), :, :].rearrange("n p i -> p n i")).then_inc(w_loaded[kind], 32)

            def save(n, b, q):
                sp.wait_ge(gated_done, n * TC + (q + 1))
                sp.sem_inc(w_taken, 1)
                sp.dma_start(out_rows[:, bass.ds(n, 1), q * NB:(q + 1) * NB],
                             gated[:, q % 2:q % 2 + 1, :]).then_inc(saved[q % 2], 16)

            def reload(kind, n):
                if kind == 0:
                    sp.wait_ge(pr_done, (n - 1) * USES + 1)
                else:
                    sp.wait_ge(pr_done, (n - 1) * USES + (5 * (kind - 1) + 6))
                sp.sem_inc(w_taken, 1)
                load(kind, n)

            sp.dma_start(norm_w[:, :], g.dram["L1_attn_b_norm_w"].rearrange("(c p) -> p c", p=P),
                         allow_slow_non_contiguous=True).then_inc(norm_loaded, 16)
            for kind in range(KINDS):
                load(kind, 0)
            for kind in range(KINDS):
                reload(kind, 1)

            with sp.Fori(0, PAIRS_L // 2 - 1) as r:
                for b in range(2):
                    n = r * 2 + b
                    for q in range(TC):
                        reload(q, n + 2)
                        save(n, b, q)
            for b in range(2):
                for q in range(TC):
                    save(PAIRS_L - 2 + b, b, q)
            for b in range(2):
                sp.wait_ge(saved[b], 16 * (PAIRS_L * TC // 2 + 1))
            sp.wait_ge(norm_loaded, 16)

        @block.gpsimd
        def _(pool):
            link = Chain(pool, consts)
            link(pool.iota(dist_i[:, :], [[1, CH]], base=0, channel_multiplier=-1))
            link(pool.tensor_copy(dist[:, :], dist_i[:, :]))
            link(pool.affine_select(out=dist[:, :], in_=dist[:, :], compare_op=ALU.is_ge, fill=FAR, base=0,
                                    pattern=[[1, CH]], channel_multiplier=-1))
            link(pool.iota(since_i[:, :], [[1, CH]], base=1, channel_multiplier=0))
            link(pool.tensor_copy(since[:, :], since_i[:, :]))
            link(pool.iota(until_i[:, :], [[0, LH]], base=CH - 1, channel_multiplier=-1))
            link(pool.tensor_copy(until[:, :], until_i[:, :]))
            link(pool.memset(state[:, :, :], 0.0))
            link(pool.memset(squares[:, :], 0.0))
            for h, s in enumerate(head_slopes()):
                link(pool.memset(slope_all[:, h:h + 1], -s))
                r = (h % 2) * LD
                link(pool.memset(slope_own[r:r + LD, h // 2:h // 2 + 1], -s))
            assert link.n == N_CONSTS

            def body(n, b, last):
                for q in range(TC):
                    m = n * TC + q
                    pool.wait_ge(o_out, m + 3)
                    pool.tensor_tensor(sq[:, :], osb[:, q % 2, :], osb[:, q % 2, :], ALU.mult).then_inc(sq_step, 1)
                    pool.wait_ge(sq_step, m + 1)
                    pool.tensor_tensor(squares[:, q * NB:(q + 1) * NB], squares[:, q * NB:(q + 1) * NB], sq[:, :], ALU.add).then_inc(sq_done, 1)
                    pool.wait_ge(sq_done, m + 3)

            pool.sem_inc(sq_done, 2)
            over_pairs(pool, body)

        @block.tensor
        def _(pe):
            def weight(kind, n, use):
                pe.wait_ge(w_loaded[kind], n * 32 + 32)
                pe.wait_ge(pr_out, use[0] * USES + (use[1] + 1))
                for k in range(DT):
                    last = nc.tensor.transpose(pr_ps[:, use[1] % 2, k * P:(k + 1) * P], wr[:, kind, k * P:(k + 1) * P], g.ident[:, :])
                last.then_inc(pr_done, 1)

            def piece(kind, t, n):
                use = 5 * kind + t + 1
                pe.wait_ge(pr_out, n * USES + (5 * kind + 2))
                pe.wait_ge(pr_out, n * USES + (use + 1))
                if t == 0:
                    pe.wait_ge(pr_out, n * USES + (5 * kind + 3))
                for k in range(DT):
                    last = nc.tensor.matmul(pr_ps[:, use % 2, :], wt[:, kind, k, :], z[:, k, t * NB:(t + 1) * NB],
                                            start=(k == 0), stop=(k == DT - 1))
                last.then_inc(pr_done, 1)

            def chunk_first(n, b, c):
                m = n * NCH + c
                cols = slice(c * CH, (c + 1) * CH)
                if c == 0:
                    pe.wait_ge(pr_out, n * USES + (USES + 2))
                pe.wait_ge(aw_done, m + 1)
                for hh in range(2):
                    rows = slice(hh * LD, (hh + 1) * LD)
                    last = nc.tensor.matmul(s_ps[:, hh, 0, :], proj[b][rows, 1, cols], proj[b][rows, 0, cols], start=True, stop=True)
                last.then_inc(s_done, 1)
                pe.wait_ge(vt_done, m + 1)
                nc.tensor.transpose(tr_ps[:, 0, :], proj[b][:, 1, cols], g.ident[:, :])
                nc.tensor.transpose(tr_ps[:, 1, :], proj[b][:, 2, cols], g.ident[:, :]).then_inc(tr_done, 1)

            def chunk_second(n, b, c):
                m = n * NCH + c
                q, r = c // TQ, c % TQ
                out = o_ps[:, q % 2, r * CH:(r + 1) * CH]
                if r == 0:
                    pe.wait_ge(o_out, n * TC + (q + 1))
                pe.wait_ge(aw_done, m + 2)
                pe.wait_ge(vt_done, m + 2)
                for hh in range(2):
                    rows = slice(hh * LD, (hh + 1) * LD)
                    last = nc.tensor.matmul(out[rows, :], vt[:, rows], aw[:, hh, :], start=True, stop=(c == 0),
                                            skip_group_check=True)
                if c >= 1:
                    if c == 1:
                        pe.wait_ge(qd_done, n + 1)
                    pe.wait_ge(state_done, m + 1)
                    last = nc.tensor.matmul(out, state[:, c % 2, :], qd[:, c * CH:(c + 1) * CH], start=False, stop=True,
                                            skip_group_check=True)
                last.then_inc(o_done, 1)
                if c < NCH - 1:
                    pe.wait_ge(state_done, m + 1)
                    nc.tensor.matmul(kv_ps[:, 0, :], kt[:, :, :].rearrange("p h d -> p (h d)"), vt[:, :], start=True, stop=True).then_inc(kv_done, 1)
                else:
                    pe.sem_inc(kv_done, 1)

            pe.sem_inc(kv_done, 1)
            pe.wait_ge(consts, N_CONSTS)
            weight(0, 0, (0, 0))
            for kind in range(KINDS):
                for t in range(TC):
                    piece(kind, t, 0)
                if kind < KINDS - 1:
                    weight(kind + 1, 0, (0, 5 * kind + 5))
                else:
                    weight(0, 1, (1, 0))

            def body(n, b, last):
                for c in range(NCH):
                    chunk_first(n, b, c)
                    if not last:
                        kind, t = c // TC, c % TC
                        piece(kind, t, n + 1)
                        if t == TC - 1 and kind < KINDS - 1:
                            weight(kind + 1, n + 1, (n + 1, 5 * kind + 5))
                        elif t == TC - 1 and prefetch[0]:
                            weight(0, n + 2, (n + 2, 0))
                    chunk_second(n, b, c)

            prefetch = [True]
            with pe.Fori(0, PAIRS_L // 2 - 1) as r:
                body(r * 2, 0, False)
                body(r * 2 + 1, 1, False)
            prefetch[0] = False
            body(PAIRS_L - 2, 0, False)
            body(PAIRS_L - 1, 1, True)

        @block.scalar
        def _(act):
            def table(n, b):
                for hh in range(2):
                    nc.scalar.activation(dd[:, b, hh, :], dist[:, :], ACT.Exp, scale=slope_all[:, bass.ds(n * 2 + hh, 1)]).then_inc(tables, 1)
                nc.scalar.activation(qdec[:, b, :], since[:, :], ACT.Exp, scale=slope_own[:, bass.ds(n, 1)]).then_inc(tables, 1)

            def weight_out(kind, use):
                act.wait_ge(pr_done, use[0] * USES + (use[1] + 1))
                nc.scalar.copy(wt[:, kind, :, :].rearrange("p k f -> p (k f)"), pr_ps[:, use[1] % 2, :]).then_inc(pr_out, 1)

            def piece_out(kind, t, n, b):
                use = 5 * kind + t + 1
                act.wait_ge(pr_done, n * USES + (use + 1))
                nc.scalar.activation(proj[b][:, kind, t * NB:(t + 1) * NB], pr_ps[:, use % 2, :],
                                     ACT.Sigmoid if kind == 3 else ACT.Silu).then_inc(pr_out, 1)

            def chunk_out(n, c):
                m = n * NCH + c
                act.wait_ge(tr_done, m + 1)
                act.wait_ge(kv_done, m + 1)
                act.sem_inc(act_passed, 1)
                for hh in range(2):
                    nc.scalar.activation(kt[:, hh, :], tr_ps[:, 0, hh * LD:(hh + 1) * LD], ACT.Copy,
                                         scale=kdec[:, bass.ds(n * 2 + hh, 1)])
                nc.scalar.copy(vt[:, :], tr_ps[:, 1, :]).then_inc(vt_done, 1)

            def quarter_out(n, q):
                act.wait_ge(o_done, n * NCH + (q + 1) * TQ)
                act.wait_ge(sq_done, n * TC + (q + 1))
                act.wait_ge(osb_used, n * TC + (q + 1))
                nc.scalar.copy(osb[:, q % 2, :], o_ps[:, q % 2, :]).then_inc(o_out, 1)

            act.sem_inc(pr_out, 2)
            act.sem_inc(vt_done, 1)
            act.sem_inc(o_out, 2)
            act.wait_ge(consts, N_CONSTS)
            nc.scalar.activation(sdec[:, :], slope_own[:, :], ACT.Exp, scale=float(CH)).then_inc(tables0, 1)
            for h in range(LH):
                nc.scalar.activation(kdec[:, h:h + 1], until[:, h:h + 1], ACT.Exp, scale=slope_all[:, h:h + 1]).then_inc(tables0, 1)
            table(0, 0)
            weight_out(0, (0, 0))
            for kind in range(KINDS):
                for t in range(TC):
                    piece_out(kind, t, 0, 0)
                if kind < KINDS - 1:
                    weight_out(kind + 1, (0, 5 * kind + 5))
                else:
                    weight_out(0, (1, 0))

            def body(n, b, last):
                for c in range(NCH):
                    chunk_out(n, c)
                    if not last:
                        kind, t = c // TC, c % TC
                        if kind == 3 and t == 0:
                            act.wait_ge(gated_done, n * TC + 1)
                        piece_out(kind, t, n + 1, 1 - b)
                        if t == TC - 1 and kind < KINDS - 1:
                            weight_out(kind + 1, (n + 1, 5 * kind + 5))
                        elif t == TC - 1 and prefetch[0]:
                            weight_out(0, (n + 2, 0))
                        if c == NCH // 2:
                            table(n + 1, 1 - b)
                    if c % TQ == TQ - 1:
                        quarter_out(n, c // TQ)

            prefetch = [True]
            with act.Fori(0, PAIRS_L // 2 - 1) as r:
                body(r * 2, 0, False)
                body(r * 2 + 1, 1, False)
            prefetch[0] = False
            body(PAIRS_L - 2, 0, False)
            body(PAIRS_L - 1, 1, True)

        @block.vector
        def _(dve):
            V = nc.vector
            dve.sem_inc(aw_done, 1)
            dve.sem_inc(state_done, 1)
            dve.sem_inc(osb_used, 2)
            dve.sem_inc(saved[0], 16)
            dve.sem_inc(saved[1], 16)
            dve.wait_ge(tables0, 1 + LH)
            dve.wait_ge(norm_loaded, 16)

            def update(n, b, c):
                m = n * NCH + c
                dve.wait_ge(kv_done, m + 2)
                if c == NCH - 1:
                    dve.sem_inc(state_done, 1)
                    return
                for hh in range(2):
                    rows = slice(hh * LD, (hh + 1) * LD)
                    new, old = state[rows, (c + 1) % 2, rows], state[rows, c % 2, rows]
                    if c == 0:
                        ins = V.tensor_copy(new, kv_ps[rows, 0, rows])
                    else:
                        ins = V.scalar_tensor_tensor(out=new, in0=old, scalar=sdec[rows, bass.ds(n, 1)], in1=kv_ps[rows, 0, rows],
                                                     op0=ALU.mult, op1=ALU.add)
                    ins.then_inc(state_step, 1)
                dve.wait_ge(state_step, n * (2 * NCH - 2) + (2 * c + 2))
                dve.sem_inc(state_done, 1)

            def body(n, b, last):
                q_all = proj[b][:, 0, :].rearrange("p (c i) -> p c i", i=CH)
                dve.wait_ge(pr_out, n * USES + (USES + 2))
                dve.wait_ge(tables, n * 3 + 3)
                V.tensor_tensor(qd[:, :].rearrange("p (c i) -> p c i", i=CH), q_all,
                                qdec[:, b, :].rearrange("p (o i) -> p o i", o=1).to_broadcast([P, NCH, CH]), ALU.mult).then_inc(qd_done, 1)
                for c in range(NCH):
                    m = n * NCH + c
                    dve.wait_ge(s_done, m + 1)
                    dve.wait_ge(kv_done, m + 1)
                    V.tensor_tensor(aw[:, :, :], s_ps[:, :, 0, :], dd[:, b, :, :], ALU.mult).then_inc(aw_done, 1)
                    update(n, b, c)
                    if c % TQ == TQ - 1:
                        q = c // TQ
                        dve.wait_ge(o_out, n * TC + (q + 3))
                        dve.wait_ge(saved[q % 2], n * 32 + (q // 2 * 16 + 16))
                        V.scalar_tensor_tensor(out=gated[:, q % 2, :], in0=osb[:, q % 2, :], scalar=norm_w[:, bass.ds(n, 1)],
                                               in1=proj[b][:, 3, q * NB:(q + 1) * NB], op0=ALU.mult, op1=ALU.mult).then_inc(gated_done, 1)
                        dve.wait_ge(gated_done, n * TC + (q + 1))
                        dve.sem_inc(osb_used, 1)

            over_pairs(dve, body)


def linear_outputs(nc, g, name, squares):
    FT = LF // P
    TOK = 2 * P
    with Layer(nc, name) as L:
        w = L.sb("w", [P, 2, LF])
        wt = L.sb("wt", [P, FT, D])
        ones = L.sb("ones", [P, 1])
        ms, rms, inv = L.sb("ms", [P, TT]), L.sb("rms", [P, TT]), L.sb("inv", [P, TT])
        gt = L.sb("gt", [P, 2, FT, TOK])
        w_ps = L.ps("w_ps", [P, 2, 4, P])
        y_ps = L.ps("y_ps", [P, 2, NB])
        ss_ps = L.ps("ss_ps", [P, NB])
        (w_done, w_out, ones_ready, ss_done, ms_ready, rms_ready, inv_ready, y_done, y_used, taken) = (
            L.sem(s) for s in ("w_done", "w_out", "ones_ready", "ss_done", "ms_ready", "rms_ready", "inv_ready", "y_done", "y_used",
                            "taken"))
        w_loaded = [L.sem(f"w_loaded{b}") for b in range(2)]
        loaded = [L.sem(f"loaded{b}") for b in range(2)]
        block = L.block()
        w_rows = g.dram["L1_attn_b_out_w"].rearrange("(c p) f -> p c f", p=P)
        g_rows = g.g_dram.rearrange("(c p) t -> p c t", p=P)

        @block.sync
        def _(sp):
            for c in range(DT):
                if c >= 2:
                    sp.wait_ge(w_done, (c - 1) * 4)
                sp.dma_start(w[:, c % 2, :], w_rows[:, c, :]).then_inc(w_loaded[c % 2], 16)
                if c < 2:
                    sp.dma_start(gt[:, c, :, :], g_rows[:, :, c * TOK:(c + 1) * TOK]).then_inc(loaded[c], 16)
            with sp.Fori(0, T // TOK // 2 - 1) as r:
                for b in range(2):
                    sp.wait_ge(y_done, r * 4 + (2 * b + 2))
                    sp.sem_inc(taken, 1)
                    sp.dma_start(gt[:, b, :, :], g_rows[:, :, bass.ds(r * (2 * TOK) + (2 + b) * TOK, TOK)]).then_inc(loaded[b], 16)
            for b in range(2):
                sp.wait_ge(w_loaded[b], 32)
                sp.wait_ge(loaded[b], 16 * (T // TOK // 2))

        @block.tensor
        def _(pe):
            pe.wait_ge(ones_ready, 1)
            for i in range(TT):
                last = nc.tensor.matmul(ss_ps[:, i:i + 1], squares[:, i * P:(i + 1) * P], ones[:, :], start=True, stop=True)
            last.then_inc(ss_done, 1)
            for c in range(DT):
                pe.wait_ge(w_loaded[c % 2], 16 * (c // 2 + 1))
                for q in range(FT // 4):
                    u = c * 4 + q
                    if u >= 2:
                        pe.wait_ge(w_out, u - 1)
                    for s in range(4):
                        last = nc.tensor.transpose(w_ps[:, u % 2, s, :], w[:, c % 2, (4 * q + s) * P:(4 * q + s + 1) * P], g.ident[:, :])
                    last.then_inc(w_done, 1)
            pe.wait_ge(w_out, DT * 4)
            with pe.Fori(0, T // TOK // 2) as r:
                for b in range(2):
                    pe.wait_ge(loaded[b], r * 16 + 16)
                    for s in range(2):
                        pe.wait_ge(y_used, r * 4 + (2 * b + s + 1))
                        for f in range(FT):
                            last = nc.tensor.matmul(y_ps[:, s, :], gt[:, b, f, s * P:(s + 1) * P], wt[:, f, :],
                                                    start=(f == 0), stop=(f == FT - 1))
                        last.then_inc(y_done, 1)

        @block.scalar
        def _(act):
            for c in range(DT):
                for q in range(FT // 4):
                    u = c * 4 + q
                    act.wait_ge(w_done, u + 1)
                    nc.scalar.copy(wt[:, 4 * q:4 * q + 4, c * P:(c + 1) * P], w_ps[:, u % 2, :, :]).then_inc(w_out, 1)
            act.wait_ge(ms_ready, 1)
            nc.scalar.activation(rms[:, :], ms[:, :], ACT.Sqrt).then_inc(rms_ready, 1)

        @block.vector
        def _(dve):
            V = nc.vector
            dve.sem_inc(y_used, 2)
            V.memset(ones[:, :], 1.0).then_inc(ones_ready, 1)
            dve.wait_ge(ss_done, 1)
            V.tensor_scalar(ms[:, :], ss_ps[:, 0:TT], 1.0 / LF, RMS_EPS, ALU.mult, ALU.add).then_inc(ms_ready, 1)
            dve.wait_ge(rms_ready, 1)
            V.reciprocal(inv[:, :], rms[:, :]).then_inc(inv_ready, 1)
            dve.wait_ge(inv_ready, 1)
            with dve.Fori(0, TT // 2) as pair:
                for s in range(2):
                    i = pair * 2 + s
                    dve.wait_ge(y_done, i + 1)
                    V.scalar_tensor_tensor(out=g.X[:, bass.ds(i, 1), :], in0=y_ps[:, s:s + 1, :], scalar=inv[:, bass.ds(i, 1)],
                                           in1=g.X[:, bass.ds(i, 1), :], op0=ALU.mult, op1=ALU.add).then_inc(y_used, 1)


class Shared:
    pass


LAYERS = {
    1: lambda nc, g: lru(nc, g),
    2: lambda nc, g: ffn(nc, g, "ffn1"),
    3: lambda nc, g: ssm(nc, g),
    4: lambda nc, g: ffn(nc, g, "ffn2"),
    5: lambda nc, g: attention(nc, g),
    6: lambda nc, g: moe(nc, g, "moe1"),
    7: lambda nc, g: linear_attention(nc, g),
    8: lambda nc, g: moe(nc, g, "moe2"),
}
ORDER = (1, 2, 3, 4, 5, 6, 7, 8)


def program(nc, dram):
    with ExitStack() as ctx:
        g = Shared()
        g.dram = dram
        g.X = ctx.enter_context(nc.sbuf_tensor("residual", [P, TT, D], F32))
        g.ident = ctx.enter_context(nc.sbuf_tensor("ident", [P, P], F32))
        g.ident16 = ctx.enter_context(nc.sbuf_tensor("ident16", [P, P], BF16))
        g.z_dram = nc.dram_tensor("normalized_rows", [T, D], F32, kind="Internal").ap()
        g.y_dram = nc.dram_tensor("expert_rows", [E_N * CAP, D], F32, kind="Internal").ap()
        g.qk_dram = [nc.dram_tensor(f"{n}_parts", [PARTS, D, T], BF16, kind="Internal").ap() for n in "qk"]
        g.row_dram = nc.dram_tensor("maximum_rows", [3, T], BF16, kind="Internal").ap()
        g.o_dram = nc.dram_tensor("attention_out", [HEADS, P, T], F32, kind="Internal").ap()
        g.inv_dram = nc.dram_tensor("inverse_sums", [HEADS, T], F32, kind="Internal").ap()
        g.g_dram = nc.dram_tensor("gated_features", [LF, T], F32, kind="Internal").ap()
        setup(nc, g)
        for n in ORDER:
            if n == 2:
                g.ffn_wt = ctx.enter_context(nc.sbuf_tensor("ffn_wt", [P, DT, D], F32))
                g.ffn_bias = ctx.enter_context(nc.sbuf_tensor("ffn_bias", [P, D], F32))
                binarized_weight(nc, g)
            LAYERS[n](nc, g)
        store(nc, g)


_OUT_SHAPE = (1, T, D)


def kernel(**inputs):
    import numpy as _np
    import concourse.bacc as _bacc
    from concourse.bass_utils import run_bass_kernel_spmd as _run

    nc = _bacc.Bacc("TRN2", target_bir_lowering=False, num_devices=1)
    arrays, dram = {}, {}
    for name, value in inputs.items():
        a = _np.ascontiguousarray(value)
        arrays[f"in_{name}"] = a
        dram[name] = nc.dram_tensor(f"in_{name}", a.shape, mybir.dt.from_np(a.dtype), kind="ExternalInput").ap()
    dram["out"] = nc.dram_tensor("out_0", _OUT_SHAPE, F32, kind="ExternalOutput").ap()
    program(nc, dram)
    r = _run(nc, [arrays], core_ids=[0])
    return r.results[0]["out_0"]
```
